# Optimizing a Trainium2 kernel written in Bass

```python
import numpy as np
import jax
import jax.numpy as jnp

def _softmax(x, axis=-1):
    return jax.nn.softmax(x, axis=axis)

def _gelu(x):
    return jax.nn.gelu(x, approximate=True)

def _silu(x):
    return jax.nn.silu(x)

def _sigmoid(x):
    return jax.nn.sigmoid(x)

def _layernorm(x, axis=-1, eps=1e-05):
    m = jnp.mean(x, axis=axis, keepdims=True)
    v = jnp.var(x, axis=axis, keepdims=True)
    return (x - m) / jnp.sqrt(v + eps)

def _scatter_add(tgt, idx, src, axis=0):
    return tgt.at[idx].add(src)

def _segment_sum(src, seg, n):
    return jax.ops.segment_sum(src, seg, n)
kernel_name = 'mk_sandwich_d4_jaxref_r8_cbfc67'

def setup_inputs(seed: int=0):
    np.random.seed(seed)
    _w = jnp.asarray

    def _L0_attn_setup():
        import jax, jax.numpy as jnp
        import numpy as np
        B, S, D = (1, 256, 512)
        H = 32
        Q_RANK, KV_RANK = (192, 64)
        NOPE, ROPE, VD = (128, 64, 128)
        QD = NOPE + ROPE
        EPS = 1e-06
        THETA = 10000.0

        def _rmsnorm(x, w):
            return x * jax.lax.rsqrt(jnp.mean(x * x, axis=-1, keepdims=True) + EPS) * w

        def _rotate_half(x):
            h = x.shape[-1] // 2
            return jnp.concatenate([-x[..., h:], x[..., :h]], axis=-1)

        def _apply_rope(x, cos, sin):
            xp = jnp.concatenate([x[..., 0::2], x[..., 1::2]], axis=-1)
            return xp * cos + _rotate_half(xp) * sin

        def _mla_forward(hidden_states, Wq_a, q_a_ln_w, Wq_b, Wkv_a, kv_a_ln_w, Wkv_b, Wo):
            b, s, _ = hidden_states.shape
            q = _rmsnorm(hidden_states @ Wq_a, q_a_ln_w) @ Wq_b
            q = q.reshape(b, s, H, QD).transpose(0, 2, 1, 3)
            q_nope, q_pe = (q[..., :NOPE], q[..., NOPE:])
            ckv = hidden_states @ Wkv_a
            compressed, k_pe = (ckv[..., :KV_RANK], ckv[..., KV_RANK:])
            kv = _rmsnorm(compressed, kv_a_ln_w) @ Wkv_b
            kv = kv.reshape(b, s, H, NOPE + VD).transpose(0, 2, 1, 3)
            k_nope, v = (kv[..., :NOPE], kv[..., NOPE:])
            k_pe = k_pe[:, None, :, :]
            inv_freq = 1.0 / THETA ** (jnp.arange(0, ROPE, 2, dtype=jnp.float32) / ROPE)
            freqs = jnp.outer(jnp.arange(s, dtype=jnp.float32), inv_freq)
            emb = jnp.concatenate([freqs, freqs], axis=-1)
            cos = jnp.cos(emb)[None, None].astype(hidden_states.dtype)
            sin = jnp.sin(emb)[None, None].astype(hidden_states.dtype)
            q_pe = _apply_rope(q_pe, cos, sin)
            k_pe = _apply_rope(k_pe, cos, sin)
            qf = jnp.concatenate([q_nope, q_pe], axis=-1)
            kf = jnp.concatenate([k_nope, jnp.broadcast_to(k_pe, (b, H, s, ROPE))], axis=-1)
            scale = QD ** (-0.5)
            scores = jnp.einsum('bhqd,bhkd->bhqk', qf, kf) * scale
            causal = jnp.tril(jnp.ones((s, s), dtype=bool))
            scores = jnp.where(causal, scores, jnp.finfo(scores.dtype).min)
            probs = jax.nn.softmax(scores, axis=-1)
            o = jnp.einsum('bhqk,bhkd->bhqd', probs, v)
            o = o.transpose(0, 2, 1, 3).reshape(b, s, H * VD)
            return o @ Wo
        key = jax.random.key(seed)
        ks = jax.random.split(key, 8)
        std = 0.02
        return {'hidden_states': jax.random.normal(ks[0], (B, S, D), jnp.float32), 'Wq_a': jax.random.normal(ks[1], (D, Q_RANK), jnp.float32) * std, 'q_a_ln_w': jnp.ones((Q_RANK,), jnp.float32), 'Wq_b': jax.random.normal(ks[2], (Q_RANK, H * QD), jnp.float32) * std, 'Wkv_a': jax.random.normal(ks[3], (D, KV_RANK + ROPE), jnp.float32) * std, 'kv_a_ln_w': jnp.ones((KV_RANK,), jnp.float32), 'Wkv_b': jax.random.normal(ks[4], (KV_RANK, H * (NOPE + VD)), jnp.float32) * std, 'Wo': jax.random.normal(ks[5], (H * VD, D), jnp.float32) * std}
    _L0_attn_in = _L0_attn_setup()

    def _L0_ffn_setup():
        import jax, jax.numpy as jnp
        import numpy as np
        LORA_RANK = 16
        LORA_ALPHA = 16
        LORA_SCALE = LORA_ALPHA / LORA_RANK
        key = jax.random.key(seed)
        k1, k2, k3, k4, k5 = jax.random.split(key, 5)
        B, S, D_IN, D_OUT, N_LORA, R = (8, 256, 512, 512, 3, LORA_RANK)
        std = 1.0 / np.sqrt(D_IN)
        x = jax.random.normal(k1, (B, S, D_IN), dtype=jnp.float32)
        weight = jax.random.truncated_normal(k2, -3.0, 3.0, (D_OUT, D_IN), dtype=jnp.float32) * std
        bias = jax.random.normal(k3, (D_OUT,), dtype=jnp.float32) * 0.01
        lora_A = jax.random.normal(k4, (N_LORA, R, D_IN), dtype=jnp.float32) * std
        lora_B = jax.random.normal(k5, (N_LORA, D_OUT, R), dtype=jnp.float32) * 0.02
        lora_start_indices = jnp.arange(4, dtype=jnp.int64) * 2
        return {'x': x, 'weight': weight, 'bias': bias, 'lora_A': lora_A, 'lora_B': lora_B, 'lora_start_indices': lora_start_indices}
    _L0_ffn_in = _L0_ffn_setup()

    def _L1_attn_setup():
        import jax, jax.numpy as jnp
        import numpy as np
        EMBED = 512
        H = 32
        KV = 8
        D = EMBED // H
        REP = H // KV

        def _rope(t, cos, sin):
            t = t.reshape(*t.shape[:-1], 2, D // 2)
            t1, t2 = (t[..., 0, :], t[..., 1, :])
            return jnp.concatenate([t1 * cos - t2 * sin, t1 * sin + t2 * cos], axis=-1)
        key = jax.random.key(seed)
        ks = jax.random.split(key, 7)
        B, S = (1, 256)
        x = jax.random.normal(ks[0], (B, S, EMBED), dtype=jnp.float32)
        wq = jax.random.normal(ks[1], (EMBED, EMBED), dtype=jnp.float32) * 0.02
        bq = jax.random.normal(ks[2], (EMBED,), dtype=jnp.float32) * 0.02
        wk = jax.random.normal(ks[3], (EMBED, KV * D), dtype=jnp.float32) * 0.02
        bk = jax.random.normal(ks[4], (KV * D,), dtype=jnp.float32) * 0.02
        wv = jax.random.normal(ks[5], (EMBED, KV * D), dtype=jnp.float32) * 0.02
        bv = jax.random.normal(ks[6], (KV * D,), dtype=jnp.float32) * 0.02
        return {'x': x, 'wq': wq, 'bq': bq, 'wk': wk, 'bk': bk, 'wv': wv, 'bv': bv}
    _L1_attn_in = _L1_attn_setup()

    def _L1_ffn_setup():
        import jax, jax.numpy as jnp
        import numpy as np
        IN_CHN = 512
        OUT_CHN = 512

        def binarize_weights(weight):
            scale = jax.lax.stop_gradient(jnp.mean(jnp.abs(weight), axis=1, keepdims=True))
            bin_no_grad = scale * jnp.sign(weight)
            clipped = jnp.clip(weight, -1.0, 1.0)
            return jax.lax.stop_gradient(bin_no_grad) - jax.lax.stop_gradient(clipped) + clipped
        key = jax.random.key(seed)
        kx, kw = jax.random.split(key)
        x = jax.random.normal(kx, (4, 256, IN_CHN), dtype=jnp.float32)
        weight = jax.random.uniform(kw, (OUT_CHN, IN_CHN), dtype=jnp.float32) * 0.001
        return {'x': x, 'weight': weight}
    _L1_ffn_in = _L1_ffn_setup()

    def _L2_attn_setup():
        import jax, jax.numpy as jnp
        import numpy as np
        HIDDEN = 512
        HEADS = 32
        D_K = HIDDEN // HEADS
        key = jax.random.key(seed)
        ks = jax.random.split(key, 5)
        scale = 1.0 / np.sqrt(HIDDEN)
        x = jax.random.normal(ks[0], (2, 256, HIDDEN), dtype=jnp.float32)
        w_q = jax.random.uniform(ks[1], (HIDDEN, HIDDEN), jnp.float32, -scale, scale)
        w_k = jax.random.uniform(ks[2], (HIDDEN, HIDDEN), jnp.float32, -scale, scale)
        w_v = jax.random.uniform(ks[3], (HIDDEN, HIDDEN), jnp.float32, -scale, scale)
        w_o = jax.random.uniform(ks[4], (HIDDEN, HIDDEN), jnp.float32, -scale, scale)
        return {'x': x, 'w_q': w_q, 'w_k': w_k, 'w_v': w_v, 'w_o': w_o}
    _L2_attn_in = _L2_attn_setup()

    def _L2_ffn_setup():
        import jax, jax.numpy as jnp
        import numpy as np
        HIDDEN = 512
        INTER = 1376
        BATCH, SEQ = (2, 256)

        def _ternary(key, shape):
            return jax.random.randint(key, shape, -1, 2).astype(jnp.float32)
        key = jax.random.key(seed)
        kx, kg, ku, kd = jax.random.split(key, 4)
        x = jax.random.normal(kx, (BATCH, SEQ, HIDDEN), dtype=jnp.float32)
        gate_w = _ternary(kg, (INTER, HIDDEN))
        up_w = _ternary(ku, (INTER, HIDDEN))
        down_w = _ternary(kd, (HIDDEN, INTER))
        gate_scale = jnp.float32(0.02)
        up_scale = jnp.float32(0.02)
        down_scale = jnp.float32(0.02)
        return {'x': x, 'gate_w': gate_w, 'up_w': up_w, 'down_w': down_w, 'gate_scale': gate_scale, 'up_scale': up_scale, 'down_scale': down_scale}
    _L2_ffn_in = _L2_ffn_setup()

    def _L3_attn_setup():
        import jax, jax.numpy as jnp
        import numpy as np
        HID = 512
        DM = 128
        DIN = 2 * DM
        DST = 16
        HD = 64
        NH = DIN // HD
        DCONV = 7
        CONV_DIM = DIN + 2 * DST
        DIN_PROJ = 2 * DIN + 2 * DST + 2 * NH
        SEQ, BATCH = (256, 4)

        def _causal_conv(x, w, b):
            y = jax.lax.conv_general_dilated(jnp.transpose(x, (0, 2, 1)), w, (1,), [(DCONV - 1, 0)], feature_group_count=CONV_DIM, dimension_numbers=('NCH', 'OIH', 'NCH'))
            return jnp.transpose(y, (0, 2, 1)) + b

        def _ssm_scan(x, dt, A, B, C):
            dA = jnp.exp(dt * A)
            dBx = dt[..., None] * x

            def step(h, t):
                dA_t, dBx_t, B_t, C_t = t
                h = dA_t[:, :, None, None] * h + dBx_t[..., None] * B_t[:, None, None, :]
                y = jnp.einsum('bhpn,bn->bhp', h, C_t)
                return (h, y)
            h0 = jnp.zeros((x.shape[0], NH, HD, DST), x.dtype)
            _, ys = jax.lax.scan(step, h0, (jnp.moveaxis(dA, 1, 0), jnp.moveaxis(dBx, 1, 0), jnp.moveaxis(B, 1, 0), jnp.moveaxis(C, 1, 0)))
            return jnp.moveaxis(ys, 0, 1)

        def _hydra(u, in_w, conv_w, conv_b, dt_bias, A_log, D, fcD_w, norm_w, out_w):
            b, l, _ = u.shape
            zxbcdt = u @ in_w.T
            z = zxbcdt[..., :DIN]
            xBC = zxbcdt[..., DIN:DIN + CONV_DIM]
            dt2 = zxbcdt[..., DIN + CONV_DIM:]
            dt_fw = jax.nn.softplus(dt2[..., :NH] + dt_bias)
            dt_bw = jax.nn.softplus(jnp.flip(dt2[..., NH:], 1) + dt_bias)
            xBC = jax.nn.silu(_causal_conv(xBC, conv_w, conv_b))
            xs = xBC[..., :DIN]
            Bm = xBC[..., DIN:DIN + DST]
            Cm = xBC[..., DIN + DST:]
            A = -jnp.exp(A_log)
            x4 = xs.reshape(b, l, NH, HD)
            y_fw = _ssm_scan(x4, dt_fw, A, Bm, Cm).reshape(b, l, DIN)
            y_bw = jnp.flip(_ssm_scan(jnp.flip(x4, 1), dt_bw, A, jnp.flip(Bm, 1), jnp.flip(Cm, 1)).reshape(b, l, DIN), 1)
            zero = jnp.zeros((b, 1, DIN), u.dtype)
            y = jnp.concatenate([zero, y_fw[:, :-1]], 1) + jnp.concatenate([y_bw[:, 1:], zero], 1)
            y = y + xs * jnp.repeat(xs @ fcD_w.T + D, HD, axis=-1)
            yz = y * jax.nn.silu(z)
            y = yz * jax.lax.rsqrt(jnp.mean(jnp.square(yz), -1, keepdims=True) + 1e-05) * norm_w
            return y @ out_w.T
        key = jax.random.key(seed)
        ks = jax.random.split(key, 12)
        rn = lambda k, shape, s=0.02: jax.random.normal(k, shape, jnp.float32) * s
        dt = jnp.exp(jax.random.uniform(ks[5], (NH,), jnp.float32, np.log(0.001), np.log(0.1)))
        return dict(x=jax.random.normal(ks[0], (SEQ, BATCH, HID), jnp.float32), w_down=rn(ks[1], (DM, HID)), b_down=jnp.zeros((DM,), jnp.float32), w_up=rn(ks[2], (HID, DM)), b_up=jnp.zeros((HID,), jnp.float32), gate1=jnp.asarray(0.6, jnp.float32), hy_in_w=rn(ks[3], (DIN_PROJ, DM)), hy_conv_w=rn(ks[4], (CONV_DIM, 1, DCONV), 0.2), hy_conv_b=jnp.zeros((CONV_DIM,), jnp.float32), hy_dt_bias=jnp.log(jnp.expm1(dt)), hy_A_log=jnp.log(jax.random.uniform(ks[6], (NH,), jnp.float32, 1.0, 16.0)), hy_D=jnp.ones((NH,), jnp.float32), hy_fcD_w=rn(ks[7], (NH, DIN)), hy_norm_w=jnp.ones((DIN,), jnp.float32), hy_out_w=rn(ks[8], (DM, DIN)))
    _L3_attn_in = _L3_attn_setup()

    def _L3_ffn_setup():
        import jax, jax.numpy as jnp
        import numpy as np
        B, S, D_IN, D_OUT = (2, 256, 512, 512)
        E, K, R = (8, 2, 16)
        SCALING = 32.0 / 16.0
        key = jax.random.key(seed)
        ks = jax.random.split(key, 6)
        x = jax.random.normal(ks[0], (B, S, D_IN), dtype=jnp.float32)
        gate_w = jax.random.normal(ks[1], (E, D_IN), dtype=jnp.float32) * 0.02
        base_w = jax.random.normal(ks[2], (D_OUT, D_IN), dtype=jnp.float32) * 0.02
        base_b = jax.random.normal(ks[3], (D_OUT,), dtype=jnp.float32) * 0.02
        lora_A = jax.random.normal(ks[4], (E, R, D_IN), dtype=jnp.float32) * 0.02
        lora_B = jax.random.normal(ks[5], (E, D_OUT, R), dtype=jnp.float32) * 0.02
        return {'x': x, 'gate_w': gate_w, 'base_w': base_w, 'base_b': base_b, 'lora_A': lora_A, 'lora_B': lora_B}
    _L3_ffn_in = _L3_ffn_setup()
    _d = {'L0_attn_hidden_states': _L0_attn_in['hidden_states'], 'L0_attn_Wq_a': _L0_attn_in['Wq_a'], 'L0_attn_q_a_ln_w': _L0_attn_in['q_a_ln_w'], 'L0_attn_Wq_b': _L0_attn_in['Wq_b'], 'L0_attn_Wkv_a': _L0_attn_in['Wkv_a'], 'L0_attn_kv_a_ln_w': _L0_attn_in['kv_a_ln_w'], 'L0_attn_Wkv_b': _L0_attn_in['Wkv_b'], 'L0_attn_Wo': _L0_attn_in['Wo'], 'L0_ffn_weight': _L0_ffn_in['weight'], 'L0_ffn_bias': _L0_ffn_in['bias'], 'L0_ffn_lora_A': _L0_ffn_in['lora_A'], 'L0_ffn_lora_B': _L0_ffn_in['lora_B'], 'L0_ffn_lora_start_indices': _L0_ffn_in['lora_start_indices'], 'L1_attn_wq': _L1_attn_in['wq'], 'L1_attn_bq': _L1_attn_in['bq'], 'L1_attn_wk': _L1_attn_in['wk'], 'L1_attn_bk': _L1_attn_in['bk'], 'L1_attn_wv': _L1_attn_in['wv'], 'L1_attn_bv': _L1_attn_in['bv'], 'L1_ffn_weight': _L1_ffn_in['weight'], 'L2_attn_w_q': _L2_attn_in['w_q'], 'L2_attn_w_k': _L2_attn_in['w_k'], 'L2_attn_w_v': _L2_attn_in['w_v'], 'L2_attn_w_o': _L2_attn_in['w_o'], 'L2_ffn_gate_w': _L2_ffn_in['gate_w'], 'L2_ffn_up_w': _L2_ffn_in['up_w'], 'L2_ffn_down_w': _L2_ffn_in['down_w'], 'L2_ffn_gate_scale': _L2_ffn_in['gate_scale'], 'L2_ffn_up_scale': _L2_ffn_in['up_scale'], 'L2_ffn_down_scale': _L2_ffn_in['down_scale'], 'L3_attn_w_down': _L3_attn_in['w_down'], 'L3_attn_b_down': _L3_attn_in['b_down'], 'L3_attn_w_up': _L3_attn_in['w_up'], 'L3_attn_b_up': _L3_attn_in['b_up'], 'L3_attn_gate1': _L3_attn_in['gate1'], 'L3_attn_hy_in_w': _L3_attn_in['hy_in_w'], 'L3_attn_hy_conv_w': _L3_attn_in['hy_conv_w'], 'L3_attn_hy_conv_b': _L3_attn_in['hy_conv_b'], 'L3_attn_hy_dt_bias': _L3_attn_in['hy_dt_bias'], 'L3_attn_hy_A_log': _L3_attn_in['hy_A_log'], 'L3_attn_hy_D': _L3_attn_in['hy_D'], 'L3_attn_hy_fcD_w': _L3_attn_in['hy_fcD_w'], 'L3_attn_hy_norm_w': _L3_attn_in['hy_norm_w'], 'L3_attn_hy_out_w': _L3_attn_in['hy_out_w'], 'L3_ffn_gate_w': _L3_ffn_in['gate_w'], 'L3_ffn_base_w': _L3_ffn_in['base_w'], 'L3_ffn_base_b': _L3_ffn_in['base_b'], 'L3_ffn_lora_A': _L3_ffn_in['lora_A'], 'L3_ffn_lora_B': _L3_ffn_in['lora_B']}
    _x0 = _d['L0_attn_hidden_states']
    _d['L0_attn_hidden_states'] = jax.random.normal(jax.random.fold_in(jax.random.key(seed), 1), (1, 1024, 512), dtype=_x0.dtype)
    del _x0
    return _d

def reference(L0_attn_hidden_states, L0_attn_Wq_a, L0_attn_q_a_ln_w, L0_attn_Wq_b, L0_attn_Wkv_a, L0_attn_kv_a_ln_w, L0_attn_Wkv_b, L0_attn_Wo, L0_ffn_weight, L0_ffn_bias, L0_ffn_lora_A, L0_ffn_lora_B, L0_ffn_lora_start_indices, L1_attn_wq, L1_attn_bq, L1_attn_wk, L1_attn_bk, L1_attn_wv, L1_attn_bv, L1_ffn_weight, L2_attn_w_q, L2_attn_w_k, L2_attn_w_v, L2_attn_w_o, L2_ffn_gate_w, L2_ffn_up_w, L2_ffn_down_w, L2_ffn_gate_scale, L2_ffn_up_scale, L2_ffn_down_scale, L3_attn_w_down, L3_attn_b_down, L3_attn_w_up, L3_attn_b_up, L3_attn_gate1, L3_attn_hy_in_w, L3_attn_hy_conv_w, L3_attn_hy_conv_b, L3_attn_hy_dt_bias, L3_attn_hy_A_log, L3_attn_hy_D, L3_attn_hy_fcD_w, L3_attn_hy_norm_w, L3_attn_hy_out_w, L3_ffn_gate_w, L3_ffn_base_w, L3_ffn_base_b, L3_ffn_lora_A, L3_ffn_lora_B):

    def _L0_attn_ref(hidden_states, Wq_a, q_a_ln_w, Wq_b, Wkv_a, kv_a_ln_w, Wkv_b, Wo):
        import jax, jax.numpy as jnp
        import numpy as np
        B, S, D = (1, 256, 512)
        H = 32
        Q_RANK, KV_RANK = (192, 64)
        NOPE, ROPE, VD = (128, 64, 128)
        QD = NOPE + ROPE
        EPS = 1e-06
        THETA = 10000.0

        def _rmsnorm(x, w):
            return x * jax.lax.rsqrt(jnp.mean(x * x, axis=-1, keepdims=True) + EPS) * w

        def _rotate_half(x):
            h = x.shape[-1] // 2
            return jnp.concatenate([-x[..., h:], x[..., :h]], axis=-1)

        def _apply_rope(x, cos, sin):
            xp = jnp.concatenate([x[..., 0::2], x[..., 1::2]], axis=-1)
            return xp * cos + _rotate_half(xp) * sin

        def _mla_forward(hidden_states, Wq_a, q_a_ln_w, Wq_b, Wkv_a, kv_a_ln_w, Wkv_b, Wo):
            b, s, _ = hidden_states.shape
            q = _rmsnorm(hidden_states @ Wq_a, q_a_ln_w) @ Wq_b
            q = q.reshape(b, s, H, QD).transpose(0, 2, 1, 3)
            q_nope, q_pe = (q[..., :NOPE], q[..., NOPE:])
            ckv = hidden_states @ Wkv_a
            compressed, k_pe = (ckv[..., :KV_RANK], ckv[..., KV_RANK:])
            kv = _rmsnorm(compressed, kv_a_ln_w) @ Wkv_b
            kv = kv.reshape(b, s, H, NOPE + VD).transpose(0, 2, 1, 3)
            k_nope, v = (kv[..., :NOPE], kv[..., NOPE:])
            k_pe = k_pe[:, None, :, :]
            inv_freq = 1.0 / THETA ** (jnp.arange(0, ROPE, 2, dtype=jnp.float32) / ROPE)
            freqs = jnp.outer(jnp.arange(s, dtype=jnp.float32), inv_freq)
            emb = jnp.concatenate([freqs, freqs], axis=-1)
            cos = jnp.cos(emb)[None, None].astype(hidden_states.dtype)
            sin = jnp.sin(emb)[None, None].astype(hidden_states.dtype)
            q_pe = _apply_rope(q_pe, cos, sin)
            k_pe = _apply_rope(k_pe, cos, sin)
            qf = jnp.concatenate([q_nope, q_pe], axis=-1)
            kf = jnp.concatenate([k_nope, jnp.broadcast_to(k_pe, (b, H, s, ROPE))], axis=-1)
            scale = QD ** (-0.5)
            scores = jnp.einsum('bhqd,bhkd->bhqk', qf, kf) * scale
            causal = jnp.tril(jnp.ones((s, s), dtype=bool))
            scores = jnp.where(causal, scores, jnp.finfo(scores.dtype).min)
            probs = jax.nn.softmax(scores, axis=-1)
            o = jnp.einsum('bhqk,bhkd->bhqd', probs, v)
            o = o.transpose(0, 2, 1, 3).reshape(b, s, H * VD)
            return o @ Wo
        return _mla_forward(hidden_states, Wq_a, q_a_ln_w, Wq_b, Wkv_a, kv_a_ln_w, Wkv_b, Wo)

    def _L0_ffn_ref(x, weight, bias, lora_A, lora_B, lora_start_indices):
        import jax, jax.numpy as jnp
        import numpy as np
        LORA_RANK = 16
        LORA_ALPHA = 16
        LORA_SCALE = LORA_ALPHA / LORA_RANK
        y = jnp.einsum('bsd,od->bso', x, weight) + bias
        B = x.shape[0]
        seg = jnp.searchsorted(lora_start_indices, jnp.arange(B), side='right') - 1
        adapter_idx = jnp.clip(seg - 1, 0, lora_A.shape[0] - 1)
        A = lora_A[adapter_idx]
        Bw = lora_B[adapter_idx]
        lo = jnp.einsum('bsr,bor->bso', jnp.einsum('bsd,brd->bsr', x, A), Bw) * LORA_SCALE
        use_lora = (seg > 0)[:, None, None]
        return y + jnp.where(use_lora, lo, jnp.zeros((), dtype=y.dtype))

    def _L1_attn_ref(x, wq, bq, wk, bk, wv, bv):
        import jax, jax.numpy as jnp
        import numpy as np
        EMBED = 512
        H = 32
        KV = 8
        D = EMBED // H
        REP = H // KV

        def _rope(t, cos, sin):
            t = t.reshape(*t.shape[:-1], 2, D // 2)
            t1, t2 = (t[..., 0, :], t[..., 1, :])
            return jnp.concatenate([t1 * cos - t2 * sin, t1 * sin + t2 * cos], axis=-1)
        B, S, E = x.shape
        xq = (x @ wq + bq).reshape(B, S, H, D)
        xk = (x @ wk + bk).reshape(B, S, KV, D)
        xv = (x @ wv + bv).reshape(B, S, KV, D)
        inv_freq = 1.0 / 10000.0 ** (jnp.arange(0, D, 2, dtype=jnp.float32) / D)
        ang = jnp.arange(S, dtype=jnp.float32)[:, None] * inv_freq[None, :]
        cos, sin = (jnp.cos(ang)[:, None, :], jnp.sin(ang)[:, None, :])
        q = _rope(xq, cos, sin)
        k = _rope(xk, cos, sin)
        k = jnp.repeat(k, REP, axis=2)
        v = jnp.repeat(xv, REP, axis=2)
        scores = jnp.einsum('bqhd,bkhd->bhqk', q, k) / jnp.sqrt(jnp.float32(D))
        probs = jax.nn.softmax(scores.astype(jnp.float32), axis=-1)
        out = jnp.einsum('bhqk,bkhd->bqhd', probs, v).reshape(B, S, E)
        return out

    def _L1_ffn_ref(x, weight):
        import jax, jax.numpy as jnp
        import numpy as np
        IN_CHN = 512
        OUT_CHN = 512

        def binarize_weights(weight):
            scale = jax.lax.stop_gradient(jnp.mean(jnp.abs(weight), axis=1, keepdims=True))
            bin_no_grad = scale * jnp.sign(weight)
            clipped = jnp.clip(weight, -1.0, 1.0)
            return jax.lax.stop_gradient(bin_no_grad) - jax.lax.stop_gradient(clipped) + clipped
        bw = binarize_weights(weight)
        return jnp.einsum('bsi,oi->bso', x, bw)

    def _L2_attn_ref(x, w_q, w_k, w_v, w_o):
        import jax, jax.numpy as jnp
        import numpy as np
        HIDDEN = 512
        HEADS = 32
        D_K = HIDDEN // HEADS
        B, S, _ = x.shape

        def proj(w):
            y = jnp.einsum('bsd,ed->bse', x, w)
            return y.reshape(B, S, HEADS, D_K).transpose(0, 2, 1, 3)
        q, k, v = (proj(w_q), proj(w_k), proj(w_v))
        scores = jnp.einsum('bhqd,bhkd->bhqk', q, k) / jnp.sqrt(jnp.float32(D_K))
        attn = jax.nn.softmax(scores, axis=-1)
        out = jnp.einsum('bhqk,bhkd->bhqd', attn, v)
        out = out.transpose(0, 2, 1, 3).reshape(B, S, HIDDEN)
        return jnp.einsum('bse,oe->bso', out, w_o)

    def _L2_ffn_ref(x, gate_w, up_w, down_w, gate_scale, up_scale, down_scale):
        import jax, jax.numpy as jnp
        import numpy as np
        HIDDEN = 512
        INTER = 1376
        BATCH, SEQ = (2, 256)

        def _ternary(key, shape):
            return jax.random.randint(key, shape, -1, 2).astype(jnp.float32)
        gate = jnp.einsum('bsh,ih->bsi', x, gate_w) * gate_scale
        up = jnp.einsum('bsh,ih->bsi', x, up_w) * up_scale
        inter = jax.nn.silu(gate) * up
        out = jnp.einsum('bsi,hi->bsh', inter, down_w) * down_scale
        return out

    def _L3_attn_ref(x, w_down, b_down, w_up, b_up, gate1, hy_in_w, hy_conv_w, hy_conv_b, hy_dt_bias, hy_A_log, hy_D, hy_fcD_w, hy_norm_w, hy_out_w):
        import jax, jax.numpy as jnp
        import numpy as np
        HID = 512
        DM = 128
        DIN = 2 * DM
        DST = 16
        HD = 64
        NH = DIN // HD
        DCONV = 7
        CONV_DIM = DIN + 2 * DST
        DIN_PROJ = 2 * DIN + 2 * DST + 2 * NH
        SEQ, BATCH = (256, 4)

        def _causal_conv(x, w, b):
            y = jax.lax.conv_general_dilated(jnp.transpose(x, (0, 2, 1)), w, (1,), [(DCONV - 1, 0)], feature_group_count=CONV_DIM, dimension_numbers=('NCH', 'OIH', 'NCH'))
            return jnp.transpose(y, (0, 2, 1)) + b

        def _ssm_scan(x, dt, A, B, C):
            dA = jnp.exp(dt * A)
            dBx = dt[..., None] * x

            def step(h, t):
                dA_t, dBx_t, B_t, C_t = t
                h = dA_t[:, :, None, None] * h + dBx_t[..., None] * B_t[:, None, None, :]
                y = jnp.einsum('bhpn,bn->bhp', h, C_t)
                return (h, y)
            h0 = jnp.zeros((x.shape[0], NH, HD, DST), x.dtype)
            _, ys = jax.lax.scan(step, h0, (jnp.moveaxis(dA, 1, 0), jnp.moveaxis(dBx, 1, 0), jnp.moveaxis(B, 1, 0), jnp.moveaxis(C, 1, 0)))
            return jnp.moveaxis(ys, 0, 1)

        def _hydra(u, in_w, conv_w, conv_b, dt_bias, A_log, D, fcD_w, norm_w, out_w):
            b, l, _ = u.shape
            zxbcdt = u @ in_w.T
            z = zxbcdt[..., :DIN]
            xBC = zxbcdt[..., DIN:DIN + CONV_DIM]
            dt2 = zxbcdt[..., DIN + CONV_DIM:]
            dt_fw = jax.nn.softplus(dt2[..., :NH] + dt_bias)
            dt_bw = jax.nn.softplus(jnp.flip(dt2[..., NH:], 1) + dt_bias)
            xBC = jax.nn.silu(_causal_conv(xBC, conv_w, conv_b))
            xs = xBC[..., :DIN]
            Bm = xBC[..., DIN:DIN + DST]
            Cm = xBC[..., DIN + DST:]
            A = -jnp.exp(A_log)
            x4 = xs.reshape(b, l, NH, HD)
            y_fw = _ssm_scan(x4, dt_fw, A, Bm, Cm).reshape(b, l, DIN)
            y_bw = jnp.flip(_ssm_scan(jnp.flip(x4, 1), dt_bw, A, jnp.flip(Bm, 1), jnp.flip(Cm, 1)).reshape(b, l, DIN), 1)
            zero = jnp.zeros((b, 1, DIN), u.dtype)
            y = jnp.concatenate([zero, y_fw[:, :-1]], 1) + jnp.concatenate([y_bw[:, 1:], zero], 1)
            y = y + xs * jnp.repeat(xs @ fcD_w.T + D, HD, axis=-1)
            yz = y * jax.nn.silu(z)
            y = yz * jax.lax.rsqrt(jnp.mean(jnp.square(yz), -1, keepdims=True) + 1e-05) * norm_w
            return y @ out_w.T
        x_init = x
        h = x @ w_down.T + b_down
        h = jnp.transpose(h, (1, 0, 2))
        h = jax.nn.gelu(h, approximate=False)
        xmid = h
        hp = (hy_in_w, hy_conv_w, hy_conv_b, hy_dt_bias, hy_A_log, hy_D, hy_fcD_w, hy_norm_w, hy_out_w)
        h = _hydra(h, *hp)
        h = _hydra(h, *hp)
        alpha = jax.nn.sigmoid(gate1)
        h = alpha * xmid + (1.0 - alpha) * h
        h = xmid + h
        h = h @ w_up.T + b_up
        return x_init + jnp.transpose(h, (1, 0, 2))

    def _L3_ffn_ref(x, gate_w, base_w, base_b, lora_A, lora_B):
        import jax, jax.numpy as jnp
        import numpy as np
        B, S, D_IN, D_OUT = (2, 256, 512, 512)
        E, K, R = (8, 2, 16)
        SCALING = 32.0 / 16.0
        gate_logits = jnp.einsum('bsd,ed->bse', x, gate_w)
        weights, selected = jax.lax.top_k(gate_logits, K)
        weights = jax.nn.softmax(weights.astype(jnp.float32), axis=2).astype(x.dtype)
        result = jnp.einsum('bsd,od->bso', x, base_w) + base_b
        w_full = jnp.sum(jax.nn.one_hot(selected, E, dtype=x.dtype) * weights[..., None], axis=2)
        low = jnp.einsum('bsd,erd->ebsr', x, lora_A)
        lora_out = jnp.einsum('ebsr,eor,bse->bso', low, lora_B, w_full)
        result = result + SCALING * lora_out
        return result
    x = L0_attn_hidden_states
    x = x + _layernorm(_L0_attn_ref(_layernorm(x, axis=-1), L0_attn_Wq_a, L0_attn_q_a_ln_w, L0_attn_Wq_b, L0_attn_Wkv_a, L0_attn_kv_a_ln_w, L0_attn_Wkv_b, L0_attn_Wo), axis=-1)
    x = x + _layernorm(_L0_ffn_ref(_layernorm(x, axis=-1), L0_ffn_weight, L0_ffn_bias, L0_ffn_lora_A, L0_ffn_lora_B, L0_ffn_lora_start_indices), axis=-1)
    x = x + _layernorm(_L1_attn_ref(_layernorm(x, axis=-1), L1_attn_wq, L1_attn_bq, L1_attn_wk, L1_attn_bk, L1_attn_wv, L1_attn_bv), axis=-1)
    x = x + _layernorm(_L1_ffn_ref(_layernorm(x, axis=-1), L1_ffn_weight), axis=-1)
    x = x + _layernorm(_L2_attn_ref(_layernorm(x, axis=-1), L2_attn_w_q, L2_attn_w_k, L2_attn_w_v, L2_attn_w_o), axis=-1)
    x = x + _layernorm(_L2_ffn_ref(_layernorm(x, axis=-1), L2_ffn_gate_w, L2_ffn_up_w, L2_ffn_down_w, L2_ffn_gate_scale, L2_ffn_up_scale, L2_ffn_down_scale), axis=-1)
    x = x + _layernorm(_L3_attn_ref(_layernorm(x, axis=-1), L3_attn_w_down, L3_attn_b_down, L3_attn_w_up, L3_attn_b_up, L3_attn_gate1, L3_attn_hy_in_w, L3_attn_hy_conv_w, L3_attn_hy_conv_b, L3_attn_hy_dt_bias, L3_attn_hy_A_log, L3_attn_hy_D, L3_attn_hy_fcD_w, L3_attn_hy_norm_w, L3_attn_hy_out_w), axis=-1)
    x = x + _layernorm(_L3_ffn_ref(_layernorm(x, axis=-1), L3_ffn_gate_w, L3_ffn_base_w, L3_ffn_base_b, L3_ffn_lora_A, L3_ffn_lora_B), axis=-1)
    return x

_drawn_inputs = setup_inputs


def setup_inputs(seed=0):
    import zlib

    import numpy as np

    out = dict(_drawn_inputs(seed))
    spreads = {'L0_attn_q_a_ln_w': (1.0, 0.6),
     'L0_attn_kv_a_ln_w': (1.0, 0.2),
     'L3_attn_b_down': (0.0, 0.8),
     'L3_attn_b_up': (0.0, 0.277),
     'L3_attn_hy_conv_b': (0.0, 0.8),
     'L3_attn_hy_D': (1.0, 0.6),
     'L3_attn_hy_norm_w': (1.0, 0.6)}
    factors = {'L0_ffn_bias': 6.066,
     'L1_attn_wq': 3.333,
     'L1_attn_bq': 8.0,
     'L1_attn_wk': 3.106,
     'L1_attn_bk': 8.0,
     'L1_ffn_weight': 64.0,
     'L2_attn_w_q': 3.299,
     'L2_attn_w_k': 3.257,
     'L3_attn_hy_in_w': 8.0,
     'L3_attn_hy_conv_w': 8.0,
     'L3_attn_hy_fcD_w': 8.0,
     'L3_attn_hy_out_w': 8.0,
     'L3_ffn_base_b': 4.93}
    for name, (base, spread) in spreads.items():
        noise = np.random.default_rng([zlib.crc32(name.encode()), seed]).standard_normal(out[name].shape)
        drawn = base * np.exp(spread * noise) if base else spread * noise
        out[name] = jnp.asarray(drawn.astype(out[name].dtype))
    for name, factor in factors.items():
        out[name] = (out[name] * factor).astype(out[name].dtype)
    return out
```

```python
from contextlib import ExitStack

import numpy as np

import concourse.bass as bass
from concourse import mybir

P = 128
T = 1024
NT = T // P
D = 512
KC = D // P
LN_EPS = 1e-5

ALU = mybir.AluOpType
ACT = mybir.ActivationFunctionType
AX = mybir.AxisListType
F32 = mybir.dt.float32
BF16 = mybir.dt.bfloat16
U32 = mybir.dt.uint32
I32 = mybir.dt.int32

LAYERS = ("L0_attn", "L0_ffn", "L1_attn", "L1_ffn", "L2_attn", "L2_ffn", "L3_attn", "L3_ffn",)


class Chip:

    def __init__(self, nc, ctx, consts):
        self.nc, self.ctx = nc, ctx
        self.consts = consts
        self.x = self.sb("x", [P, NT, D])
        self.f = self.sb("f", [P, NT, D])
        self.yT = self.sb("yT", [P, KC, T])
        self.ident = self.sb("ident", [P, P])
        self.neghalf = self.sb("neghalf", [P, 16])
        self.stats = self.sb("stats", [P, NT, 6])
        self.moments = self.sb("moments", [P, NT, 2])
        self.var = self.sb("var", [P, NT])
        self.rstd = self.sb("rstd", [P, NT])
        self.shift = self.sb("shift", [P, NT])
        self.ps = ctx.enter_context(nc.psum_tensor("ps", [P, 8, 512], F32))
        self.count = {}
        self.sems = {}

    def sb(self, name, shape, dt=F32):
        return self.ctx.enter_context(self.nc.sbuf_tensor(name, shape, dt))

    def sem(self, name):
        if name not in self.sems:
            self.sems[name] = self.ctx.enter_context(self.nc.semaphore(name))
            self.count[name] = 0
        return self.sems[name]

    def base(self, name):
        self.sem(name)
        return self.count[name]

    def spent(self, **rises):
        for name, n in rises.items():
            self.sem(name)
            self.count[name] += n


def start(chip, x_dram):
    nc = chip.nc
    s_load = chip.sem("start_loaded")
    s_const = chip.sem("const_written")
    with nc.Block() as block:
        @block.sync
        def _(sp):
            xv = x_dram.rearrange("a (t p) d -> p (a t) d", p=P)
            for h in range(2):
                sp.dma_start(chip.x[:, 4 * h:4 * h + 4, :], xv[:, 4 * h:4 * h + 4, :]).then_inc(s_load, 16)
            sp.dma_start(chip.ident[:], chip.consts["ident"]).then_inc(s_load, 16)
            sp.wait_ge(s_load, 48)

        @block.vector
        def _(dve):
            nc.vector.memset(chip.neghalf[:], -0.5).then_inc(s_const, 1)


def renorm(chip, name, add_f, out_dram=None, loads=None):
    nc = chip.nc
    x, f, stats, mom, ps = chip.x, chip.f, chip.stats, chip.moments, chip.ps
    s_stats, s_var, s_rstd, s_shift = (chip.sem(n) for n in ("ln_stats", "ln_var", "ln_rstd", "ln_shift"))
    s_scaled, s_added, s_turned, s_out = (chip.sem(n) for n in ("ln_scaled", "ln_added", "ln_turned", "x_stored"))
    b_stats, b_var, b_rstd, b_shift = (chip.base(n) for n in ("ln_stats", "ln_var", "ln_rstd", "ln_shift"))
    b_scaled, b_added, b_turned = (chip.base(n) for n in ("ln_scaled", "ln_added", "ln_turned"))
    last = out_dram is not None
    passes = ([f] if add_f else []) + ([] if last else [x])

    with nc.Block() as block:
        @block.sync
        def _(sp):
            if loads:
                loads(sp)
            if last:
                ov = out_dram.rearrange("a (t p) d -> p (a t) d", p=P)
                for t in range(NT):
                    sp.wait_ge(s_added, b_added + t + 1)
                    sp.dma_start(ov[:, t, :], x[:, t, :]).then_inc(s_out, 16)
                sp.wait_ge(s_out, 16 * NT)

        @block.vector
        def _(dve):
            for n, src in enumerate(passes):
                for t in range(NT):
                    if src is x and add_f:
                        dve.wait_ge(s_added, b_added + t + 1)
                    nc.vector.bn_stats(stats[:, t, :], src[:, t, :]).then_inc(s_stats, 1)
                for t in range(NT):
                    dve.wait_ge(s_stats, b_stats + 16 * n + t + 1)
                    nc.vector.bn_aggr(mom[:, t, :], stats[:, t, :]).then_inc(s_stats, 1)
                dve.wait_ge(s_stats, b_stats + 16 * n + 16)
                nc.vector.tensor_scalar(chip.var[:], mom[:, :, 1], LN_EPS, None, ALU.add).then_inc(s_var, 1)
                dve.wait_ge(s_rstd, b_rstd + n + 1)
                nc.vector.scalar_tensor_tensor(out=chip.shift[:], in0=mom[:, :, 0], scalar=-1.0, in1=chip.rstd[:],
                                               op0=ALU.mult, op1=ALU.mult).then_inc(s_shift, 1)
                if src is f:
                    for t in range(NT):
                        dve.wait_ge(s_scaled, b_scaled + t + 1)
                        nc.vector.tensor_tensor(x[:, t, :], x[:, t, :], f[:, t, :], ALU.add).then_inc(s_added, 1)
            if not last:
                for t in range(1, NT, 2):
                    dve.wait_ge(s_turned, b_turned + t + 1)
                    nc.vector.tensor_copy(chip.yT[:, :, t * P:(t + 1) * P],
                                          ps[:, t, :].rearrange("p (c q) -> p c q", c=KC))

        @block.gpsimd
        def _(pool):
            for n in range(len(passes)):
                pool.wait_ge(s_var, b_var + n + 1)
                nc.gpsimd.tensor_tensor(chip.rstd[:], chip.var[:], chip.neghalf[:, 0:NT],
                                        ALU.pow).then_inc(s_rstd, 1)

        @block.scalar
        def _(act):
            for n, src in enumerate(passes):
                act.wait_ge(s_shift, b_shift + n + 1)
                for t in range(NT):
                    if n and add_f:
                        act.wait_ge(s_added, b_added + t + 1)
                    nc.scalar.activation(f[:, t, :], src[:, t, :], ACT.Identity, bias=chip.shift[:, t:t + 1],
                                         scale=chip.rstd[:, t:t + 1]).then_inc(s_scaled, 1)
            if not last:
                for t in range(0, NT, 2):
                    act.wait_ge(s_turned, b_turned + t + 1)
                    nc.scalar.copy(chip.yT[:, :, t * P:(t + 1) * P],
                                   ps[:, t, :].rearrange("p (c q) -> p c q", c=KC))

        @block.tensor
        def _(pe):
            if last:
                return
            for t in range(NT):
                pe.wait_ge(s_scaled, b_scaled + NT * (len(passes) - 1) + t + 1)
                for c in range(KC):
                    mm = nc.tensor.transpose(ps[:, t, c * P:(c + 1) * P], f[:, t, c * P:(c + 1) * P], chip.ident[:])
                mm.then_inc(s_turned, 1)

    n = len(passes)
    chip.spent(ln_stats=16 * n, ln_var=n, ln_rstd=n, ln_shift=n, ln_scaled=NT * n,
               ln_added=NT * add_f, ln_turned=NT * (not last))


def weights_view(w):
    return w.rearrange("(c p) m -> p c m", p=P)


def l0_ffn(chip, add_f, W, bias, A, B, starts, want):
    nc, ps, yT = chip.nc, chip.ps, chip.yT
    NA, R = 3, 16
    s_w = chip.sem("l0f_loaded")
    s_m, s_low, s_lowT, s_row = (chip.sem("l0f_" + n) for n in ("mask", "low", "lowT", "rows"))
    with ExitStack() as mem:
        w = mem.enter_context(nc.sbuf_tensor("l0f_w", [P, KC, D], F32))
        a = mem.enter_context(nc.sbuf_tensor("l0f_a", [P, KC, NA * R], F32))
        b = mem.enter_context(nc.sbuf_tensor("l0f_b", [NA * R, D], F32))
        bb = mem.enter_context(nc.sbuf_tensor("l0f_bias", [P, D], F32))
        st = mem.enter_context(nc.sbuf_tensor("l0f_starts", [NA * R, 4], I32))
        stf = mem.enter_context(nc.sbuf_tensor("l0f_startsf", [NA * R, 4], F32))
        wt = mem.enter_context(nc.sbuf_tensor("l0f_want", [NA * R, 1], F32))
        m = mem.enter_context(nc.sbuf_tensor("l0f_mask", [NA * R, 2], F32))
        lowT = mem.enter_context(nc.sbuf_tensor("l0f_lowT", [NA * R, T], F32))

        def loads(sp):
            sp.dma_start(a[:], weights_view(A)).then_inc(s_w, 16)
            sp.dma_start(b[:], B).then_inc(s_w, 16)
            sp.dma_start(st[:], starts.partition_broadcast(NA * R)).then_inc(s_w, 16)
            sp.dma_start(wt[:], want).then_inc(s_w, 16)
            sp.dma_start(w[:], weights_view(W)).then_inc(s_w, 16)
            sp.dma_start(bb[:], bias.partition_broadcast(P)).then_inc(s_w, 16)

        renorm(chip, "l0f", add_f, loads=loads)
        with nc.Block() as block:
            @block.vector
            def _(dve):
                dve.wait_ge(s_w, 96)
                nc.vector.tensor_copy(stf[:], st[:]).then_inc(s_m, 1)
                dve.wait_ge(s_m, 1)
                nc.vector.tensor_scalar(stf[:], stf[:], 0.0, None, ALU.is_le).then_inc(s_m, 1)
                dve.wait_ge(s_m, 2)
                nc.vector.reduce_sum(m[:, 0:1], stf[:], AX.X).then_inc(s_m, 1)
                dve.wait_ge(s_m, 3)
                nc.vector.tensor_tensor(m[:, 1:2], m[:, 0:1], wt[:], ALU.is_equal).then_inc(s_m, 1)
                dve.wait_ge(s_m, 4)
                for h in range(2):
                    dve.wait_ge(s_low, h + 1)
                    nc.vector.tensor_scalar(lowT[:, 512 * h:512 * h + 512], ps[0:NA * R, h, :], m[:, 1:2], None,
                                            ALU.mult).then_inc(s_lowT, 1)
                for t in range(NT):
                    dve.wait_ge(s_row, t + 1)
                    nc.vector.tensor_tensor(chip.f[:, t, :], ps[:, (2 + t) % 8, :], bb[:], ALU.add)

            @block.tensor
            def _(pe):
                pe.wait_ge(s_w, 96)
                for h in range(2):
                    for c in range(KC):
                        mm = nc.tensor.matmul(ps[0:NA * R, h, :], a[:, c, :], yT[:, c, 512 * h:512 * h + 512],
                                              start=c == 0, stop=c == KC - 1)
                    mm.then_inc(s_low, 1)
                pe.wait_ge(s_lowT, 2)
                for t in range(NT):
                    out = ps[:, (2 + t) % 8, :]
                    for c in range(KC):
                        nc.tensor.matmul(out, yT[:, c, t * P:(t + 1) * P], w[:, c, :], start=c == 0, stop=False)
                    nc.tensor.matmul(out, lowT[:, t * P:(t + 1) * P], b[:], start=False, stop=True).then_inc(s_row, 1)


def l1_ffn(chip, add_f, W):
    nc, ps, yT = chip.nc, chip.ps, chip.yT
    s_w, s_b, s_t, s_wT, s_row = (chip.sem("l1f_" + n) for n in ("loaded", "binary", "turned", "wT", "rows"))
    with ExitStack() as mem:
        w = mem.enter_context(nc.sbuf_tensor("l1f_w", [P, KC, D], F32))
        pos = mem.enter_context(nc.sbuf_tensor("l1f_pos", [P, KC, D], F32))
        neg = mem.enter_context(nc.sbuf_tensor("l1f_neg", [P, KC, D], F32))
        wT = mem.enter_context(nc.sbuf_tensor("l1f_wT", [P, KC, D], F32))
        sc = mem.enter_context(nc.sbuf_tensor("l1f_scale", [P, KC], F32))

        def loads(sp):
            sp.dma_start(w[:], weights_view(W)).then_inc(s_w, 16)

        renorm(chip, "l1f", add_f, loads=loads)
        with nc.Block() as block:
            @block.vector
            def _(dve):
                dve.wait_ge(s_w, 16)
                n = 0
                nc.vector.tensor_reduce(sc[:], w[:], AX.X, ALU.add, apply_absolute_value=True).then_inc(s_b, 1)
                dve.wait_ge(s_b, 1)
                nc.vector.tensor_scalar(sc[:], sc[:], 1.0 / D, None, ALU.mult).then_inc(s_b, 1)
                dve.wait_ge(s_b, 2)
                for o in range(KC):
                    k = 2 + 6 * o
                    nc.vector.tensor_scalar(pos[:, o, :], w[:, o, :], 0.0, sc[:, o:o + 1], ALU.is_gt,
                                            ALU.mult).then_inc(s_b, 1)
                    nc.vector.tensor_scalar(neg[:, o, :], w[:, o, :], 0.0, sc[:, o:o + 1], ALU.is_lt,
                                            ALU.mult).then_inc(s_b, 1)
                    nc.vector.tensor_scalar(w[:, o, :], w[:, o, :], 1.0, -1.0, ALU.min, ALU.max).then_inc(s_b, 1)
                    dve.wait_ge(s_b, k + 3)
                    nc.vector.tensor_tensor(pos[:, o, :], pos[:, o, :], neg[:, o, :], ALU.subtract).then_inc(s_b, 1)
                    dve.wait_ge(s_b, k + 4)
                    nc.vector.tensor_tensor(pos[:, o, :], pos[:, o, :], w[:, o, :], ALU.subtract).then_inc(s_b, 1)
                    dve.wait_ge(s_b, k + 5)
                    nc.vector.tensor_tensor(pos[:, o, :], pos[:, o, :], w[:, o, :], ALU.add).then_inc(s_b, 1)
                for t in range(1, NT, 2):
                    dve.wait_ge(s_row, t + 1)
                    nc.vector.tensor_copy(chip.f[:, t, :], ps[:, (4 + t) % 8, :])

            @block.scalar
            def _(act):
                for o in range(KC):
                    act.wait_ge(s_t, o + 1)
                    nc.scalar.copy(wT[:, :, o * P:(o + 1) * P],
                                   ps[:, o, :].rearrange("p (c q) -> p c q", c=KC)).then_inc(s_wT, 1)
                for t in range(0, NT, 2):
                    act.wait_ge(s_row, t + 1)
                    nc.scalar.copy(chip.f[:, t, :], ps[:, (4 + t) % 8, :])

            @block.tensor
            def _(pe):
                for o in range(KC):
                    pe.wait_ge(s_b, 2 + 6 * (o + 1))
                    for c in range(KC):
                        mm = nc.tensor.transpose(ps[:, o, c * P:(c + 1) * P], pos[:, o, c * P:(c + 1) * P],
                                                 chip.ident[:])
                    mm.then_inc(s_t, 1)
                pe.wait_ge(s_wT, KC)
                for t in range(NT):
                    for c in range(KC):
                        mm = nc.tensor.matmul(ps[:, (4 + t) % 8, :], yT[:, c, t * P:(t + 1) * P], wT[:, c, :],
                                              start=c == 0, stop=c == KC - 1)
                    mm.then_inc(s_row, 1)


def l2_ffn(chip, add_f, G, U, DN, gs, us, ds):
    nc, ps, yT = chip.nc, chip.ps, chip.yT
    INTER = 1376
    FULL = INTER // P
    REST = INTER - FULL * P
    NM = FULL + 1
    s_w = [chip.sem(f"l2f_loaded{i}") for i in range(3)]
    s_d, s_s, s_g, s_silu, s_h, s_row, s_sc = (
        chip.sem("l2f_" + n) for n in ("down_loaded", "scales_loaded", "gate_up", "silu", "hidden", "rows", "scaled"))
    cuts = [0, 2 * P, 6 * P, INTER]
    with ExitStack() as mem:
        g = mem.enter_context(nc.sbuf_tensor("l2f_g", [P, KC, INTER], F32))
        u = mem.enter_context(nc.sbuf_tensor("l2f_u", [P, KC, INTER], F32))
        dn = mem.enter_context(nc.sbuf_tensor("l2f_dn", [P, NM, D], F32))
        hT = mem.enter_context(nc.sbuf_tensor("l2f_hT", [P, NM, T], F32))
        silu = mem.enter_context(nc.sbuf_tensor("l2f_silu", [P, 2, 512], F32))
        sc = mem.enter_context(nc.sbuf_tensor("l2f_sc", [P, 3], F32))

        def loads(sp):
            for i, s in enumerate((gs, us, ds)):
                sp.dma_start(sc[:, i:i + 1], s.partition_broadcast(P)).then_inc(s_s, 16)
            for i in range(3):
                sp.dma_start(g[:, :, cuts[i]:cuts[i + 1]], weights_view(G)[:, :, cuts[i]:cuts[i + 1]]).then_inc(s_w[i], 16)
                sp.dma_start(u[:, :, cuts[i]:cuts[i + 1]], weights_view(U)[:, :, cuts[i]:cuts[i + 1]]).then_inc(s_w[i], 16)
            sp.dma_start(dn[:, 0:FULL, :], DN[0:FULL * P, :].rearrange("(c p) m -> p c m", p=P)).then_inc(s_d, 16)
            sp.dma_start(dn[0:REST, FULL, :], DN[FULL * P:, :]).then_inc(s_d, 16)

        renorm(chip, "l2f", add_f, loads=loads)
        jobs = [(m, h) for m in range(NM) for h in range(2)]
        with nc.Block() as block:
            @block.tensor
            def _(pe):
                for n, (m, h) in enumerate(jobs):
                    M = P if m < FULL else REST
                    for i in range(3):
                        if h == 0 and m * P == cuts[i]:
                            pe.wait_ge(s_w[i], 32)
                    if n >= 3:
                        pe.wait_ge(s_h, n - 2)
                    for k, wt in enumerate((g, u)):
                        for c in range(KC):
                            mm = nc.tensor.matmul(ps[0:M, 2 * (n % 3) + k, :], wt[:, c, m * P:m * P + M],
                                                  yT[:, c, 512 * h:512 * h + 512], start=c == 0, stop=c == KC - 1)
                    mm.then_inc(s_g, 1)
                pe.wait_ge(s_d, 32)
                pe.wait_ge(s_h, len(jobs))
                for t in range(NT):
                    if t >= 2:
                        pe.wait_ge(s_row, t - 1)
                    for m in range(NM):
                        M = P if m < FULL else REST
                        mm = nc.tensor.matmul(ps[:, 6 + t % 2, :], hT[0:M, m, t * P:(t + 1) * P], dn[0:M, m, :],
                                              start=m == 0, stop=m == NM - 1)
                    mm.then_inc(s_sc, 1)

            @block.scalar
            def _(act):
                act.wait_ge(s_s, 48)
                for n, (m, h) in enumerate(jobs):
                    M = P if m < FULL else REST
                    act.wait_ge(s_g, n + 1)
                    if n >= 2:
                        act.wait_ge(s_h, n - 1)
                    nc.scalar.activation(silu[0:M, n % 2, :], ps[0:M, 2 * (n % 3), :], ACT.Silu,
                                         scale=sc[0:M, 0:1]).then_inc(s_silu, 1)

            @block.vector
            def _(dve):
                dve.wait_ge(s_s, 48)
                for n, (m, h) in enumerate(jobs):
                    M = P if m < FULL else REST
                    dve.wait_ge(s_silu, n + 1)
                    nc.vector.scalar_tensor_tensor(out=hT[0:M, m, 512 * h:512 * h + 512],
                                                   in0=ps[0:M, 2 * (n % 3) + 1, :], scalar=sc[0:M, 1:2],
                                                   in1=silu[0:M, n % 2, :], op0=ALU.mult,
                                                   op1=ALU.mult).then_inc(s_h, 1)
                for t in range(NT):
                    dve.wait_ge(s_sc, t + 1)
                    nc.vector.tensor_scalar(chip.f[:, t, :], ps[:, 6 + t % 2, :], sc[:, 2:3], None,
                                            ALU.mult).then_inc(s_row, 1)


def l3_attn(chip, add_f, WD, bd, WU, bu, gate, IN, conv_w, conv_b, Dh, FCD, norm_w, OUT):
    nc, ps, yT = chip.nc, chip.ps, chip.yT
    DIN, NH = 2 * P, 4
    s_w, s_pr, s_e, s_xm = (chip.sem("l3a_" + n) for n in ("loaded", "prepared", "gate_exp", "mid"))
    s_pe, s_act, s_dve, s_pool = (chip.sem("l3a_" + n) for n in ("pe_done", "act_done", "dve_done", "pool_done"))
    with ExitStack() as mem:
        def sb(name, shape, dt=F32):
            return mem.enter_context(nc.sbuf_tensor("l3a_" + name, shape, dt))
        wd = sb("wd", [P, KC, P])
        wu = sb("wu", [P, D])
        bub = sb("bu", [P, D])
        win = sb("in", [P, 2 * DIN])
        wout = sb("out", [P, 2, P])
        fc = sb("fc", [P, 2, NH])
        fcr = sb("fcr", [P, 2, NH, 64])
        col = sb("col", [P, 16])
        mid = sb("mid", [P, T])
        u = sb("u", [P, T])
        z = sb("z", [P, 2, T])
        xs = sb("xs", [P, 2, T])
        yz = sb("yz", [P, 2, T])
        sq = sb("sq", [P, 2, T])
        ones = sb("ones", [P, 2])
        ms = sb("ms", [P, NT])
        rs = sb("rs", [P, NT])
        urow = sb("urow", [P, NT, P])
        al = sb("al", [P, 4])
        BD, CW, CB, DD, NW, GT = 0, 1, 3, 5, 7, 9
        NL = 14 + NH

        def loads(sp):
            def ld(dst, src):
                sp.dma_start(dst, src).then_inc(s_w, 16)
            ld(wd[:], weights_view(WD))
            ld(win[:], IN[:, 0:2 * DIN])
            ld(fc[:], FCD.rearrange("(c p) h -> p c h", p=P))
            ld(wout[:], weights_view(OUT))
            ld(wu[:], WU)
            ld(bub[:], bu.partition_broadcast(P))
            ld(col[:, BD:BD + 1], bd.rearrange("(p a) -> p a", a=1))
            for c in range(2):
                ld(col[:, CW + c:CW + c + 1], conv_w[c * P:(c + 1) * P])
                ld(col[:, CB + c:CB + c + 1], conv_b[c * P:(c + 1) * P])
                ld(col[:, NW + c:NW + c + 1], norm_w[c * P:(c + 1) * P])
            ld(col[:, GT:GT + 1], gate.partition_broadcast(P))
            for h in range(NH):
                ld(col[64 * (h % 2):64 * (h % 2) + 64, DD + h // 2:DD + h // 2 + 1],
                   Dh[h:h + 1].partition_broadcast(64))

        renorm(chip, "l3a", add_f, loads=loads)
        with nc.Block() as block:
            @block.vector
            def _(dve):
                dve.wait_ge(s_w, 16 * NL)
                n = [0]

                def step(ins):
                    n[0] += 1
                    ins.then_inc(s_pr, 1)
                step(nc.vector.memset(ones[:], 1.0))
                step(nc.vector.tensor_copy(fcr[:], fc[:].unsqueeze(3).broadcast_to([P, 2, NH, 64])))
                for c in range(2):
                    step(nc.vector.tensor_scalar(wout[:, c, :], wout[:, c, :], col[:, NW + c:NW + c + 1], None, ALU.mult))
                dve.wait_ge(s_e, 1)
                step(nc.vector.tensor_scalar(al[:, 1:2], al[:, 0:1], 1.0, None, ALU.add))
                dve.wait_ge(s_pr, 5)
                step(nc.vector.reciprocal(al[:, 2:3], al[:, 1:2]))
                dve.wait_ge(s_pr, 6)
                step(nc.vector.tensor_scalar(al[:, 3:4], al[:, 2:3], -1.0, 1.0, ALU.mult, ALU.add))
                step(nc.vector.tensor_scalar(al[:, 1:2], al[:, 2:3], 1.0, None, ALU.add))
                dve.wait_ge(s_pr, 8)

            @block.scalar
            def _(act):
                act.wait_ge(s_w, 16 * NL)
                nc.scalar.activation(al[:, 0:1], col[:, GT:GT + 1], ACT.Exp, scale=-1.0).then_inc(s_e, 1)
                for h in range(2):
                    act.wait_ge(s_pe, h + 1)
                    nc.scalar.activation(mid[:, 512 * h:512 * h + 512], ps[:, h, :], ACT.Gelu,
                                         bias=col[:, BD:BD + 1])

            @block.tensor
            def _(pe):
                pe.wait_ge(s_w, 16 * NL)
                for h in range(2):
                    for c in range(KC):
                        mm = nc.tensor.matmul(ps[:, h, :], wd[:, c, :], yT[:, c, 512 * h:512 * h + 512],
                                              start=c == 0, stop=c == KC - 1)
                    mm.then_inc(s_pe, 1)
        chip.spent(l3a_pe_done=2)
        for r in range(2):
            src = mid if r == 0 else u
            bp, ba, bv, bo = (chip.base("l3a_" + n) for n in ("pe_done", "act_done", "dve_done", "pool_done"))
            with nc.Block() as block:
                @block.tensor
                def _(pe):
                    for m in range(4):
                        for h in range(2):
                            nc.tensor.matmul(ps[:, 2 * m + h, :], win[:, m * P:(m + 1) * P],
                                             src[:, 512 * h:512 * h + 512], start=True, stop=True).then_inc(s_pe, 1)
                    pe.wait_ge(s_act, ba + 8)
                    for m in range(2):
                        for h in range(2):
                            for c in range(2):
                                mm = nc.tensor.matmul(ps[:, 2 * m + h, :],
                                                      fcr[:, c, 2 * m:2 * m + 2, :].rearrange("p a b -> p (a b)"),
                                                      xs[:, c, 512 * h:512 * h + 512], start=c == 0, stop=c == 1)
                            mm.then_inc(s_pe, 1)
                    pe.wait_ge(s_act, ba + 12)
                    for t in range(NT):
                        for c in range(2):
                            mm = nc.tensor.matmul(ps[:, 4, t:t + 1], sq[:, c, t * P:(t + 1) * P], ones[:, 0:1],
                                                  start=c == 0, stop=c == 1)
                    mm.then_inc(s_pe, 1)
                    for t in range(NT):
                        for c in range(2):
                            mm = nc.tensor.matmul(ps[:, 5 + t // 4, (t % 4) * P:(t % 4 + 1) * P],
                                                  yz[:, c, t * P:(t + 1) * P], wout[:, c, :],
                                                  start=c == 0, stop=c == 1)
                    mm.then_inc(s_pe, 1)
                    for t in range(NT):
                        pe.wait_ge(s_act, ba + 13 + t)
                        mm = nc.tensor.transpose(ps[:, t // 4, (t % 4) * P:(t % 4 + 1) * P], urow[:, t, :],
                                                 chip.ident[:])
                    mm.then_inc(s_pe, 1)

                @block.scalar
                def _(act):
                    for m in range(4):
                        for h in range(2):
                            act.wait_ge(s_pe, bp + 2 * m + h + 1)
                            if m < 2:
                                nc.scalar.activation(z[:, m, 512 * h:512 * h + 512], ps[:, 2 * m + h, :],
                                                     ACT.Silu).then_inc(s_act, 1)
                            else:
                                nc.scalar.activation(xs[:, m - 2, 512 * h:512 * h + 512], ps[:, 2 * m + h, :],
                                                     ACT.Silu, bias=col[:, CB + m - 2:CB + m - 1],
                                                     scale=col[:, CW + m - 2:CW + m - 1]).then_inc(s_act, 1)
                    for m in range(2):
                        for h in range(2):
                            act.wait_ge(s_dve, bv + 2 * (2 * m + h) + 2)
                            nc.scalar.activation(sq[:, m, 512 * h:512 * h + 512], yz[:, m, 512 * h:512 * h + 512],
                                                 ACT.Square).then_inc(s_act, 1)
                    act.wait_ge(s_pool, bo + 1)
                    act.wait_ge(s_pe, bp + 14)
                    for t in range(NT):
                        nc.scalar.activation(urow[:, t, :], ps[:, 5 + t // 4, (t % 4) * P:(t % 4 + 1) * P], ACT.Copy,
                                             scale=rs[:, t:t + 1]).then_inc(s_act, 1)

                @block.vector
                def _(dve):
                    k = 0
                    for m in range(2):
                        for h in range(2):
                            cut = slice(512 * h, 512 * h + 512)
                            dve.wait_ge(s_pe, bp + 8 + k + 1)
                            nc.vector.scalar_tensor_tensor(out=yz[:, m, cut], in0=ps[:, 2 * m + h, :],
                                                           scalar=col[:, DD + m:DD + m + 1], in1=xs[:, m, cut],
                                                           op0=ALU.add, op1=ALU.mult).then_inc(s_dve, 1)
                            dve.wait_ge(s_dve, bv + 2 * k + 1)
                            nc.vector.tensor_tensor(yz[:, m, cut], yz[:, m, cut], z[:, m, cut],
                                                    ALU.mult).then_inc(s_dve, 1)
                            k += 1
                    dve.wait_ge(s_pe, bp + 13)
                    nc.vector.tensor_scalar(ms[:], ps[:, 4, 0:NT], 1.0 / DIN, 1e-5, ALU.mult,
                                            ALU.add).then_inc(s_dve, 1)
                    dve.wait_ge(s_pe, bp + 15)
                    for h in range(2):
                        cut = slice(512 * h, 512 * h + 512)
                        if r == 0:
                            nc.vector.tensor_copy(u[:, cut], ps[:, h, :])
                        else:
                            nc.vector.tensor_scalar(mid[:, cut], mid[:, cut], al[:, 1:2], None,
                                                    ALU.mult).then_inc(s_dve, 1)
                            dve.wait_ge(s_dve, bv + 10 + h)
                            nc.vector.scalar_tensor_tensor(out=u[:, cut], in0=ps[:, h, :], scalar=al[:, 3:4],
                                                           in1=mid[:, cut], op0=ALU.mult, op1=ALU.add)

                @block.gpsimd
                def _(pool):
                    pool.wait_ge(s_dve, bv + 9)
                    nc.gpsimd.tensor_tensor(rs[:], ms[:], chip.neghalf[:, 0:NT], ALU.pow).then_inc(s_pool, 1)
            chip.spent(l3a_pe_done=15, l3a_act_done=20, l3a_dve_done=9 + 2 * r, l3a_pool_done=1)
        bp, bv = chip.base("l3a_pe_done"), chip.base("l3a_dve_done")
        with nc.Block() as block:
            @block.tensor
            def _(pe):
                for t in range(NT):
                    nc.tensor.matmul(ps[:, t, :], u[:, t * P:(t + 1) * P], wu[:], start=True, stop=True).then_inc(s_pe, 1)

            @block.vector
            def _(dve):
                for t in range(NT):
                    dve.wait_ge(s_pe, bp + t + 1)
                    nc.vector.tensor_tensor(chip.f[:, t, :], chip.f[:, t, :], ps[:, t, :], ALU.add).then_inc(s_dve, 1)
                    if t:
                        dve.wait_ge(s_dve, bv + t)
                        nc.vector.tensor_tensor(chip.f[:, t - 1, :], chip.f[:, t - 1, :], bub[:], ALU.add)
                dve.wait_ge(s_dve, bv + NT)
                nc.vector.tensor_tensor(chip.f[:, NT - 1, :], chip.f[:, NT - 1, :], bub[:], ALU.add)


def l3_ffn(chip, add_f, GT, W, bias, A, B, iota):
    nc, ps, yT = chip.nc, chip.ps, chip.yT
    E, R = 8, 16
    s_w, s_low, s_r, s_e, s_lw, s_t, s_lT = (
        chip.sem("l3f_" + n) for n in ("loaded", "low", "route", "exp", "weighted", "turned", "lowT"))
    with ExitStack() as mem:
        def sb(name, shape, dt=F32):
            return mem.enter_context(nc.sbuf_tensor("l3f_" + name, shape, dt))
        w = sb("w", [P, KC, D])
        ag = sb("ag", [P, KC, E * R + E])
        b = sb("b", [P, D])
        bb = sb("bb", [P, D])
        io = sb("io", [P, E])
        lg = sb("lg", [P, NT, E])
        top = sb("top", [P, NT, E])
        idx = sb("idx", [P, NT, E], U32)
        idf = sb("idf", [P, NT, E])
        dd = sb("dd", [P, NT, 4])
        m1 = sb("m1", [P, NT, E])
        m2 = sb("m2", [P, NT, E])
        low = sb("low", [P, NT, E * R])
        lowT = sb("lowT", [P, T])

        def loads(sp):
            def ld(dst, src):
                sp.dma_start(dst, src).then_inc(s_w, 16)
            ld(ag[:, :, 0:E * R], weights_view(A))
            ld(ag[:, :, E * R:], weights_view(GT))
            ld(io[:], iota.partition_broadcast(P))
            ld(b[:], B)
            ld(bb[:], bias.partition_broadcast(P))
            ld(w[:], weights_view(W))

        renorm(chip, "l3f", add_f, loads=loads)
        N = E * R + E
        with nc.Block() as block:
            @block.tensor
            def _(pe):
                pe.wait_ge(s_w, 96)
                for t in range(NT):
                    for c in range(KC):
                        mm = nc.tensor.matmul(ps[:, t // 2, (t % 2) * 256:(t % 2) * 256 + N],
                                              yT[:, c, t * P:(t + 1) * P], ag[:, c, :], start=c == 0, stop=c == KC - 1)
                mm.then_inc(s_low, 1)
                for t in range(NT):
                    pe.wait_ge(s_lw, t + 1)
                    mm = nc.tensor.transpose(ps[:, 4 + t // 4, (t % 4) * P:(t % 4 + 1) * P], low[:, t, :],
                                             chip.ident[:])
                    if t % 4 == 3:
                        mm.then_inc(s_t, 1)
                for t in range(NT):
                    if t == 0:
                        pe.wait_ge(s_lT, 2)
                    bank = (6, 7, 0, 1, 2, 3, 4, 5)[t]
                    for c in range(KC):
                        nc.tensor.matmul(ps[:, bank, :], yT[:, c, t * P:(t + 1) * P], w[:, c, :], start=c == 0, stop=False)
                    nc.tensor.matmul(ps[:, bank, :], lowT[:, t * P:(t + 1) * P], b[:], start=False,
                                     stop=True).then_inc(s_t, 1)

            @block.vector
            def _(dve):
                dve.wait_ge(s_w, 96)
                dve.wait_ge(s_low, 1)
                nc.vector.tensor_copy(lg[:], ps[:, 0:4, :].rearrange("p b (a n) -> p (b a) n", a=2)[:, :, E * R:N]
                                      ).then_inc(s_r, 1)
                dve.wait_ge(s_r, 1)
                for t in range(NT):
                    nc.vector.max(top[:, t, :], lg[:, t, :]).then_inc(s_r, 1)
                for t in range(NT):
                    dve.wait_ge(s_r, 2 + t)
                    nc.vector.max_index(idx[:, t, :], top[:, t, :], lg[:, t, :]).then_inc(s_r, 1)
                nc.vector.tensor_tensor(dd[:, :, 0], top[:, :, 1], top[:, :, 0], ALU.subtract).then_inc(s_r, 1)
                dve.wait_ge(s_r, 17)
                nc.vector.tensor_copy(idf[:], idx[:]).then_inc(s_r, 1)
                dve.wait_ge(s_r, 19)
                iob = io[:].unsqueeze(1).broadcast_to([P, NT, E])
                nc.vector.tensor_tensor(m1[:], iob, idf[:, :, 0:1].broadcast_to([P, NT, E]), ALU.is_equal).then_inc(s_r, 1)
                nc.vector.tensor_tensor(m2[:], iob, idf[:, :, 1:2].broadcast_to([P, NT, E]), ALU.is_equal).then_inc(s_r, 1)
                dve.wait_ge(s_e, 1)
                nc.vector.tensor_scalar(dd[:, :, 2], dd[:, :, 1], 1.0, 0.5, ALU.add, ALU.mult).then_inc(s_r, 1)
                dve.wait_ge(s_r, 22)
                nc.vector.reciprocal(dd[:, :, 3], dd[:, :, 2]).then_inc(s_r, 1)
                nc.vector.tensor_tensor(m2[:], m2[:], dd[:, :, 1:2].broadcast_to([P, NT, E]), ALU.mult).then_inc(s_r, 1)
                dve.wait_ge(s_r, 24)
                nc.vector.tensor_tensor(m1[:], m1[:], m2[:], ALU.add).then_inc(s_r, 1)
                dve.wait_ge(s_r, 25)
                nc.vector.tensor_tensor(m1[:], m1[:], dd[:, :, 3:4].broadcast_to([P, NT, E]), ALU.mult).then_inc(s_r, 1)
                dve.wait_ge(s_r, 26)
                for t in range(NT):
                    nc.vector.tensor_tensor(
                        low[:, t, :].rearrange("p (e r) -> p e r", e=E),
                        ps[:, t // 2, (t % 2) * 256:(t % 2) * 256 + E * R].rearrange("p (e r) -> p e r", e=E),
                        m1[:, t, :].unsqueeze(2).broadcast_to([P, E, R]), ALU.mult).then_inc(s_lw, 1)
                for h in range(2):
                    dve.wait_ge(s_t, h + 1)
                    nc.vector.tensor_copy(lowT[:, 512 * h:512 * h + 512], ps[:, 4 + h, :]).then_inc(s_lT, 1)
                for t in range(NT):
                    dve.wait_ge(s_t, 2 + t + 1)
                    nc.vector.tensor_tensor(chip.f[:, t, :], ps[:, (6, 7, 0, 1, 2, 3, 4, 5)[t], :], bb[:], ALU.add)

            @block.scalar
            def _(act):
                act.wait_ge(s_r, 18)
                nc.scalar.activation(dd[:, :, 1], dd[:, :, 0], ACT.Exp).then_inc(s_e, 1)


HD = 16
HEADS = 32
GROUP = 4
GROUPS = HEADS // GROUP
Q_RUNS = [(0, 3), (1, 2), (2, 1)]
K_RUNS = [(0, 3), (0, 2), (0, 1)]
ROWS = 6 * HD
MAX_ROW = ROWS
EXT = MAX_ROW + 1


def rows_out(chip, name, W):
    nc, ps, f, yT = chip.nc, chip.ps, chip.f, chip.yT
    s_w, s_t, s_c, s_row = (chip.sem(name + n) for n in ("_out_loaded", "_out_turned", "_out_copied", "_out_rows"))
    with ExitStack() as mem:
        w = mem.enter_context(nc.sbuf_tensor(name + "_wo", [P, KC, D], F32))
        with nc.Block() as block:
            @block.sync
            def _(sp):
                sp.dma_start(w[:], weights_view(W)).then_inc(s_w, 16)

            @block.tensor
            def _(pe):
                for t in range(NT):
                    for c in range(KC):
                        mm = nc.tensor.transpose(ps[:, t, c * P:(c + 1) * P], f[:, t, c * P:(c + 1) * P], chip.ident[:])
                    mm.then_inc(s_t, 1)
                pe.wait_ge(s_w, 16)
                for t in range(NT):
                    pe.wait_ge(s_c, t + 1)
                    for c in range(KC):
                        mm = nc.tensor.matmul(ps[:, t, :], yT[:, c, t * P:(t + 1) * P], w[:, c, :],
                                              start=c == 0, stop=c == KC - 1)
                    mm.then_inc(s_row, 1)

            @block.scalar
            def _(act):
                for t in range(NT):
                    act.wait_ge(s_t, t + 1)
                    nc.scalar.copy(yT[:, :, t * P:(t + 1) * P],
                                   ps[:, t, :].rearrange("p (c q) -> p c q", c=KC)).then_inc(s_c, 1)

            @block.vector
            def _(dve):
                for t in range(NT):
                    dve.wait_ge(s_row, t + 1)
                    nc.vector.tensor_copy(f[:, t, :], ps[:, t, :])


def split_qkv(chip, name, mem, a, kv_heads, rope, add_f, q_parts, k_parts, vext):
    nc, ps, yT = chip.nc, chip.ps, chip.yT
    NV = kv_heads * HD

    def sb(n, shape, dt=F32):
        return mem.enter_context(nc.sbuf_tensor(f"{name}_{n}", shape, dt))
    wq, wk, wv = sb("wq", [P, KC, D]), sb("wk", [P, KC, NV]), sb("wv", [P, KC, NV])
    if rope:
        cos, sin = sb("cos", [P, T]), sb("sin", [P, T])
        bq, bk, bv = sb("bq", [P, 4]), sb("bk", [P, 2]), sb("bv", [P, NV])
        ab, tmp = sb("ab", [P, 2, 2, T]), sb("tmp", [P, 2, 2, T])
    res = sb("res", [P, 2, T])
    part = sb("part", [P, 2, 3, T], BF16)
    rest = sb("rest", [P, 2, T])
    s_w, s_mm, s_bias, s_rot, s_res, s_part, s_v, s_one = (
        chip.sem(f"{name}_{n}") for n in ("loaded", "qk", "biased", "rotated", "result", "high_mid", "v", "v_rows"))
    s_store = [chip.sem(f"{name}_stored{i}") for i in range(2)]
    s_pt, s_lo = chip.sem(f"{name}_pool_rotated"), chip.sem(f"{name}_rest_low")

    units = []
    if rope:
        for g in range(2):
            units.append((wq, bq, [(2 * h + g) * P for h in range(2)], [2 * h + g for h in range(2)], P,
                          [q_parts[:, 16 * g:16 * g + 16, 8 * h:8 * h + 8, :] for h in range(2)]))
        units.append((wk, bk, [0, 64], [0, 1], 64, [k_parts[:, :, 8 * h:8 * h + 8, :] for h in range(2)]))
    else:
        for w, dst in ((wq, q_parts), (wk, k_parts)):
            for m in range(4):
                units.append((w, None, [m * P], [0], P, [dst[:, 8 * m:8 * m + 8, :, :]]))
    NL = 3 + (5 if rope else 0)
    tiles = [(u, i) for u, unit in enumerate(units) for i in range(len(unit[2]))]
    per = 2 if rope else 1

    def loads(sp):
        def ld(dst, src):
            sp.dma_start(dst, src).then_inc(s_w, 16)
        ld(wq[:], weights_view(a[name + "_wq"]))
        ld(wk[:], weights_view(a[name + "_wk"]))
        ld(wv[:], weights_view(a[name + "_wv"]))
        if rope:
            ld(cos[:], a[name + "_cos"])
            ld(sin[:], a[name + "_sin"])
            ld(bq[:], a[name + "_bq"])
            ld(bk[0:64, :], a[name + "_bk"])
            ld(bv[:], a[name + "_bv"].partition_broadcast(P))

    renorm(chip, name, add_f, loads=loads)

    def tile_of(n):
        M = units[tiles[n][0]][4]
        return res[0:M, n % 2, :] if rope else ps[0:M, 2 * (n % 2):2 * (n % 2) + 2, :].rearrange("p b n -> p (b n)")

    with nc.Block() as block:
        @block.tensor
        def _(pe):
            pe.wait_ge(s_w, 16 * NL)
            for u, (w, _, cols, _, M, _) in enumerate(units):
                for i, col in enumerate(cols):
                    bank = (4 * (u % 2) + 2 * i) if rope else 2 * (u % 2)
                    if u >= 2:
                        pe.wait_ge(s_bias if rope else s_lo, 2 * (u - 1) if rope else 2 * u - 3)
                    for h in range(2):
                        for c in range(KC):
                            mm = nc.tensor.matmul(ps[0:M, bank + h, :], w[:, c, col:col + M],
                                                  yT[:, c, 512 * h:512 * h + 512], start=c == 0, stop=c == KC - 1)
                    mm.then_inc(s_mm, 1)
            if rope:
                pe.wait_ge(s_bias, 2 * len(units))
            for t in range(NT):
                if t >= 4:
                    pe.wait_ge(s_v, t - 3)
                for c in range(KC):
                    mm = nc.tensor.matmul(ps[:, 4 + t % 4, 0:NV], yT[:, c, t * P:(t + 1) * P], wv[:, c, :],
                                          start=c == 0, stop=c == KC - 1)
                mm.then_inc(s_one, 1)

        @block.scalar
        def _(act):
            n = 0
            for u, (_, b, cols, bc, M, _) in enumerate(units):
                if rope:
                    for i in range(2):
                        act.wait_ge(s_mm, 2 * u + i + 1)
                        if u >= 2:
                            act.wait_ge(s_res, u - 1)
                            act.wait_ge(s_pt, 3 * (u - 1))
                        bank = 4 * (u % 2) + 2 * i
                        nc.scalar.activation(ab[0:M, u % 2, i, :],
                                             ps[0:M, bank:bank + 2, :].rearrange("p b n -> p (b n)"),
                                             ACT.Identity, bias=b[0:M, bc[i]:bc[i] + 1]).then_inc(s_bias, 1)
                for i in range(len(cols)):
                    if rope and i == 0:
                        act.wait_ge(s_res, u + 1)
                    elif rope:
                        act.wait_ge(s_pt, 3 * u + 3)
                    else:
                        act.wait_ge(s_mm, n + 1)
                    if n >= 2:
                        act.wait_ge(s_store[n % 2], 48 * (n // 2))
                    nc.scalar.copy(part[0:M, n % 2, 0, :], tile_of(n)).then_inc(s_part, 1)
                    act.wait_ge(s_lo, 2 * n + 1)
                    nc.scalar.copy(part[0:M, n % 2, 1, :], rest[0:M, n % 2, :]).then_inc(s_part, 1)
                    n += 1

        @block.gpsimd
        def _(pool):
            nc.gpsimd.memset(vext[:, :, :, HD:2 * HD], 1.0)
            if rope:
                for u, (_, _, _, _, M, _) in enumerate(units):
                    pool.wait_ge(s_bias, 2 * u + 2)
                    nc.gpsimd.tensor_tensor(tmp[0:M, 1, 0, :], ab[0:M, u % 2, 0, :], sin[0:M, :], ALU.mult).then_inc(s_pt, 1)
                    nc.gpsimd.tensor_tensor(tmp[0:M, 1, 1, :], ab[0:M, u % 2, 1, :], cos[0:M, :], ALU.mult).then_inc(s_pt, 1)
                    pool.wait_ge(s_pt, 3 * u + 2)
                    if u >= 1:
                        pool.wait_ge(s_lo, 4 * u - 1)
                    nc.gpsimd.tensor_tensor(res[0:M, 1, :], tmp[0:M, 1, 0, :], tmp[0:M, 1, 1, :], ALU.add).then_inc(s_pt, 1)

        @block.vector
        def _(dve):
            n = 0
            for u, (_, _, cols, _, M, _) in enumerate(units):
                if rope:
                    dve.wait_ge(s_bias, 2 * u + 2)
                    nc.vector.tensor_tensor(tmp[0:M, 0, 0, :], ab[0:M, u % 2, 0, :], cos[0:M, :], ALU.mult).then_inc(s_rot, 1)
                    nc.vector.tensor_tensor(tmp[0:M, 0, 1, :], ab[0:M, u % 2, 1, :], sin[0:M, :], ALU.mult).then_inc(s_rot, 1)
                    dve.wait_ge(s_rot, 2 * u + 2)
                    nc.vector.tensor_tensor(res[0:M, 0, :], tmp[0:M, 0, 0, :], tmp[0:M, 0, 1, :], ALU.subtract).then_inc(s_res, 1)
                for i in range(len(cols)):
                    if rope and i == 1:
                        dve.wait_ge(s_pt, 3 * u + 3)
                    dve.wait_ge(s_part, 2 * n + 1)
                    nc.vector.tensor_tensor(rest[0:M, n % 2, :], tile_of(n), part[0:M, n % 2, 0, :],
                                            ALU.subtract).then_inc(s_lo, 1)
                    dve.wait_ge(s_part, 2 * n + 2)
                    nc.vector.tensor_tensor(part[0:M, n % 2, 2, :], rest[0:M, n % 2, :], part[0:M, n % 2, 1, :],
                                            ALU.subtract).then_inc(s_lo, 1)
                    n += 1
            for t in range(NT):
                dve.wait_ge(s_one, t + 1)
                src = ps[:, 4 + t % 4, 0:NV].rearrange("p (h e) -> p h e", e=HD)
                if rope:
                    nc.vector.tensor_tensor(vext[:, t, :, 0:HD], src, bv[:].rearrange("p (h e) -> p h e", e=HD),
                                            ALU.add).then_inc(s_v, 1)
                else:
                    nc.vector.tensor_copy(vext[:, t, :, 0:HD], src).then_inc(s_v, 1)

        @block.sync
        def _(sp):
            for n, (u, i) in enumerate(tiles):
                M, dst = units[u][4], units[u][5][i]
                for k in range(3):
                    sp.wait_ge((s_part, s_part, s_lo)[k], 2 * n + (1, 2, 2)[k])
                    sp.dma_start(dst[k], part[0:M, n % 2, k, :]).then_inc(s_store[n % 2], 16)
            for i in range(2):
                sp.wait_ge(s_store[i], 48 * (len(tiles) // 2))


def small_attn(chip, add_f, name, a, kv_heads, rope):
    nc, ps, f = chip.nc, chip.ps, chip.f
    KH = GROUP if kv_heads == HEADS else 1
    SCALE = float(HD) ** -0.5
    q_parts = nc.dram_tensor(f"{name}_q_parts", (3, HEADS, HD, T), BF16).ap()
    k_parts = nc.dram_tensor(f"{name}_k_parts", (3, kv_heads, HD, T), BF16).ap()
    with ExitStack() as outer:
        vext = outer.enter_context(nc.sbuf_tensor(f"{name}_vext", [P, NT, kv_heads, 2 * HD], F32))
        with ExitStack() as mem:
            split_qkv(chip, name, mem, a, kv_heads, rope, add_f, q_parts, k_parts, vext)
        attend(chip, name, outer, a, KH, SCALE, q_parts, k_parts, vext)
    if not rope:
        rows_out(chip, name, a[name + "_wo"])


def attend(chip, name, mem, a, KH, SCALE, q_parts, k_parts, vext):
    nc, ps, f = chip.nc, chip.ps, chip.f

    def sb(n, shape, dt=F32):
        return mem.enter_context(nc.sbuf_tensor(f"{name}_{n}", shape, dt))
    q6 = sb("q6", [EXT, 2, GROUP, T], BF16)
    k6 = sb("k6", [EXT, 2, KH, T], BF16)
    prob = sb("prob", [P, 2 * GROUP, T])
    vst = sb("vst", [P, 2, NT, KH, 2 * HD])
    osb = sb("osb", [P, T])
    mx = sb("mx", [P, GROUP, NT, 2])
    mcol = sb("mcol", [P, NT, GROUP], BF16)
    mrow = sb("mrow", [GROUP, T], BF16)
    ident16 = sb("ident16", [P, P], BF16)
    rden = sb("rden", [P, NT, GROUP])
    s_ld = [chip.sem(f"{name}_heads_loaded{i}") for i in range(2)]
    (s_c, s_v, s_mm, s_red0, s_red1, s_neg, s_mt, s_mrow, s_row, s_st, s_exp, s_pv, s_oev, s_ot, s_rd, s_out,
     s_ones) = (
        chip.sem(f"{name}_{n}") for n in (
            "consts", "v_staged", "max_scores", "reduced0", "reduced1", "negated", "max_turned",
            "max_rows", "max_stored", "scores", "exps", "pv", "o_out", "o_turned", "recip", "o_done", "rows_of_ones"))
    ST = [ps[:, 0:2, :], ps[:, 2:4, :]]
    O = ps[:, 4:6, :]
    MB = [ps[:, 6, :], ps[:, 7, :]]
    STEPS = NT * GROUP
    TILES = GROUP * NT
    LOADS = 16 * 12
    FIRST_STEP, MAX_STEPS, TURN_STEP = 3, 24, 27

    def tiles_at(s):
        return [m for m in range(TILES) if FIRST_STEP + m * MAX_STEPS // TILES == s]

    def kh(hh):
        return hh if KH == GROUP else 0

    with nc.Block() as block:
        @block.sync
        def _(sp):
            sp.dma_start(ident16[:], a["ident16"]).then_inc(s_c, 16)

            def load(g, par):
                row = 0
                for part, n in Q_RUNS:
                    src = q_parts[part, bass.ds(g * GROUP, GROUP)].rearrange("h r t -> r h t")
                    for k in range(n):
                        sp.dma_start(q6[row:row + HD, par, :, :], src).then_inc(s_ld[par], 16)
                        row += HD
                row = 0
                for part, n in K_RUNS:
                    for k in range(n):
                        src = k_parts[part + k, bass.ds(g * KH, KH)].rearrange("h r t -> r h t")
                        sp.dma_start(k6[row:row + HD, par, :, :], src).then_inc(s_ld[par], 16)
                        row += HD

            def place_max(g, par):
                sp.wait_ge(s_mrow, g + 1)
                sp.dma_start(q6[MAX_ROW:EXT, par, :, :], mrow[:]).then_inc(s_row, 16)

            def reload(g, par):
                sp.wait_ge(s_pv, (g - 1) * NT)
                load(g, par)

            load(0, 0)
            load(1, 1)
            place_max(0, 0)
            place_max(1, 1)
            with sp.Fori(1, GROUPS // 2) as i:
                reload(i * 2, 0)
                place_max(i * 2, 0)
                reload(i * 2 + 1, 1)
                place_max(i * 2 + 1, 1)

        @block.gpsimd
        def _(pool):
            def stage(g, par):
                nc.gpsimd.tensor_copy(vst[:, par, :, :, :], vext[:, :, bass.ds(g * KH, KH), :]).then_inc(s_v, 1)
            stage(0, 0)
            stage(1, 1)
            with pool.Fori(1, GROUPS // 2) as i:
                pool.wait_ge(s_pv, (i * 2 - 1) * NT)
                stage(i * 2, 0)
                pool.wait_ge(s_pv, i * 2 * NT)
                stage(i * 2 + 1, 1)

        @block.tensor
        def _(pe):
            def max_tile(g, par, turn, m):
                hh, qt = m // NT, m % NT
                if m == 0:
                    pe.wait_ge(s_ld[par], turn * LOADS + LOADS)
                for c in range(2):
                    if m:
                        pe.wait_ge((s_red0, s_red1)[c], g * TILES + m)
                    nc.tensor.matmul(MB[c], q6[0:ROWS, par, hh, qt * P:(qt + 1) * P],
                                     k6[0:ROWS, par, kh(hh), 512 * c:512 * c + 512],
                                     start=True, stop=True).then_inc(s_mm, 1)

            def max_turn(g):
                pe.wait_ge(s_neg, g + 1)
                for t in range(NT):
                    mm = nc.tensor.transpose(MB[0].bitcast(BF16)[0:GROUP, t * P:(t + 1) * P], mcol[:, t, :],
                                             ident16[:])
                mm.then_inc(s_mt, 1)

            def scores(g, par, s):
                j, hh = s // GROUP, s % GROUP
                if s == 0:
                    pe.wait_ge(s_row, g * 16 + 16)
                for c in range(2):
                    mm = nc.tensor.matmul(ST[s % 2][:, c, :], k6[:, par, kh(hh), j * P:(j + 1) * P],
                                          q6[:, par, hh, 512 * c:512 * c + 512], start=True, stop=True)
                mm.then_inc(s_st, 1)

            def pv(g, par, j, c):
                for hh in range(GROUP):
                    mm = nc.tensor.matmul(O[32 * hh:32 * hh + 32, c, :], vst[:, par, j, kh(hh), :],
                                          prob[:, (j % 2) * GROUP + hh, 512 * c:512 * c + 512],
                                          start=j == 0, stop=j == NT - 1)
                if c:
                    mm.then_inc(s_pv, 1)

            def o_turn(g):
                pe.wait_ge(s_oev, g + 1)
                for t in range(NT):
                    mm = nc.tensor.transpose(MB[t // 4][:, (t % 4) * P:(t % 4 + 1) * P], osb[:, t * P:(t + 1) * P],
                                             chip.ident[:])
                mm.then_inc(s_ot, 1)

            def group(g, par, next_turn, first, last):
                for s in range(STEPS):
                    pe.wait_ge(s_exp, g * STEPS + s + 1)
                    if s + 2 < STEPS:
                        scores(g, par, s + 2)
                    elif not last:
                        scores(g + 1, 1 - par, s + 2 - STEPS)
                    if s == 2 and not first:
                        o_turn(g - 1)
                    if s == FIRST_STEP and not first and not last:
                        pe.wait_ge(s_out, g)
                    tiles = [] if last else tiles_at(s)
                    for m in tiles[:1]:
                        max_tile(g + 1, 1 - par, next_turn, m)
                    if s == GROUP - 1:
                        pe.wait_ge(s_v, g + 1)
                        if not first:
                            pe.wait_ge(s_oev, g)
                    if s % GROUP == GROUP - 1:
                        pv(g, par, s // GROUP, 0)
                    if s % GROUP == 0 and s:
                        pv(g, par, s // GROUP - 1, 1)
                    if s == STEPS - 1:
                        pv(g, par, NT - 1, 1)
                    for m in tiles[1:]:
                        max_tile(g + 1, 1 - par, next_turn, m)
                    if s == TURN_STEP and not last:
                        max_turn(g + 1)

            pe.wait_ge(s_ones, 1)
            pe.wait_ge(s_c, 16)
            for m in range(TILES):
                max_tile(0, 0, 0, m)
            max_turn(0)
            scores(0, 0, 0)
            scores(0, 0, 1)
            group(0, 0, 0, True, False)
            with pe.Fori(0, GROUPS // 2 - 1) as i:
                group(i * 2 + 1, 1, i + 1, False, False)
                group(i * 2 + 2, 0, i + 1, False, False)
            group(GROUPS - 1, 1, None, False, True)
            pe.wait_ge(s_out, GROUPS - 1)
            o_turn(GROUPS - 1)

        @block.scalar
        def _(act):
            def max_out(g):
                act.wait_ge(s_mt, g + 1)
                nc.scalar.copy(mrow[:], MB[0].bitcast(BF16)[0:GROUP, :]).then_inc(s_mrow, 1)

            def o_out(g):
                act.wait_ge(s_pv, g * NT + NT)
                nc.scalar.copy(osb[:], O.rearrange("p b n -> p (b n)")).then_inc(s_oev, 1)

            def group(g, first, last):
                for s in range(STEPS):
                    act.wait_ge(s_st, g * STEPS + s + 1)
                    if s % GROUP == 0 and not (first and s < 2 * GROUP):
                        act.wait_ge(s_pv, g * NT + s // GROUP - 1)
                    nc.scalar.activation(prob[:, s % (2 * GROUP), :], ST[s % 2].rearrange("p b n -> p (b n)"),
                                         ACT.Exp, scale=SCALE).then_inc(s_exp, 1)
                    if s == 1 and not first:
                        o_out(g - 1)
                    if s == TURN_STEP + 1 and not last:
                        max_out(g + 1)

            max_out(0)
            group(0, True, False)
            with act.Fori(1, GROUPS - 1) as g:
                group(g, False, False)
            group(GROUPS - 1, False, True)
            o_out(GROUPS - 1)

        @block.vector
        def _(dve):
            def maxima(g):
                for m in range(TILES):
                    hh, qt = m // NT, m % NT
                    dve.wait_ge(s_mm, g * (2 * TILES) + 2 * m + 1)
                    nc.vector.tensor_reduce(mx[:, hh, qt, 0:1], MB[0], AX.X, ALU.max).then_inc(s_red0, 1)
                    dve.wait_ge(s_mm, g * (2 * TILES) + 2 * m + 2)
                    nc.vector.tensor_reduce(mx[:, hh, qt, 1:2], MB[1], AX.X, ALU.max).then_inc(s_red1, 1)
                dve.wait_ge(s_red0, g * TILES + TILES)
                dve.wait_ge(s_red1, g * TILES + TILES)
                nc.vector.tensor_reduce(mcol[:].rearrange("p t h -> p h t"), mx[:], AX.X, ALU.max,
                                        negate=True).then_inc(s_neg, 1)

            def epilogue(g):
                dve.wait_ge(s_ot, g + 1)
                both = ps[:, 6:8, :].rearrange("p b (t h e) -> p (b t) h e", h=GROUP, e=2 * HD)
                nc.vector.reciprocal(rden[:], both[:, :, :, HD]).then_inc(s_rd, 1)
                dve.wait_ge(s_rd, g + 1)
                for hh in range(GROUP):
                    o = nc.vector.tensor_tensor(f[:, :, bass.ds((g * GROUP + hh) * HD, HD)], both[:, :, hh, 0:HD],
                                                rden[:, :, hh:hh + 1].broadcast_to([P, NT, HD]), ALU.mult)
                o.then_inc(s_out, 1)

            nc.vector.memset(k6[MAX_ROW:EXT, :, :, :], 1.0).then_inc(s_ones, 1)
            maxima(0)
            maxima(1)
            with dve.Fori(0, GROUPS - 2) as g:
                epilogue(g)
                maxima(g + 2)
            epilogue(GROUPS - 2)
            epilogue(GROUPS - 1)


MLA_HEADS = 32
Q_RANK, KV_RANK, NOPE, ROPE, VD = 192, 64, 128, 64, 128
HALF = ROPE // 2
RMS_EPS = 1e-6
JOBS = 17
MAX_CHUNKS = []
for _qt in range(NT):
    if _qt < 4:
        MAX_CHUNKS.append((_qt, 0, P * (_qt + 1), P * _qt))
    else:
        MAX_CHUNKS.append((_qt, 0, 512, None))
        MAX_CHUNKS.append((_qt, 1, P * (_qt - 3), P * (_qt - 4)))
NMAX = len(MAX_CHUNKS)


def l0_attn(chip, add_f, a):
    nc, ps = chip.nc, chip.ps
    flat = chip.f[:].rearrange("p t d -> p (t d)")
    qT0, qT1, kT = flat[:, 0:T], flat[:, T:2 * T], flat[:, 2 * T:3 * T]
    cext = flat[:, 3 * T:4 * T].rearrange("p (t e) -> p t e", t=NT)
    with ExitStack() as mem:
        k16 = mem.enter_context(nc.sbuf_tensor("l0a_k16", [P, T], BF16))
        oT = mem.enter_context(nc.sbuf_tensor("l0a_oT", [P, MLA_HEADS // 2, T], F32))
        wo = mem.enter_context(nc.sbuf_tensor("l0a_wo", [P, MLA_HEADS // 2, D], F32))
        with ExitStack() as temp:
            latents(chip, temp, add_f, a, qT0, qT1, kT, k16, cext)
        with ExitStack() as temp:
            mla_heads(chip, temp, a, qT0, qT1, kT, k16, cext, oT, wo)
        s_row = chip.sem("l0a_rows")
        with nc.Block() as block:
            @block.tensor
            def _(pe):
                for t in range(NT):
                    for i in range(MLA_HEADS // 2):
                        mm = nc.tensor.matmul(ps[:, t, :], oT[:, i, t * P:(t + 1) * P], wo[:, i, :],
                                              start=i == 0, stop=i == MLA_HEADS // 2 - 1)
                    mm.then_inc(s_row, 1)

            @block.vector
            def _(dve):
                for t in range(NT):
                    dve.wait_ge(s_row, t + 1)
                    nc.vector.tensor_copy(chip.f[:, t, :], ps[:, t, :])


def latents(chip, mem, add_f, a, qT0, qT1, kT, k16, cext):
    nc, ps, yT = chip.nc, chip.ps, chip.yT
    NW = Q_RANK + KV_RANK + ROPE

    def sb(n, shape, dt=F32):
        return mem.enter_context(nc.sbuf_tensor("l0a_" + n, shape, dt))
    w = sb("wa", [P, KC, NW])
    wkv = sb("wkv", [P, KV_RANK])
    wq = sb("wqn", [P, 2])
    cos, sin = sb("cos_t", [P, NT, HALF]), sb("sin_t", [P, NT, HALF])
    sq = sb("sq", [P, 2, Q_RANK])
    ss, ms, rs = sb("ss", [P, 2, NT]), sb("ms", [P, 2, NT]), sb("rs", [P, 2, NT])
    qn = sb("qn", [P, NT, 2 * P])
    kf = sb("kf", [P, NT, P])
    tmp = sb("tmp", [P, 4, NT, HALF])
    s_w, s_mm, s_sq, s_ms, s_rs, s_qn, s_kf, s_rt, s_z, s_t, s_c = (
        chip.sem("l0a_" + n) for n in ("loaded", "latent", "squares", "mean", "rms", "qn", "kf", "rot", "pad",
                                       "turned", "ready"))

    def loads(sp):
        def ld(dst, src):
            sp.dma_start(dst, src).then_inc(s_w, 16)
        ld(w[:], weights_view(a["l0a_wa"]))
        ld(wkv[:], a["l0a_wkv"].partition_broadcast(P))
        ld(wq[:], a["l0a_wqn"])
        ld(cos[:], a["l0a_cos_t"])
        ld(sin[:], a["l0a_sin_t"])

    renorm(chip, "l0a", add_f, loads=loads)
    with nc.Block() as block:
        @block.tensor
        def _(pe):
            pe.wait_ge(s_w, 80)
            for t in range(NT):
                for c in range(KC):
                    mm = nc.tensor.matmul(ps[:, t, 0:NW], yT[:, c, t * P:(t + 1) * P], w[:, c, :],
                                          start=c == 0, stop=c == KC - 1)
                mm.then_inc(s_mm, 1)
            pe.wait_ge(s_qn, NT)
            pe.wait_ge(s_kf, NT + 2)
            pe.wait_ge(s_z, 2)
            for b in range(3):
                for t in range(NT):
                    src = kf[:, t, :] if b == 2 else qn[:, t, b * P:(b + 1) * P]
                    mm = nc.tensor.transpose(ps[:, 2 * b + t // 4, (t % 4) * P:(t % 4 + 1) * P], src, chip.ident[:])
                mm.then_inc(s_t, 1)

        @block.scalar
        def _(act):
            for t in range(NT):
                act.wait_ge(s_mm, t + 1)
                if t:
                    act.wait_ge(s_sq, 2 * t)
                nc.scalar.activation(sq[:, 0, :], ps[:, t, 0:Q_RANK], ACT.Square,
                                     accum_out=ss[:, 0, t:t + 1]).then_inc(s_sq, 1)
                nc.scalar.activation(sq[:, 1, 0:KV_RANK], ps[:, t, Q_RANK:Q_RANK + KV_RANK], ACT.Square,
                                     accum_out=ss[:, 1, t:t + 1]).then_inc(s_sq, 1)
            act.wait_ge(s_rs, 1)
            act.wait_ge(s_rt, 4)
            for t in range(NT):
                nc.scalar.activation(qn[:, t, 0:Q_RANK], ps[:, t, 0:Q_RANK], ACT.Copy,
                                     scale=rs[:, 0, t:t + 1]).then_inc(s_qn, 1)
            act.wait_ge(s_t, 2)
            nc.scalar.activation(qT0, ps[:, 0:2, :].rearrange("p b n -> p (b n)"), ACT.Copy, scale=wq[:, 0:1])
            nc.scalar.activation(qT1[0:64], ps[0:64, 2:4, :].rearrange("p b n -> p (b n)"), ACT.Copy,
                                 scale=wq[0:64, 1:2])
            act.wait_ge(s_c, 1)
            nc.scalar.copy(k16[:], kT)

        @block.gpsimd
        def _(pool):
            nc.gpsimd.memset(qn[:, :, Q_RANK:2 * P], 0.0).then_inc(s_z, 1)
            nc.gpsimd.memset(cext[:, :, KV_RANK:P], 1.0).then_inc(s_z, 1)
            pool.wait_ge(s_ms, 2)
            nc.gpsimd.tensor_tensor(rs[:].rearrange("p a t -> p (a t)"), ms[:].rearrange("p a t -> p (a t)"),
                                    chip.neghalf[:], ALU.pow).then_inc(s_rs, 1)

        @block.vector
        def _(dve):
            dve.wait_ge(s_w, 80)
            dve.wait_ge(s_mm, NT)
            dve.wait_ge(s_sq, 2 * NT)
            ra = ps[:, 0:NT, Q_RANK + KV_RANK:Q_RANK + KV_RANK + HALF]
            rb = ps[:, 0:NT, Q_RANK + KV_RANK + HALF:NW]
            for k, (x, y) in enumerate(((ra, cos), (rb, sin), (ra, sin), (rb, cos))):
                nc.vector.tensor_tensor(tmp[:, k], x, y[:], ALU.mult).then_inc(s_rt, 1)
            dve.wait_ge(s_rt, 4)
            nc.vector.tensor_tensor(kf[:, :, KV_RANK:KV_RANK + HALF], tmp[:, 0], tmp[:, 1], ALU.subtract).then_inc(s_kf, 1)
            nc.vector.tensor_tensor(kf[:, :, KV_RANK + HALF:P], tmp[:, 2], tmp[:, 3], ALU.add).then_inc(s_kf, 1)
            for k, n in enumerate((Q_RANK, KV_RANK)):
                nc.vector.tensor_scalar(ms[:, k, :], ss[:, k, :], 1.0 / n, RMS_EPS, ALU.mult, ALU.add).then_inc(s_ms, 1)
            dve.wait_ge(s_rs, 1)
            for t in range(NT):
                dve.wait_ge(s_qn, t + 1)
                nc.vector.scalar_tensor_tensor(out=kf[:, t, 0:KV_RANK], in0=ps[:, t, Q_RANK:Q_RANK + KV_RANK],
                                               scalar=rs[:, 1, t:t + 1], in1=wkv[:], op0=ALU.mult,
                                               op1=ALU.mult).then_inc(s_kf, 1)
            dve.wait_ge(s_kf, NT + 2)
            nc.vector.tensor_copy(cext[:, :, 0:KV_RANK], kf[:, :, 0:KV_RANK])
            dve.wait_ge(s_t, 3)
            nc.vector.tensor_copy(kT, ps[:, 4:6, :].rearrange("p b n -> p (b n)")).then_inc(s_c, 1)


def mla_heads(chip, mem, a, qT0, qT1, kT, k16, cext, oT, wo):
    nc, ps = chip.nc, chip.ps
    prob = chip.yT
    SCALE = float(NOPE + ROPE) ** -0.5

    def sb(n, shape, dt=F32):
        return mem.enter_context(nc.sbuf_tensor("l0a_" + n, shape, dt))
    cos, sin = sb("cosT", [P, T]), sb("sinT", [P, T])
    ident16, mask = sb("ident16", [P, P], BF16), sb("mask", [P, P], BF16)
    ones, diag = sb("ones", [NT, P], BF16), sb("diag8", [NT, NT, P])
    wqn, wk, wv = sb("wqnT", [P, 2, Q_RANK]), sb("wkT", [P, 2, KV_RANK]), sb("wvT", [P, 2, KV_RANK])
    woh, wh = sb("woh", [P, 2, D]), sb("wh", [P, 2, 2, P])
    q32, q16 = sb("q32", [P, 2, T]), sb("q16", [P, 2, T], BF16)
    rot = sb("rot", [P, 2, 512])
    mx, mcol = sb("mx", [P, NT, 2]), sb("mcol0", [P, P])
    mrow = sb("mrow", [NT, 2, T], BF16)
    osum = sb("osum", [KV_RANK + 1, T])
    rows8, recip8 = sb("rows8", [P, NT]), sb("recip8", [P, NT])
    rbc = sb("recip_all", [KV_RANK, T])
    recip_row = nc.dram_tensor("l0a_recip_row", (T,), F32).ap()
    s_ld = [chip.sem(f"l0a_weights{i}") for i in range(2)]
    (s_c, s_one, s_absmm, s_abs, s_prj, s_qc, s_rt, s_rope, s_q16, s_womm, s_wo, s_mm, s_red, s_neg, s_mt, s_mrow,
     s_st, s_exp, s_pv, s_os, s_r8, s_rd, s_rst, s_rb, s_on) = (chip.sem("l0h_" + n) for n in (
         "consts", "ones", "absorbed", "absorbed_out", "q", "q_copied", "rot_terms", "rotated", "q16", "vo", "vo_out",
         "max_scores", "reduced", "negated", "max_turned", "max_rows", "scores", "exps", "pv", "o_out", "sums_spread", "recip", "recip_stored",
         "recip_loaded", "o_done"))
    ST = [ps[:, 0:2, :].rearrange("p b n -> p (b n)"), ps[:, 2:4, :].rearrange("p b n -> p (b n)")]
    O = ps[:, 4:6, :].rearrange("p b n -> p (b n)")
    LOADS = 16 * 6
    NH = MLA_HEADS

    def bank(par, k):
        return ps[:, 6 + (par + k) % 2, :]

    def spans(j):
        return [(max(P * j, 512 * c), 512 * c + 512) for c in range(2) if P * j < 512 * c + 512]

    with nc.Block() as block:
        @block.sync
        def _(sp):
            for dst, name in ((cos[64:P, :], "l0a_cosT"), (sin[64:P, :], "l0a_sinT"), (ident16[:], "ident16"),
                              (mask[:], "l0a_mask"), (diag[:], "l0a_diag")):
                sp.dma_start(dst, a[name]).then_inc(s_c, 16)

            def load(n, par):
                def ld(dst, src):
                    sp.dma_start(dst, src).then_inc(s_ld[par], 16)
                one = bass.ds(n, 1)
                ld(wqn[:, par, :], a["l0a_wqnT"][one].rearrange("h p r -> p (h r)"))
                ld(wk[:, par, :], a["l0a_wkT"][one].rearrange("h p r -> p (h r)"))
                ld(wh[:, par, 0, KV_RANK:P], a["l0a_wqpe"][one, 0:P].rearrange("h p r -> p (h r)"))
                ld(wh[0:64, par, 1, KV_RANK:P], a["l0a_wqpe"][one, P:Q_RANK].rearrange("h p r -> p (h r)"))
                ld(wv[:, par, :], a["l0a_wvT"][one].rearrange("h p r -> p (h r)"))
                ld(woh[:, par, :], a["l0a_wo"][one].rearrange("h p r -> p (h r)"))
            load(0, 0)
            load(1, 1)

            def reload(n, par):
                sp.wait_ge(s_womm, n - 1)
                load(n, par)

            def spread(h):
                sp.wait_ge(s_os, h + 1)
                sp.dma_start(rows8[:], osum[KV_RANK:KV_RANK + 1, :]).then_inc(s_r8, 16)
                sp.wait_ge(s_rd, h + 1)
                sp.dma_start(recip_row.rearrange("(p c) -> p c", p=P), recip8[:]).then_inc(s_rst, 16)
                sp.wait_ge(s_rst, h * 16 + 16)
                sp.dma_start(rbc[:], recip_row.partition_broadcast(KV_RANK)).then_inc(s_rb, 16)

            reload(2, 0)
            reload(3, 1)
            spread(0)
            reload(4, 0)
            with sp.Fori(0, NH // 2 - 3) as i:
                spread(i * 2 + 1)
                reload(i * 2 + 5, 1)
                spread(i * 2 + 2)
                reload(i * 2 + 6, 0)
            spread(NH - 5)
            reload(NH - 1, 1)
            with sp.Fori(NH - 4, NH) as h:
                spread(h)

        @block.tensor
        def _(pe):
            def job(h, par, turn, k, first):
                b = bank(par, k)
                if k == 0:
                    pe.wait_ge(s_ld[par], turn * LOADS + LOADS)
                    if not first:
                        pe.wait_ge(s_red, h * NMAX)
                    nc.tensor.matmul(b[:, 0:64], wqn[:, par, 0:P], wk[:, par, :], start=True, stop=True)
                    nc.tensor.matmul(b[0:64, 64:128], wqn[:, par, P:Q_RANK], wk[:, par, :], start=True,
                                     stop=True).then_inc(s_absmm, 1)
                elif k in (1, 2):
                    pe.wait_ge(s_abs, h + 1)
                    if k == 1 and not first:
                        pe.wait_ge(s_mrow, h)
                    cut = slice(512 * (k - 1), 512 * k)
                    nc.tensor.matmul(b, wh[:, par, 0, :], qT0[:, cut], start=True, stop=False)
                    nc.tensor.matmul(b, wh[0:64, par, 1, :], qT1[0:64, cut], start=False, stop=True).then_inc(s_prj, 1)
                elif k == 3:
                    pe.wait_ge(s_qc, h * 2 + 1)
                    pe.wait_ge(s_rope, h * 2 + 1)
                    nc.tensor.matmul(b[0:64, :], wv[:, par, :], woh[:, par, :], start=True, stop=True).then_inc(s_womm, 1)
                elif k < 4 + NMAX:
                    n = k - 4
                    qt, c, width, dg = MAX_CHUNKS[n]
                    if n == 0:
                        pe.wait_ge(s_qc, h * 2 + 2)
                        pe.wait_ge(s_rope, h * 2 + 2)
                        pe.wait_ge(s_q16, h * 2 + 1)
                    elif n == 1:
                        pe.wait_ge(s_wo, h + 1)
                    else:
                        pe.wait_ge(s_red, h * NMAX + n - 1)
                    if n == 4:
                        pe.wait_ge(s_q16, h * 2 + 2)
                    mm = nc.tensor.matmul(b[:, 0:width], q16[:, par, qt * P:(qt + 1) * P], k16[:, 512 * c:512 * c + width],
                                          start=True, stop=dg is None)
                    if dg is not None:
                        mm = nc.tensor.matmul(b[:, dg:dg + P], ident16[:], mask[:], start=False, stop=True)
                    mm.then_inc(s_mm, 1)
                else:
                    pe.wait_ge(s_neg, h + 1)
                    nc.tensor.transpose(b[:, 0:P], mcol[:], chip.ident[:]).then_inc(s_mt, 1)

            def scores(h, par, j):
                if j == 0:
                    pe.wait_ge(s_mrow, h + 1)
                for lo, hi in spans(j):
                    out = ST[j % 2][:, lo:hi]
                    diagonal = lo == P * j
                    nc.tensor.matmul(out, kT[:, j * P:(j + 1) * P], q32[:, par, lo:hi], start=True, stop=False)
                    mm = nc.tensor.matmul(out, ones[:], mrow[:, par, lo:hi], start=False, stop=not diagonal)
                    if diagonal:
                        mm = nc.tensor.matmul(ST[j % 2][:, lo:lo + P], mask[:], ident16[:], start=False, stop=True)
                mm.then_inc(s_st, 1)

            def pv(j):
                for lo, hi in spans(j):
                    mm = nc.tensor.matmul(O[:, lo:hi], cext[:, j, :], prob[:, j % 4, lo:hi], start=j == 0,
                                          stop=j == (3 if hi == 512 else NT - 1))
                mm.then_inc(s_pv, 1)

            PLAN = [(0, 3, 3), (3, 4, 5), (5, 7, 8), (8, 10, 12), (12, 14, 16), (16, 17, 17), (17, 17, 17), (17, 17, 17)]

            def head(h, par, next_turn, first, last):
                for j in range(NT):
                    pe.wait_ge(s_exp, h * NT + j + 1)
                    if j + 2 < NT:
                        scores(h, par, j + 2)
                    elif not last:
                        scores(h + 1, 1 - par, j + 2 - NT)
                    if not last:
                        for k in range(*PLAN[j][0:2]):
                            job(h + 1, 1 - par, next_turn, k, False)
                    if j == 0 and not first:
                        pe.wait_ge(s_os, h)
                    pv(j)
                    if not last:
                        for k in range(*PLAN[j][1:3]):
                            job(h + 1, 1 - par, next_turn, k, False)

            pe.wait_ge(s_c, 80)
            pe.wait_ge(s_one, 3)
            for k in range(JOBS):
                job(0, 0, 0, k, True)
            scores(0, 0, 0)
            scores(0, 0, 1)
            head(0, 0, 0, True, False)
            with pe.Fori(0, NH // 2 - 1) as i:
                head(i * 2 + 1, 1, i + 1, False, False)
                head(i * 2 + 2, 0, i + 1, False, False)
            head(NH - 1, 1, None, False, True)

        @block.scalar
        def _(act):
            def ready(h, par, pair, stage):
                if stage == 0:
                    act.wait_ge(s_absmm, h + 1)
                    nc.scalar.copy(wh[:, par, 0, 0:64], bank(par, 0)[:, 0:64])
                    nc.scalar.copy(wh[0:64, par, 1, 0:64], bank(par, 0)[0:64, 64:128]).then_inc(s_abs, 1)
                elif stage == 1:
                    for c in range(2):
                        act.wait_ge(s_prj, h * 2 + c + 1)
                        nc.scalar.copy(q32[0:64, par, 512 * c:512 * c + 512], bank(par, 1 + c)[0:64, :]).then_inc(s_qc, 1)
                elif stage == 2:
                    act.wait_ge(s_womm, h + 1)
                    nc.scalar.copy(wo[64 * par:64 * par + 64, bass.ds(pair, 1), :].rearrange("p a n -> p (a n)"),
                                   bank(par, 3)[0:64, :]).then_inc(s_wo, 1)
                    cast(h, par, 0)
                elif stage == 3:
                    cast(h, par, 1)

            def cast(h, par, c):
                act.wait_ge(s_rope, h * 2 + c + 1)
                act.wait_ge(s_qc, h * 2 + c + 1)
                nc.scalar.copy(q16[:, par, 512 * c:512 * c + 512], q32[:, par, 512 * c:512 * c + 512]).then_inc(s_q16, 1)

            def head(h, par, next_pair, first, last, second=False):
                for j in range(NT):
                    act.wait_ge(s_st, h * NT + j + 1)
                    if not (first and j < 4):
                        act.wait_ge(s_pv, h * NT + j - 3)
                    nc.scalar.activation(prob[:, j % 4, P * j:T], ST[j % 2][:, P * j:T], ACT.Exp,
                                         scale=SCALE).then_inc(s_exp, 1)
                    if j == 0 and not first:
                        if not second:
                            act.wait_ge(s_on, h - 1)
                        lift(h - 1)
                    if not last:
                        ready(h + 1, 1 - par, next_pair, j)

            def lift(h):
                act.wait_ge(s_pv, h * NT + NT)
                nc.scalar.copy(osum[:], O[0:KV_RANK + 1, :]).then_inc(s_os, 1)

            act.wait_ge(s_one, 3)
            for stage in range(4):
                ready(0, 0, 0, stage)
            head(0, 0, 0, True, False)
            head(1, 1, 1, False, False, second=True)
            head(2, 0, 1, False, False)
            with act.Fori(1, NH // 2 - 1) as i:
                head(i * 2 + 1, 1, i + 1, False, False)
                head(i * 2 + 2, 0, i + 1, False, False)
            head(NH - 1, 1, None, False, True)
            act.wait_ge(s_on, NH - 1)
            lift(NH - 1)

        @block.vector
        def _(dve):
            def prepare(h, par, done=None):
                for c in range(2):
                    cut = slice(512 * c, 512 * c + 512)
                    b = bank(par, 1 + c)
                    dve.wait_ge(s_prj, h * 2 + c + 1)
                    if c:
                        dve.wait_ge(s_rope, h * 2 + 1)
                    nc.vector.tensor_tensor(rot[64:128, 0, :], b[64:128, :], cos[64:128, cut], ALU.mult).then_inc(s_rt, 1)
                    nc.vector.tensor_tensor(rot[64:96, 1, :], b[96:128, :], sin[64:96, cut], ALU.mult).then_inc(s_rt, 1)
                    nc.vector.tensor_tensor(rot[96:128, 1, :], b[64:96, :], sin[96:128, cut], ALU.mult).then_inc(s_rt, 1)
                    dve.wait_ge(s_rt, h * 6 + 3 * c + 3)
                    nc.vector.tensor_tensor(q32[64:128, par, cut], rot[64:128, 0, :], rot[64:128, 1, :],
                                            ALU.add).then_inc(s_rope, 1)
                for n, (qt, c, width, _) in enumerate(MAX_CHUNKS):
                    if n == 6 and done is not None:
                        invert(done)
                    dve.wait_ge(s_mm, h * NMAX + n + 1)
                    nc.vector.tensor_reduce(mx[:, qt, c:c + 1], bank(par, 4 + n)[:, 0:width], AX.X,
                                            ALU.max).then_inc(s_red, 1)
                dve.wait_ge(s_red, h * NMAX + NMAX)
                nc.vector.tensor_reduce(mcol[:, 0:NT], mx[:], AX.X, ALU.max, negate=True).then_inc(s_neg, 1)
                dve.wait_ge(s_mt, h + 1)
                nc.vector.tensor_tensor(mrow[:, par, :].rearrange("r (t q) -> r t q", t=NT),
                                        bank(par, 16)[0:NT, 0:P].unsqueeze(1).broadcast_to([NT, NT, P]), diag[:],
                                        ALU.mult).then_inc(s_mrow, 1)

            def invert(h):
                dve.wait_ge(s_r8, h * 16 + 16)
                nc.vector.reciprocal(recip8[:], rows8[:]).then_inc(s_rd, 1)

            def finish(h, par, pair):
                dve.wait_ge(s_rb, h * 16 + 16)
                nc.vector.tensor_tensor(oT[64 * par:64 * par + 64, bass.ds(pair, 1), :].rearrange("p a n -> p (a n)"),
                                        osum[0:KV_RANK, :], rbc[:], ALU.mult).then_inc(s_on, 1)

            nc.vector.memset(ones[:], 1.0).then_inc(s_one, 1)
            nc.vector.memset(mcol[:], 0.0).then_inc(s_one, 1)
            nc.vector.memset(mx[:, 0:4, 1], -3.0e38).then_inc(s_one, 1)
            dve.wait_ge(s_one, 3)
            dve.wait_ge(s_c, 80)
            prepare(0, 0)
            prepare(1, 1)
            with dve.Fori(0, NH // 2 - 1) as i:
                prepare(i * 2 + 2, 0, i * 2)
                finish(i * 2, 0, i)
                prepare(i * 2 + 3, 1, i * 2 + 1)
                finish(i * 2 + 1, 1, i)
            for h in (NH - 2, NH - 1):
                invert(h)
                finish(h, h % 2, NH // 2 - 1)


def program(nc, a, out):
    with ExitStack() as ctx:
        chip = Chip(nc, ctx, a)
        start(chip, a["x"])
        add_f = False
        for layer in LAYERS:
            if layer == "L0_attn":
                l0_attn(chip, add_f, a)
            if layer == "L0_ffn":
                l0_ffn(chip, add_f, a["l0f_w"], a["l0f_bias"], a["l0f_a"], a["l0f_b"], a["l0f_starts"], a["l0f_want"])
            if layer == "L1_attn":
                small_attn(chip, add_f, "l1a", a, kv_heads=8, rope=True)
            if layer == "L1_ffn":
                l1_ffn(chip, add_f, a["l1f_w"])
            if layer == "L2_attn":
                small_attn(chip, add_f, "l2a", a, kv_heads=32, rope=False)
            if layer == "L2_ffn":
                l2_ffn(chip, add_f, a["l2f_g"], a["l2f_u"], a["l2f_dn"], a["l2f_gs"], a["l2f_us"], a["l2f_ds"])
            if layer == "L3_attn":
                l3_attn(chip, add_f, a["l3a_wd"], a["l3a_bd"], a["l3a_wu"], a["l3a_bu"], a["l3a_gate"], a["l3a_in"],
                        a["l3a_cw"], a["l3a_cb"], a["l3a_d"], a["l3a_fc"], a["l3a_nw"], a["l3a_out"])
            if layer == "L3_ffn":
                l3_ffn(chip, add_f, a["l3f_g"], a["l3f_w"], a["l3f_bias"], a["l3f_a"], a["l3f_b"], a["l3f_iota"])
            add_f = True
        renorm(chip, "end", True, out_dram=out)


def _rope_tables(dim, period):
    inv = (1.0 / np.float32(10000.0) ** (np.arange(0, dim, 2, dtype=np.float32) / np.float32(dim))).astype(np.float32)
    ang = (inv[:, None] * np.arange(T, dtype=np.float32)[None, :]).astype(np.float32)
    return np.cos(ang).astype(np.float32), np.sin(ang).astype(np.float32)


def kernel(**inputs):
    import numpy as _np
    import concourse.bacc as _bacc
    from concourse import mybir as _mybir
    from concourse.bass_utils import run_bass_kernel_spmd as _run

    g = {k: _np.asarray(v) for k, v in inputs.items()}
    h = {"x": g["L0_attn_hidden_states"], "ident": _np.eye(P, dtype=_np.float32)}
    if "L0_ffn" in LAYERS:
        h.update(l0f_w=g["L0_ffn_weight"].T, l0f_bias=g["L0_ffn_bias"],
                 l0f_a=g["L0_ffn_lora_A"].reshape(48, D).T,
                 l0f_b=g["L0_ffn_lora_B"].transpose(0, 2, 1).reshape(48, D),
                 l0f_starts=g["L0_ffn_lora_start_indices"],
                 l0f_want=(_np.arange(48) // 16 + 2).astype(_np.float32).reshape(48, 1))
    if "L1_ffn" in LAYERS:
        h.update(l1f_w=g["L1_ffn_weight"])
    if "L2_ffn" in LAYERS:
        h.update(l2f_g=g["L2_ffn_gate_w"].T, l2f_u=g["L2_ffn_up_w"].T, l2f_dn=g["L2_ffn_down_w"].T,
                 l2f_gs=g["L2_ffn_gate_scale"].reshape(1), l2f_us=g["L2_ffn_up_scale"].reshape(1),
                 l2f_ds=g["L2_ffn_down_scale"].reshape(1))
    if "L3_attn" in LAYERS:
        p = "L3_attn_"
        h.update(l3a_wd=g[p + "w_down"].T, l3a_bd=g[p + "b_down"], l3a_wu=g[p + "w_up"].T, l3a_bu=g[p + "b_up"],
                 l3a_gate=g[p + "gate1"].reshape(1), l3a_in=g[p + "hy_in_w"].T,
                 l3a_cw=g[p + "hy_conv_w"][:, 0, 6].reshape(-1, 1), l3a_cb=g[p + "hy_conv_b"].reshape(-1, 1),
                 l3a_d=g[p + "hy_D"], l3a_fc=g[p + "hy_fcD_w"].T, l3a_nw=g[p + "hy_norm_w"].reshape(-1, 1),
                 l3a_out=g[p + "hy_out_w"].T)
    if "L3_ffn" in LAYERS:
        h.update(l3f_g=g["L3_ffn_gate_w"].T, l3f_w=g["L3_ffn_base_w"].T, l3f_bias=g["L3_ffn_base_b"],
                 l3f_a=g["L3_ffn_lora_A"].reshape(P, D).T,
                 l3f_b=g["L3_ffn_lora_B"].transpose(0, 2, 1).reshape(P, D),
                 l3f_iota=_np.arange(8, dtype=_np.float32))
    import ml_dtypes as _ml
    h.update(ident16=_np.eye(P).astype(_ml.bfloat16))
    if "L1_attn" in LAYERS:
        p = "L1_attn_"
        cos, sin = _rope_tables(HD, T)
        h.update(l1a_wq=g[p + "wq"].reshape(D, HEADS, 2, 8).transpose(0, 2, 1, 3).reshape(D, D),
                 l1a_bq=g[p + "bq"].reshape(HEADS, 2, 8).transpose(1, 0, 2).reshape(4, P).T,
                 l1a_wk=g[p + "wk"].reshape(D, 8, 2, 8).transpose(0, 2, 1, 3).reshape(D, P),
                 l1a_bk=g[p + "bk"].reshape(8, 2, 8).transpose(1, 0, 2).reshape(2, 64).T,
                 l1a_wv=g[p + "wv"], l1a_bv=g[p + "bv"],
                 l1a_cos=_np.tile(cos, (16, 1)), l1a_sin=_np.tile(sin, (16, 1)))
    if "L2_attn" in LAYERS:
        p = "L2_attn_"
        h.update(l2a_wq=g[p + "w_q"].T, l2a_wk=g[p + "w_k"].T, l2a_wv=g[p + "w_v"].T, l2a_wo=g[p + "w_o"].T)
    if "L0_attn" in LAYERS:
        p = "L0_attn_"
        turn = _np.r_[_np.arange(0, ROPE, 2), _np.arange(1, ROPE, 2)]
        wqb = g[p + "Wq_b"].reshape(Q_RANK, MLA_HEADS, NOPE + ROPE)
        wkv = g[p + "Wkv_b"].reshape(KV_RANK, MLA_HEADS, NOPE + VD)
        wkva = g[p + "Wkv_a"]
        cos, sin = _rope_tables(ROPE, T)
        q_scale = _np.zeros((P, 2), _np.float32)
        q_scale[:, 0] = g[p + "q_a_ln_w"][0:P]
        q_scale[0:64, 1] = g[p + "q_a_ln_w"][P:]
        h.update(l0a_wa=_np.concatenate([g[p + "Wq_a"], wkva[:, :KV_RANK], wkva[:, KV_RANK:][:, turn]], 1),
                 l0a_wkv=g[p + "kv_a_ln_w"], l0a_wqn=q_scale,
                 l0a_cos_t=cos.T.reshape(NT, P, HALF).transpose(1, 0, 2),
                 l0a_sin_t=sin.T.reshape(NT, P, HALF).transpose(1, 0, 2),
                 l0a_cosT=_np.concatenate([cos, cos]), l0a_sinT=_np.concatenate([-sin, sin]),
                 l0a_mask=_np.triu(_np.full((P, P), -1e30), 1).astype(_ml.bfloat16),
                 l0a_diag=_np.repeat(_np.eye(NT, dtype=_np.float32)[:, :, None], P, 2),
                 l0a_wqnT=wqb[:, :, :NOPE].transpose(1, 2, 0),
                 l0a_wqpe=wqb[:, :, NOPE:][:, :, turn].transpose(1, 0, 2),
                 l0a_wkT=wkv[:, :, :NOPE].transpose(1, 2, 0), l0a_wvT=wkv[:, :, NOPE:].transpose(1, 2, 0),
                 l0a_wo=g[p + "Wo"].reshape(MLA_HEADS, VD, D))
    nc = _bacc.Bacc("TRN2", target_bir_lowering=False, num_devices=1)
    arrays, args = {}, {}
    for name, v in h.items():
        v = _np.ascontiguousarray(v)
        arrays[f"in_{name}"] = v
        args[name] = nc.dram_tensor(f"in_{name}", v.shape, _mybir.dt.from_np(v.dtype), kind="ExternalInput").ap()
    out = nc.dram_tensor("out_0", (1, T, D), _mybir.dt.float32, kind="ExternalOutput").ap()
    program(nc, args, out)
    r = _run(nc, [arrays], core_ids=[0])
    return r.results[0]["out_0"]
```

```python
from contextlib import ExitStack

import numpy as np

import concourse.bass as bass
from concourse import mybir

P = 128
T = 1024
NT = T // P
D = 512
KC = D // P
LN_EPS = 1e-5

ALU = mybir.AluOpType
ACT = mybir.ActivationFunctionType
AX = mybir.AxisListType
F32 = mybir.dt.float32
BF16 = mybir.dt.bfloat16
U32 = mybir.dt.uint32
I32 = mybir.dt.int32

LAYERS = ("L0_attn", "L0_ffn", "L1_attn", "L1_ffn", "L2_attn", "L2_ffn", "L3_attn", "L3_ffn",)


class Chip:

    def __init__(self, nc, ctx, consts):
        self.nc, self.ctx = nc, ctx
        self.consts = consts
        self.x = self.sb("x", [P, NT, D])
        self.f = self.sb("f", [P, NT, D])
        self.yT = self.sb("yT", [P, KC, T])
        self.ident = self.sb("ident", [P, P])
        self.neghalf = self.sb("neghalf", [P, 16])
        self.stats = self.sb("stats", [P, 2, NT, 6])
        self.moments = self.sb("moments", [P, 2, NT, 2])
        self.prepared = self.sb("prepared", [P, 2, 2, NT])
        self.applied = self.sb("applied", [P, 2, 2, NT])
        self.normed = False
        self.out = None
        self.ps = ctx.enter_context(nc.psum_tensor("ps", [P, 8, 512], F32))
        self.count = {}
        self.sems = {}

    def sb(self, name, shape, dt=F32):
        return self.ctx.enter_context(self.nc.sbuf_tensor(name, shape, dt))

    def sem(self, name):
        if name not in self.sems:
            self.sems[name] = self.ctx.enter_context(self.nc.semaphore(name))
            self.count[name] = 0
        return self.sems[name]

    def base(self, name):
        self.sem(name)
        return self.count[name]

    def spent(self, **rises):
        for name, n in rises.items():
            self.sem(name)
            self.count[name] += n


def start(chip, x_dram):
    nc = chip.nc
    s_load = chip.sem("start_loaded")
    s_const = chip.sem("const_written")
    with nc.Block() as block:
        @block.sync
        def _(sp):
            xv = x_dram.rearrange("a (t p) d -> p (a t) d", p=P)
            for h in range(2):
                sp.dma_start(chip.x[:, 4 * h:4 * h + 4, :], xv[:, 4 * h:4 * h + 4, :]).then_inc(s_load, 16)
            sp.dma_start(chip.ident[:], chip.consts["ident"]).then_inc(s_load, 16)
            sp.wait_ge(s_load, 48)

        @block.vector
        def _(dve):
            nc.vector.memset(chip.neghalf[:], -0.5).then_inc(s_const, 1)


class Norms:

    GPSIMD_SUMS = (0, 1)

    def __init__(self, chip, residual, last, f_rows=None):
        self.chip, self.residual, self.last = chip, residual, last
        self.f_rows = f_rows
        self.passes = ([0] if residual else []) + ([] if last else [1])
        steps = [[(n, k - 2 * n * residual) for n in self.passes] for k in range(NT // 2 + 2)]
        self.steps = [[(n, p) for n, p in step if 0 <= p < NT // 2] for step in steps]
        self.order = [at for step in self.steps for at in step]
        self.base = {kind: chip.base("ln_" + kind)
                     for kind in ("stats", "prepared", "pow", "applied", "scaled", "added", "summed")}
        N = len(self.order)
        chip.spent(ln_stats=4 * N, ln_prepared=2 * N, ln_pow=N, ln_applied=N, ln_scaled=2 * N,
                   ln_added=len(self.GPSIMD_SUMS) * residual,
                   ln_summed=(NT // 2 - len(self.GPSIMD_SUMS)) * residual)

    def count(self, kind, at, each):
        return self.base[kind] + each * (self.order.index(at) + 1)

    def wait_sum(self, engine, p):
        kind, n = ("added", p) if p in self.GPSIMD_SUMS else ("summed", p - len(self.GPSIMD_SUMS))
        engine.wait_ge(self.chip.sem("ln_" + kind), self.base[kind] + n + 1)

    def vector(self, dve, k):
        chip, nc = self.chip, self.chip.nc
        s_stats, s_prepared, s_scaled, s_summed = (
            chip.sem("ln_" + n) for n in ("stats", "prepared", "scaled", "summed"))
        if self.residual and k >= 2 and k - 2 not in self.GPSIMD_SUMS:
            pair = slice(2 * (k - 2), 2 * (k - 2) + 2)
            dve.wait_ge(s_scaled, self.count("scaled", (0, k - 2), 2))
            nc.vector.tensor_tensor(chip.x[:, pair, :], chip.x[:, pair, :], chip.f[:, pair, :],
                                    ALU.add).then_inc(s_summed, 1)
        for n, p in self.steps[k]:
            src = chip.x if n else chip.f
            if n and self.residual:
                self.wait_sum(dve, p)
            if n == 0 and self.f_rows:
                dve.wait_ge(self.f_rows[0], self.f_rows[1] + 2 * p + 2)
            done = self.count("stats", (n, p), 4)
            for t in (2 * p, 2 * p + 1):
                nc.vector.bn_stats(chip.stats[:, n, t, :], src[:, t, :]).then_inc(s_stats, 1)
            for i, t in enumerate((2 * p, 2 * p + 1)):
                dve.wait_ge(s_stats, done - 3 + i)
                nc.vector.bn_aggr(chip.moments[:, n, t, :], chip.stats[:, n, t, :]).then_inc(s_stats, 1)
            dve.wait_ge(s_stats, done)
            pair = slice(2 * p, 2 * p + 2)
            nc.vector.tensor_scalar(chip.prepared[:, n, 0, pair], chip.moments[:, n, pair, 0], -1.0, None,
                                    ALU.mult).then_inc(s_prepared, 1)
            nc.vector.tensor_scalar(chip.prepared[:, n, 1, pair], chip.moments[:, n, pair, 1], LN_EPS, None,
                                    ALU.add).then_inc(s_prepared, 1)

    def gpsimd(self, pool):
        chip, nc = self.chip, self.chip.nc
        s_prepared, s_pow, s_applied, s_scaled, s_added = (
            chip.sem("ln_" + n) for n in ("prepared", "pow", "applied", "scaled", "added"))

        def add(p):
            pool.wait_ge(s_scaled, self.count("scaled", (0, p), 2))
            pair = slice(2 * p, 2 * p + 2)
            nc.gpsimd.tensor_tensor(chip.x[:, pair, :], chip.x[:, pair, :], chip.f[:, pair, :],
                                    ALU.add).then_inc(s_added, 1)

        for k, step in enumerate(self.steps):
            for n, p in step:
                pair = slice(2 * p, 2 * p + 2)
                pool.wait_ge(s_prepared, self.count("prepared", (n, p), 2))
                nc.gpsimd.tensor_tensor(chip.applied[:, n, 0, pair], chip.prepared[:, n, 1, pair],
                                        chip.neghalf[:, 0:2], ALU.pow).then_inc(s_pow, 1)
                pool.wait_ge(s_pow, self.count("pow", (n, p), 1))
                nc.gpsimd.tensor_tensor(chip.applied[:, n, 1, pair], chip.prepared[:, n, 0, pair],
                                        chip.applied[:, n, 0, pair], ALU.mult).then_inc(s_applied, 1)
                if n == 0 and p and p - 1 in self.GPSIMD_SUMS:
                    add(p - 1)

    def scalar(self, act):
        chip, nc = self.chip, self.chip.nc
        s_applied, s_scaled = chip.sem("ln_applied"), chip.sem("ln_scaled")
        for n, p in self.order:
            act.wait_ge(s_applied, self.count("applied", (n, p), 1))
            if n and self.residual:
                self.wait_sum(act, p)
            for t in (2 * p, 2 * p + 1):
                nc.scalar.activation(chip.f[:, t, :], (chip.x if n else chip.f)[:, t, :], ACT.Identity,
                                     bias=chip.applied[:, n, 1, t:t + 1],
                                     scale=chip.applied[:, n, 0, t:t + 1]).then_inc(s_scaled, 1)

    def sync(self, sp):
        if not self.last:
            return
        chip = self.chip
        s_out = chip.sem("x_stored")
        ov = chip.out.rearrange("a (t p) d -> p (a t) d", p=P)
        for p in range(NT // 2):
            self.wait_sum(sp, p)
            sp.dma_start(ov[:, 2 * p:2 * p + 2, :], chip.x[:, 2 * p:2 * p + 2, :]).then_inc(s_out, 16)
        sp.wait_ge(s_out, 16 * (NT // 2))


def stage_norms(chip):
    chip.normed = True
    f_rows = chip.sem("f_rows")
    norms = Norms(chip, True, chip.last, (f_rows, chip.base("f_rows")))
    chip.spent(f_rows=NT)
    return f_rows, norms


def renorm(chip, name, add_f, loads=None):
    nc, ps, f = chip.nc, chip.ps, chip.f
    norms = None if chip.normed else Norms(chip, bool(add_f), False)
    chip.normed = False
    s_turned, b_turned = chip.sem("ln_turned"), chip.base("ln_turned")
    with nc.Block() as block:
        @block.sync
        def _(sp):
            if loads:
                loads(sp)

        @block.tensor
        def _(pe):
            for t in range(NT):
                if norms and t % 2 == 0:
                    pe.wait_ge(chip.sem("ln_scaled"), norms.count("scaled", (1, t // 2), 2))
                for c in range(KC):
                    mm = nc.tensor.transpose(ps[:, t, c * P:(c + 1) * P], f[:, t, c * P:(c + 1) * P], chip.ident[:])
                mm.then_inc(s_turned, 1)

        @block.vector
        def _(dve):
            if norms:
                for k in range(len(norms.steps)):
                    norms.vector(dve, k)
            for t in range(1, NT, 2):
                dve.wait_ge(s_turned, b_turned + t + 1)
                nc.vector.tensor_copy(chip.yT[:, :, t * P:(t + 1) * P],
                                      ps[:, t, :].rearrange("p (c q) -> p c q", c=KC))

        if norms:
            @block.gpsimd
            def _(pool):
                norms.gpsimd(pool)

        @block.scalar
        def _(act):
            if norms:
                norms.scalar(act)
            for t in range(0, NT, 2):
                act.wait_ge(s_turned, b_turned + t + 1)
                nc.scalar.copy(chip.yT[:, :, t * P:(t + 1) * P],
                               ps[:, t, :].rearrange("p (c q) -> p c q", c=KC))
    chip.spent(ln_turned=NT)


def store(chip):
    norms = Norms(chip, True, True)
    with chip.nc.Block() as block:
        @block.vector
        def _(dve):
            for k in range(len(norms.steps)):
                norms.vector(dve, k)

        @block.gpsimd
        def _(pool):
            norms.gpsimd(pool)

        @block.scalar
        def _(act):
            norms.scalar(act)

        @block.sync
        def _(sp):
            norms.sync(sp)


def weights_view(w):
    return w.rearrange("(c p) m -> p c m", p=P)


def l0_ffn(chip, add_f, W, bias, A, B, starts, want):
    nc, ps, yT = chip.nc, chip.ps, chip.yT
    NA, R = 3, 16
    s_w = chip.sem("l0f_loaded")
    s_m, s_low, s_lowT, s_row = (chip.sem("l0f_" + n) for n in ("mask", "low", "lowT", "rows"))
    with ExitStack() as mem:
        w = mem.enter_context(nc.sbuf_tensor("l0f_w", [P, KC, D], F32))
        a = mem.enter_context(nc.sbuf_tensor("l0f_a", [P, KC, NA * R], F32))
        b = mem.enter_context(nc.sbuf_tensor("l0f_b", [NA * R, D], F32))
        bb = mem.enter_context(nc.sbuf_tensor("l0f_bias", [P, D], F32))
        st = mem.enter_context(nc.sbuf_tensor("l0f_starts", [NA * R, 4], I32))
        stf = mem.enter_context(nc.sbuf_tensor("l0f_startsf", [NA * R, 4], F32))
        wt = mem.enter_context(nc.sbuf_tensor("l0f_want", [NA * R, 1], F32))
        m = mem.enter_context(nc.sbuf_tensor("l0f_mask", [NA * R, 2], F32))
        lowT = mem.enter_context(nc.sbuf_tensor("l0f_lowT", [NA * R, T], F32))

        def loads(sp):
            sp.dma_start(a[:], weights_view(A)).then_inc(s_w, 16)
            sp.dma_start(b[:], B).then_inc(s_w, 16)
            sp.dma_start(st[:], starts.partition_broadcast(NA * R)).then_inc(s_w, 16)
            sp.dma_start(wt[:], want).then_inc(s_w, 16)
            sp.dma_start(w[:], weights_view(W)).then_inc(s_w, 16)
            sp.dma_start(bb[:], bias.partition_broadcast(P)).then_inc(s_w, 16)

        renorm(chip, "l0f", add_f, loads=loads)
        s_f, norms = stage_norms(chip)
        with nc.Block() as block:
            @block.vector
            def _(dve):
                dve.wait_ge(s_w, 96)
                nc.vector.tensor_copy(stf[:], st[:]).then_inc(s_m, 1)
                dve.wait_ge(s_m, 1)
                nc.vector.tensor_scalar(stf[:], stf[:], 0.0, None, ALU.is_le).then_inc(s_m, 1)
                dve.wait_ge(s_m, 2)
                nc.vector.reduce_sum(m[:, 0:1], stf[:], AX.X).then_inc(s_m, 1)
                dve.wait_ge(s_m, 3)
                nc.vector.tensor_tensor(m[:, 1:2], m[:, 0:1], wt[:], ALU.is_equal).then_inc(s_m, 1)
                dve.wait_ge(s_m, 4)
                for h in range(2):
                    dve.wait_ge(s_low, h + 1)
                    nc.vector.tensor_scalar(lowT[:, 512 * h:512 * h + 512], ps[0:NA * R, h, :], m[:, 1:2], None,
                                            ALU.mult).then_inc(s_lowT, 1)
                for t in range(NT):
                    dve.wait_ge(s_row, t + 1)
                    nc.vector.tensor_tensor(chip.f[:, t, :], ps[:, (2 + t) % 8, :], bb[:], ALU.add).then_inc(s_f, 1)
                    if t % 2:
                        norms.vector(dve, t // 2)
                for k in (4, 5):
                    norms.vector(dve, k)

            @block.scalar
            def _(act):
                norms.scalar(act)

            @block.gpsimd
            def _(pool):
                norms.gpsimd(pool)

            @block.sync
            def _(sp):
                norms.sync(sp)

            @block.tensor
            def _(pe):
                pe.wait_ge(s_w, 96)
                for h in range(2):
                    for c in range(KC):
                        mm = nc.tensor.matmul(ps[0:NA * R, h, :], a[:, c, :], yT[:, c, 512 * h:512 * h + 512],
                                              start=c == 0, stop=c == KC - 1)
                    mm.then_inc(s_low, 1)
                pe.wait_ge(s_lowT, 2)
                for t in range(NT):
                    out = ps[:, (2 + t) % 8, :]
                    for c in range(KC):
                        nc.tensor.matmul(out, yT[:, c, t * P:(t + 1) * P], w[:, c, :], start=c == 0, stop=False)
                    nc.tensor.matmul(out, lowT[:, t * P:(t + 1) * P], b[:], start=False, stop=True).then_inc(s_row, 1)


def l1_ffn(chip, add_f, W):
    nc, ps, yT = chip.nc, chip.ps, chip.yT
    s_w, s_b, s_t, s_wT, s_row = (chip.sem("l1f_" + n) for n in ("loaded", "binary", "turned", "wT", "rows"))
    with ExitStack() as mem:
        w = mem.enter_context(nc.sbuf_tensor("l1f_w", [P, KC, D], F32))
        pos = mem.enter_context(nc.sbuf_tensor("l1f_pos", [P, KC, D], F32))
        neg = mem.enter_context(nc.sbuf_tensor("l1f_neg", [P, KC, D], F32))
        wT = mem.enter_context(nc.sbuf_tensor("l1f_wT", [P, KC, D], F32))
        sc = mem.enter_context(nc.sbuf_tensor("l1f_scale", [P, KC], F32))

        def loads(sp):
            sp.dma_start(w[:], weights_view(W)).then_inc(s_w, 16)

        renorm(chip, "l1f", add_f, loads=loads)
        s_f, norms = stage_norms(chip)
        with nc.Block() as block:
            @block.vector
            def _(dve):
                dve.wait_ge(s_w, 16)
                n = 0
                nc.vector.tensor_reduce(sc[:], w[:], AX.X, ALU.add, apply_absolute_value=True).then_inc(s_b, 1)
                dve.wait_ge(s_b, 1)
                nc.vector.tensor_scalar(sc[:], sc[:], 1.0 / D, None, ALU.mult).then_inc(s_b, 1)
                dve.wait_ge(s_b, 2)
                for o in range(KC):
                    k = 2 + 6 * o
                    nc.vector.tensor_scalar(pos[:, o, :], w[:, o, :], 0.0, sc[:, o:o + 1], ALU.is_gt,
                                            ALU.mult).then_inc(s_b, 1)
                    nc.vector.tensor_scalar(neg[:, o, :], w[:, o, :], 0.0, sc[:, o:o + 1], ALU.is_lt,
                                            ALU.mult).then_inc(s_b, 1)
                    nc.vector.tensor_scalar(w[:, o, :], w[:, o, :], 1.0, -1.0, ALU.min, ALU.max).then_inc(s_b, 1)
                    dve.wait_ge(s_b, k + 3)
                    nc.vector.tensor_tensor(pos[:, o, :], pos[:, o, :], neg[:, o, :], ALU.subtract).then_inc(s_b, 1)
                    dve.wait_ge(s_b, k + 4)
                    nc.vector.tensor_tensor(pos[:, o, :], pos[:, o, :], w[:, o, :], ALU.subtract).then_inc(s_b, 1)
                    dve.wait_ge(s_b, k + 5)
                    nc.vector.tensor_tensor(pos[:, o, :], pos[:, o, :], w[:, o, :], ALU.add).then_inc(s_b, 1)
                for t in range(NT):
                    dve.wait_ge(s_row, t + 1)
                    nc.vector.tensor_copy(chip.f[:, t, :], ps[:, (4 + t) % 8, :]).then_inc(s_f, 1)
                    if t % 2:
                        norms.vector(dve, t // 2)
                for k in (4, 5):
                    norms.vector(dve, k)

            @block.scalar
            def _(act):
                for o in range(KC):
                    act.wait_ge(s_t, o + 1)
                    nc.scalar.copy(wT[:, :, o * P:(o + 1) * P],
                                   ps[:, o, :].rearrange("p (c q) -> p c q", c=KC)).then_inc(s_wT, 1)
                norms.scalar(act)

            @block.gpsimd
            def _(pool):
                norms.gpsimd(pool)

            @block.sync
            def _(sp):
                norms.sync(sp)

            @block.tensor
            def _(pe):
                for o in range(KC):
                    pe.wait_ge(s_b, 2 + 6 * (o + 1))
                    for c in range(KC):
                        mm = nc.tensor.transpose(ps[:, o, c * P:(c + 1) * P], pos[:, o, c * P:(c + 1) * P],
                                                 chip.ident[:])
                    mm.then_inc(s_t, 1)
                pe.wait_ge(s_wT, KC)
                for t in range(NT):
                    for c in range(KC):
                        mm = nc.tensor.matmul(ps[:, (4 + t) % 8, :], yT[:, c, t * P:(t + 1) * P], wT[:, c, :],
                                              start=c == 0, stop=c == KC - 1)
                    mm.then_inc(s_row, 1)


def l2_ffn(chip, add_f, G, U, DN, gs, us, ds):
    nc, ps, yT = chip.nc, chip.ps, chip.yT
    INTER = 1376
    FULL = INTER // P
    REST = INTER - FULL * P
    NM = FULL + 1
    s_w = [chip.sem(f"l2f_loaded{i}") for i in range(3)]
    s_d, s_s, s_g, s_silu, s_h, s_sc = (
        chip.sem("l2f_" + n) for n in ("down_loaded", "scales_loaded", "gate_up", "silu", "hidden", "rows"))
    cuts = [0, 2 * P, 6 * P, INTER]
    with ExitStack() as mem:
        g = mem.enter_context(nc.sbuf_tensor("l2f_g", [P, KC, INTER], F32))
        u = mem.enter_context(nc.sbuf_tensor("l2f_u", [P, KC, INTER], F32))
        dn = mem.enter_context(nc.sbuf_tensor("l2f_dn", [P, NM, D], F32))
        hT = mem.enter_context(nc.sbuf_tensor("l2f_hT", [P, NM, T], F32))
        silu = mem.enter_context(nc.sbuf_tensor("l2f_silu", [P, 2, 512], F32))
        sc = mem.enter_context(nc.sbuf_tensor("l2f_sc", [P, 3], F32))

        def loads(sp):
            for i, s in enumerate((gs, us, ds)):
                sp.dma_start(sc[:, i:i + 1], s.partition_broadcast(P)).then_inc(s_s, 16)
            for i in range(3):
                sp.dma_start(g[:, :, cuts[i]:cuts[i + 1]], weights_view(G)[:, :, cuts[i]:cuts[i + 1]]).then_inc(s_w[i], 16)
                sp.dma_start(u[:, :, cuts[i]:cuts[i + 1]], weights_view(U)[:, :, cuts[i]:cuts[i + 1]]).then_inc(s_w[i], 16)
            sp.dma_start(dn[:, 0:FULL, :], DN[0:FULL * P, :].rearrange("(c p) m -> p c m", p=P)).then_inc(s_d, 16)
            sp.dma_start(dn[0:REST, FULL, :], DN[FULL * P:, :]).then_inc(s_d, 16)

        renorm(chip, "l2f", add_f, loads=loads)
        s_f, norms = stage_norms(chip)
        b_f = chip.base("f_rows") - NT
        jobs = [(m, h) for m in range(NM) for h in range(2)]
        with nc.Block() as block:
            @block.tensor
            def _(pe):
                for n, (m, h) in enumerate(jobs):
                    M = P if m < FULL else REST
                    for i in range(3):
                        if h == 0 and m * P == cuts[i]:
                            pe.wait_ge(s_w[i], 32)
                    if n >= 3:
                        pe.wait_ge(s_h, n - 2)
                    for k, wt in enumerate((g, u)):
                        for c in range(KC):
                            mm = nc.tensor.matmul(ps[0:M, 2 * (n % 3) + k, :], wt[:, c, m * P:m * P + M],
                                                  yT[:, c, 512 * h:512 * h + 512], start=c == 0, stop=c == KC - 1)
                    mm.then_inc(s_g, 1)
                pe.wait_ge(s_d, 32)
                pe.wait_ge(s_h, len(jobs))
                for t in range(NT):
                    if t >= 2:
                        pe.wait_ge(s_f, b_f + t - 1)
                    for m in range(NM):
                        M = P if m < FULL else REST
                        mm = nc.tensor.matmul(ps[:, 6 + t % 2, :], hT[0:M, m, t * P:(t + 1) * P], dn[0:M, m, :],
                                              start=m == 0, stop=m == NM - 1)
                    mm.then_inc(s_sc, 1)

            @block.scalar
            def _(act):
                act.wait_ge(s_s, 48)
                for n, (m, h) in enumerate(jobs):
                    M = P if m < FULL else REST
                    act.wait_ge(s_g, n + 1)
                    if n >= 2:
                        act.wait_ge(s_h, n - 1)
                    nc.scalar.activation(silu[0:M, n % 2, :], ps[0:M, 2 * (n % 3), :], ACT.Silu,
                                         scale=sc[0:M, 0:1]).then_inc(s_silu, 1)
                norms.scalar(act)

            @block.vector
            def _(dve):
                dve.wait_ge(s_s, 48)
                for n, (m, h) in enumerate(jobs):
                    M = P if m < FULL else REST
                    dve.wait_ge(s_silu, n + 1)
                    nc.vector.scalar_tensor_tensor(out=hT[0:M, m, 512 * h:512 * h + 512],
                                                   in0=ps[0:M, 2 * (n % 3) + 1, :], scalar=sc[0:M, 1:2],
                                                   in1=silu[0:M, n % 2, :], op0=ALU.mult,
                                                   op1=ALU.mult).then_inc(s_h, 1)
                for t in range(NT):
                    dve.wait_ge(s_sc, t + 1)
                    nc.vector.tensor_scalar(chip.f[:, t, :], ps[:, 6 + t % 2, :], sc[:, 2:3], None,
                                            ALU.mult).then_inc(s_f, 1)
                    if t % 2:
                        norms.vector(dve, t // 2)
                for k in (4, 5):
                    norms.vector(dve, k)

            @block.gpsimd
            def _(pool):
                norms.gpsimd(pool)

            @block.sync
            def _(sp):
                norms.sync(sp)


def l3_attn(chip, add_f, WD, bd, WU, bu, gate, IN, conv_w, conv_b, Dh, FCD, norm_w, OUT):
    nc, ps, yT = chip.nc, chip.ps, chip.yT
    DIN, NH = 2 * P, 4
    s_w, s_pr, s_e, s_xm = (chip.sem("l3a_" + n) for n in ("loaded", "prepared", "gate_exp", "mid"))
    s_pe, s_act, s_dve, s_pool = (chip.sem("l3a_" + n) for n in ("pe_done", "act_done", "dve_done", "pool_done"))
    with ExitStack() as mem:
        def sb(name, shape, dt=F32):
            return mem.enter_context(nc.sbuf_tensor("l3a_" + name, shape, dt))
        wd = sb("wd", [P, KC, P])
        wu = sb("wu", [P, D])
        bub = sb("bu", [P, D])
        win = sb("in", [P, 2 * DIN])
        wout = sb("out", [P, 2, P])
        fc = sb("fc", [P, 2, NH])
        fcr = sb("fcr", [P, 2, NH, 64])
        col = sb("col", [P, 16])
        mid = sb("mid", [P, T])
        u = sb("u", [P, T])
        z = sb("z", [P, 2, T])
        xs = sb("xs", [P, 2, T])
        yz = sb("yz", [P, 2, T])
        sq = sb("sq", [P, 2, T])
        ones = sb("ones", [P, 2])
        ms = sb("ms", [P, NT])
        rs = sb("rs", [P, NT])
        urow = sb("urow", [P, NT, P])
        al = sb("al", [P, 4])
        BD, CW, CB, DD, NW, GT = 0, 1, 3, 5, 7, 9
        NL = 14 + NH

        def loads(sp):
            def ld(dst, src):
                sp.dma_start(dst, src).then_inc(s_w, 16)
            ld(wd[:], weights_view(WD))
            ld(win[:], IN[:, 0:2 * DIN])
            ld(fc[:], FCD.rearrange("(c p) h -> p c h", p=P))
            ld(wout[:], weights_view(OUT))
            ld(wu[:], WU)
            ld(bub[:], bu.partition_broadcast(P))
            ld(col[:, BD:BD + 1], bd.rearrange("(p a) -> p a", a=1))
            for c in range(2):
                ld(col[:, CW + c:CW + c + 1], conv_w[c * P:(c + 1) * P])
                ld(col[:, CB + c:CB + c + 1], conv_b[c * P:(c + 1) * P])
                ld(col[:, NW + c:NW + c + 1], norm_w[c * P:(c + 1) * P])
            ld(col[:, GT:GT + 1], gate.partition_broadcast(P))
            for h in range(NH):
                ld(col[64 * (h % 2):64 * (h % 2) + 64, DD + h // 2:DD + h // 2 + 1],
                   Dh[h:h + 1].partition_broadcast(64))

        renorm(chip, "l3a", add_f, loads=loads)
        with nc.Block() as block:
            @block.vector
            def _(dve):
                dve.wait_ge(s_w, 16 * NL)
                n = [0]

                def step(ins):
                    n[0] += 1
                    ins.then_inc(s_pr, 1)
                step(nc.vector.memset(ones[:], 1.0))
                step(nc.vector.tensor_copy(fcr[:], fc[:].unsqueeze(3).broadcast_to([P, 2, NH, 64])))
                for c in range(2):
                    step(nc.vector.tensor_scalar(wout[:, c, :], wout[:, c, :], col[:, NW + c:NW + c + 1], None, ALU.mult))
                dve.wait_ge(s_e, 1)
                step(nc.vector.tensor_scalar(al[:, 1:2], al[:, 0:1], 1.0, None, ALU.add))
                dve.wait_ge(s_pr, 5)
                step(nc.vector.reciprocal(al[:, 2:3], al[:, 1:2]))
                dve.wait_ge(s_pr, 6)
                step(nc.vector.tensor_scalar(al[:, 3:4], al[:, 2:3], -1.0, 1.0, ALU.mult, ALU.add))
                step(nc.vector.tensor_scalar(al[:, 1:2], al[:, 2:3], 1.0, None, ALU.add))
                dve.wait_ge(s_pr, 8)

            @block.scalar
            def _(act):
                act.wait_ge(s_w, 16 * NL)
                nc.scalar.activation(al[:, 0:1], col[:, GT:GT + 1], ACT.Exp, scale=-1.0).then_inc(s_e, 1)
                for h in range(2):
                    act.wait_ge(s_pe, h + 1)
                    nc.scalar.activation(mid[:, 512 * h:512 * h + 512], ps[:, h, :], ACT.Gelu,
                                         bias=col[:, BD:BD + 1])

            @block.tensor
            def _(pe):
                pe.wait_ge(s_w, 16 * NL)
                for h in range(2):
                    for c in range(KC):
                        mm = nc.tensor.matmul(ps[:, h, :], wd[:, c, :], yT[:, c, 512 * h:512 * h + 512],
                                              start=c == 0, stop=c == KC - 1)
                    mm.then_inc(s_pe, 1)
        chip.spent(l3a_pe_done=2)
        for r in range(2):
            src = mid if r == 0 else u
            bp, ba, bv, bo = (chip.base("l3a_" + n) for n in ("pe_done", "act_done", "dve_done", "pool_done"))
            with nc.Block() as block:
                @block.tensor
                def _(pe):
                    for m in range(4):
                        for h in range(2):
                            nc.tensor.matmul(ps[:, 2 * m + h, :], win[:, m * P:(m + 1) * P],
                                             src[:, 512 * h:512 * h + 512], start=True, stop=True).then_inc(s_pe, 1)
                    pe.wait_ge(s_act, ba + 8)
                    for m in range(2):
                        for h in range(2):
                            for c in range(2):
                                mm = nc.tensor.matmul(ps[:, 2 * m + h, :],
                                                      fcr[:, c, 2 * m:2 * m + 2, :].rearrange("p a b -> p (a b)"),
                                                      xs[:, c, 512 * h:512 * h + 512], start=c == 0, stop=c == 1)
                            mm.then_inc(s_pe, 1)
                    pe.wait_ge(s_act, ba + 12)
                    for t in range(NT):
                        for c in range(2):
                            mm = nc.tensor.matmul(ps[:, 4, t:t + 1], sq[:, c, t * P:(t + 1) * P], ones[:, 0:1],
                                                  start=c == 0, stop=c == 1)
                    mm.then_inc(s_pe, 1)
                    for t in range(NT):
                        for c in range(2):
                            mm = nc.tensor.matmul(ps[:, 5 + t // 4, (t % 4) * P:(t % 4 + 1) * P],
                                                  yz[:, c, t * P:(t + 1) * P], wout[:, c, :],
                                                  start=c == 0, stop=c == 1)
                    mm.then_inc(s_pe, 1)
                    for t in range(NT):
                        pe.wait_ge(s_act, ba + 13 + t)
                        mm = nc.tensor.transpose(ps[:, t // 4, (t % 4) * P:(t % 4 + 1) * P], urow[:, t, :],
                                                 chip.ident[:])
                    mm.then_inc(s_pe, 1)

                @block.scalar
                def _(act):
                    for m in range(4):
                        for h in range(2):
                            act.wait_ge(s_pe, bp + 2 * m + h + 1)
                            if m < 2:
                                nc.scalar.activation(z[:, m, 512 * h:512 * h + 512], ps[:, 2 * m + h, :],
                                                     ACT.Silu).then_inc(s_act, 1)
                            else:
                                nc.scalar.activation(xs[:, m - 2, 512 * h:512 * h + 512], ps[:, 2 * m + h, :],
                                                     ACT.Silu, bias=col[:, CB + m - 2:CB + m - 1],
                                                     scale=col[:, CW + m - 2:CW + m - 1]).then_inc(s_act, 1)
                    for m in range(2):
                        for h in range(2):
                            act.wait_ge(s_dve, bv + 2 * (2 * m + h) + 2)
                            nc.scalar.activation(sq[:, m, 512 * h:512 * h + 512], yz[:, m, 512 * h:512 * h + 512],
                                                 ACT.Square).then_inc(s_act, 1)
                    act.wait_ge(s_pool, bo + 1)
                    act.wait_ge(s_pe, bp + 14)
                    for t in range(NT):
                        nc.scalar.activation(urow[:, t, :], ps[:, 5 + t // 4, (t % 4) * P:(t % 4 + 1) * P], ACT.Copy,
                                             scale=rs[:, t:t + 1]).then_inc(s_act, 1)

                @block.vector
                def _(dve):
                    k = 0
                    for m in range(2):
                        for h in range(2):
                            cut = slice(512 * h, 512 * h + 512)
                            dve.wait_ge(s_pe, bp + 8 + k + 1)
                            nc.vector.scalar_tensor_tensor(out=yz[:, m, cut], in0=ps[:, 2 * m + h, :],
                                                           scalar=col[:, DD + m:DD + m + 1], in1=xs[:, m, cut],
                                                           op0=ALU.add, op1=ALU.mult).then_inc(s_dve, 1)
                            dve.wait_ge(s_dve, bv + 2 * k + 1)
                            nc.vector.tensor_tensor(yz[:, m, cut], yz[:, m, cut], z[:, m, cut],
                                                    ALU.mult).then_inc(s_dve, 1)
                            k += 1
                    dve.wait_ge(s_pe, bp + 13)
                    nc.vector.tensor_scalar(ms[:], ps[:, 4, 0:NT], 1.0 / DIN, 1e-5, ALU.mult,
                                            ALU.add).then_inc(s_dve, 1)
                    dve.wait_ge(s_pe, bp + 15)
                    for h in range(2):
                        cut = slice(512 * h, 512 * h + 512)
                        if r == 0:
                            nc.vector.tensor_copy(u[:, cut], ps[:, h, :])
                        else:
                            nc.vector.tensor_scalar(mid[:, cut], mid[:, cut], al[:, 1:2], None,
                                                    ALU.mult).then_inc(s_dve, 1)
                            dve.wait_ge(s_dve, bv + 10 + h)
                            nc.vector.scalar_tensor_tensor(out=u[:, cut], in0=ps[:, h, :], scalar=al[:, 3:4],
                                                           in1=mid[:, cut], op0=ALU.mult, op1=ALU.add)

                @block.gpsimd
                def _(pool):
                    pool.wait_ge(s_dve, bv + 9)
                    nc.gpsimd.tensor_tensor(rs[:], ms[:], chip.neghalf[:, 0:NT], ALU.pow).then_inc(s_pool, 1)
            chip.spent(l3a_pe_done=15, l3a_act_done=20, l3a_dve_done=9 + 2 * r, l3a_pool_done=1)
        bp, bv = chip.base("l3a_pe_done"), chip.base("l3a_dve_done")
        s_f, norms = stage_norms(chip)
        with nc.Block() as block:
            @block.tensor
            def _(pe):
                for t in range(NT):
                    nc.tensor.matmul(ps[:, t, :], u[:, t * P:(t + 1) * P], wu[:], start=True, stop=True).then_inc(s_pe, 1)

            @block.vector
            def _(dve):
                for t in range(NT):
                    dve.wait_ge(s_pe, bp + t + 1)
                    nc.vector.tensor_tensor(chip.f[:, t, :], chip.f[:, t, :], ps[:, t, :], ALU.add).then_inc(s_dve, 1)
                    dve.wait_ge(s_dve, bv + t + 1)
                    nc.vector.tensor_tensor(chip.f[:, t, :], chip.f[:, t, :], bub[:], ALU.add).then_inc(s_f, 1)
                    if t % 2:
                        norms.vector(dve, t // 2)
                for k in (4, 5):
                    norms.vector(dve, k)

            @block.scalar
            def _(act):
                norms.scalar(act)

            @block.gpsimd
            def _(pool):
                norms.gpsimd(pool)

            @block.sync
            def _(sp):
                norms.sync(sp)


def l3_ffn(chip, add_f, GT, W, bias, A, B, iota):
    nc, ps, yT = chip.nc, chip.ps, chip.yT
    E, R = 8, 16
    s_w, s_low, s_r, s_e, s_lw, s_t, s_lT = (
        chip.sem("l3f_" + n) for n in ("loaded", "low", "route", "exp", "weighted", "turned", "lowT"))
    with ExitStack() as mem:
        def sb(name, shape, dt=F32):
            return mem.enter_context(nc.sbuf_tensor("l3f_" + name, shape, dt))
        w = sb("w", [P, KC, D])
        ag = sb("ag", [P, KC, E * R + E])
        b = sb("b", [P, D])
        bb = sb("bb", [P, D])
        io = sb("io", [P, E])
        lg = sb("lg", [P, NT, E])
        top = sb("top", [P, NT, E])
        idx = sb("idx", [P, NT, E], U32)
        idf = sb("idf", [P, NT, E])
        dd = sb("dd", [P, NT, 4])
        m1 = sb("m1", [P, NT, E])
        m2 = sb("m2", [P, NT, E])
        low = sb("low", [P, NT, E * R])
        lowT = sb("lowT", [P, T])

        def loads(sp):
            def ld(dst, src):
                sp.dma_start(dst, src).then_inc(s_w, 16)
            ld(ag[:, :, 0:E * R], weights_view(A))
            ld(ag[:, :, E * R:], weights_view(GT))
            ld(io[:], iota.partition_broadcast(P))
            ld(b[:], B)
            ld(bb[:], bias.partition_broadcast(P))
            ld(w[:], weights_view(W))

        renorm(chip, "l3f", add_f, loads=loads)
        s_f, norms = stage_norms(chip)
        N = E * R + E
        with nc.Block() as block:
            @block.tensor
            def _(pe):
                pe.wait_ge(s_w, 96)
                for t in range(NT):
                    for c in range(KC):
                        mm = nc.tensor.matmul(ps[:, t // 2, (t % 2) * 256:(t % 2) * 256 + N],
                                              yT[:, c, t * P:(t + 1) * P], ag[:, c, :], start=c == 0, stop=c == KC - 1)
                mm.then_inc(s_low, 1)
                for t in range(NT):
                    pe.wait_ge(s_lw, t + 1)
                    mm = nc.tensor.transpose(ps[:, 4 + t // 4, (t % 4) * P:(t % 4 + 1) * P], low[:, t, :],
                                             chip.ident[:])
                    if t % 4 == 3:
                        mm.then_inc(s_t, 1)
                for t in range(NT):
                    if t == 0:
                        pe.wait_ge(s_lT, 2)
                    bank = (6, 7, 0, 1, 2, 3, 4, 5)[t]
                    for c in range(KC):
                        nc.tensor.matmul(ps[:, bank, :], yT[:, c, t * P:(t + 1) * P], w[:, c, :], start=c == 0, stop=False)
                    nc.tensor.matmul(ps[:, bank, :], lowT[:, t * P:(t + 1) * P], b[:], start=False,
                                     stop=True).then_inc(s_t, 1)

            @block.vector
            def _(dve):
                dve.wait_ge(s_w, 96)
                dve.wait_ge(s_low, 1)
                nc.vector.tensor_copy(lg[:], ps[:, 0:4, :].rearrange("p b (a n) -> p (b a) n", a=2)[:, :, E * R:N]
                                      ).then_inc(s_r, 1)
                dve.wait_ge(s_r, 1)
                for t in range(NT):
                    nc.vector.max(top[:, t, :], lg[:, t, :]).then_inc(s_r, 1)
                for t in range(NT):
                    dve.wait_ge(s_r, 2 + t)
                    nc.vector.max_index(idx[:, t, :], top[:, t, :], lg[:, t, :]).then_inc(s_r, 1)
                nc.vector.tensor_tensor(dd[:, :, 0], top[:, :, 1], top[:, :, 0], ALU.subtract).then_inc(s_r, 1)
                dve.wait_ge(s_r, 17)
                nc.vector.tensor_copy(idf[:], idx[:]).then_inc(s_r, 1)
                dve.wait_ge(s_r, 19)
                iob = io[:].unsqueeze(1).broadcast_to([P, NT, E])
                nc.vector.tensor_tensor(m1[:], iob, idf[:, :, 0:1].broadcast_to([P, NT, E]), ALU.is_equal).then_inc(s_r, 1)
                nc.vector.tensor_tensor(m2[:], iob, idf[:, :, 1:2].broadcast_to([P, NT, E]), ALU.is_equal).then_inc(s_r, 1)
                dve.wait_ge(s_e, 1)
                nc.vector.tensor_scalar(dd[:, :, 2], dd[:, :, 1], 1.0, 0.5, ALU.add, ALU.mult).then_inc(s_r, 1)
                dve.wait_ge(s_r, 22)
                nc.vector.reciprocal(dd[:, :, 3], dd[:, :, 2]).then_inc(s_r, 1)
                nc.vector.tensor_tensor(m2[:], m2[:], dd[:, :, 1:2].broadcast_to([P, NT, E]), ALU.mult).then_inc(s_r, 1)
                dve.wait_ge(s_r, 24)
                nc.vector.tensor_tensor(m1[:], m1[:], m2[:], ALU.add).then_inc(s_r, 1)
                dve.wait_ge(s_r, 25)
                nc.vector.tensor_tensor(m1[:], m1[:], dd[:, :, 3:4].broadcast_to([P, NT, E]), ALU.mult).then_inc(s_r, 1)
                dve.wait_ge(s_r, 26)
                for t in range(NT):
                    nc.vector.tensor_tensor(
                        low[:, t, :].rearrange("p (e r) -> p e r", e=E),
                        ps[:, t // 2, (t % 2) * 256:(t % 2) * 256 + E * R].rearrange("p (e r) -> p e r", e=E),
                        m1[:, t, :].unsqueeze(2).broadcast_to([P, E, R]), ALU.mult).then_inc(s_lw, 1)
                for h in range(2):
                    dve.wait_ge(s_t, h + 1)
                    nc.vector.tensor_copy(lowT[:, 512 * h:512 * h + 512], ps[:, 4 + h, :]).then_inc(s_lT, 1)
                for t in range(NT):
                    dve.wait_ge(s_t, 2 + t + 1)
                    nc.vector.tensor_tensor(chip.f[:, t, :], ps[:, (6, 7, 0, 1, 2, 3, 4, 5)[t], :], bb[:],
                                            ALU.add).then_inc(s_f, 1)
                    if t % 2:
                        norms.vector(dve, t // 2)
                for k in (4, 5):
                    norms.vector(dve, k)

            @block.scalar
            def _(act):
                act.wait_ge(s_r, 18)
                nc.scalar.activation(dd[:, :, 1], dd[:, :, 0], ACT.Exp).then_inc(s_e, 1)
                norms.scalar(act)

            @block.gpsimd
            def _(pool):
                norms.gpsimd(pool)

            @block.sync
            def _(sp):
                norms.sync(sp)


HD = 16
HEADS = 32
GROUP = 4
GROUPS = HEADS // GROUP
Q_RUNS = [(0, 3), (1, 2), (2, 1)]
K_RUNS = [(0, 3), (0, 2), (0, 1)]
ROWS = 6 * HD
MAX_ROW = ROWS
EXT = MAX_ROW + 1


def rows_out(chip, name, W):
    nc, ps, f, yT = chip.nc, chip.ps, chip.f, chip.yT
    s_w, s_t, s_c, s_row = (chip.sem(name + n) for n in ("_out_loaded", "_out_turned", "_out_copied", "_out_rows"))
    s_f, norms = stage_norms(chip)
    with ExitStack() as mem:
        w = mem.enter_context(nc.sbuf_tensor(name + "_wo", [P, KC, D], F32))
        with nc.Block() as block:
            @block.sync
            def _(sp):
                sp.dma_start(w[:], weights_view(W)).then_inc(s_w, 16)
                norms.sync(sp)

            @block.tensor
            def _(pe):
                for t in range(NT):
                    for c in range(KC):
                        mm = nc.tensor.transpose(ps[:, t, c * P:(c + 1) * P], f[:, t, c * P:(c + 1) * P], chip.ident[:])
                    mm.then_inc(s_t, 1)
                pe.wait_ge(s_w, 16)
                for t in range(NT):
                    pe.wait_ge(s_c, t + 1)
                    for c in range(KC):
                        mm = nc.tensor.matmul(ps[:, t, :], yT[:, c, t * P:(t + 1) * P], w[:, c, :],
                                              start=c == 0, stop=c == KC - 1)
                    mm.then_inc(s_row, 1)

            @block.scalar
            def _(act):
                for t in range(NT):
                    act.wait_ge(s_t, t + 1)
                    nc.scalar.copy(yT[:, :, t * P:(t + 1) * P],
                                   ps[:, t, :].rearrange("p (c q) -> p c q", c=KC)).then_inc(s_c, 1)
                norms.scalar(act)

            @block.gpsimd
            def _(pool):
                norms.gpsimd(pool)

            @block.vector
            def _(dve):
                for t in range(NT):
                    dve.wait_ge(s_row, t + 1)
                    nc.vector.tensor_copy(f[:, t, :], ps[:, t, :]).then_inc(s_f, 1)
                    if t % 2:
                        norms.vector(dve, t // 2)
                for k in (4, 5):
                    norms.vector(dve, k)


def split_qkv(chip, name, mem, a, kv_heads, rope, add_f, q_parts, k_parts, vext):
    nc, ps, yT = chip.nc, chip.ps, chip.yT
    NV = kv_heads * HD

    def sb(n, shape, dt=F32):
        return mem.enter_context(nc.sbuf_tensor(f"{name}_{n}", shape, dt))
    wq, wk, wv = sb("wq", [P, KC, D]), sb("wk", [P, KC, NV]), sb("wv", [P, KC, NV])
    if rope:
        cos, sin = sb("cos", [P, T]), sb("sin", [P, T])
        bq, bk, bv = sb("bq", [P, 4]), sb("bk", [P, 2]), sb("bv", [P, NV])
        ab, tmp = sb("ab", [P, 2, 2, T]), sb("tmp", [P, 2, 2, T])
    res = sb("res", [P, 2, T])
    part = sb("part", [P, 2, 3, T], BF16)
    rest = sb("rest", [P, 2, T])
    s_w, s_mm, s_bias, s_rot, s_res, s_part, s_v, s_one = (
        chip.sem(f"{name}_{n}") for n in ("loaded", "qk", "biased", "rotated", "result", "high_mid", "v", "v_rows"))
    s_store = [chip.sem(f"{name}_stored{i}") for i in range(2)]
    s_pt, s_lo = chip.sem(f"{name}_pool_rotated"), chip.sem(f"{name}_rest_low")

    def by_heads(parts):
        return parts.rearrange("s e h t -> s h e t")

    units = []
    if rope:
        for g in range(2):
            units.append((wq, bq, [(2 * h + g) * P for h in range(2)], [2 * h + g for h in range(2)], P,
                          [by_heads(q_parts[:, 8 * h:8 * h + 8, 16 * g:16 * g + 16, :]) for h in range(2)]))
        units.append((wk, bk, [0, 64], [0, 1], 64, [by_heads(k_parts[:, 8 * h:8 * h + 8, :, :]) for h in range(2)]))
    else:
        for w, dst in ((wq, q_parts), (wk, k_parts)):
            for m in range(4):
                units.append((w, None, [m * P], [0], P, [by_heads(dst[:, :, 8 * m:8 * m + 8, :])]))
    NL = 3 + (5 if rope else 0)
    tiles = [(u, i) for u, unit in enumerate(units) for i in range(len(unit[2]))]
    per = 2 if rope else 1

    def loads(sp):
        def ld(dst, src):
            sp.dma_start(dst, src).then_inc(s_w, 16)
        ld(wq[:], weights_view(a[name + "_wq"]))
        ld(wk[:], weights_view(a[name + "_wk"]))
        ld(wv[:], weights_view(a[name + "_wv"]))
        if rope:
            ld(cos[:], a[name + "_cos"])
            ld(sin[:], a[name + "_sin"])
            ld(bq[:], a[name + "_bq"])
            ld(bk[0:64, :], a[name + "_bk"])
            ld(bv[:], a[name + "_bv"].partition_broadcast(P))

    renorm(chip, name, add_f, loads=loads)

    def tile_of(n):
        M = units[tiles[n][0]][4]
        return res[0:M, n % 2, :] if rope else ps[0:M, 2 * (n % 2):2 * (n % 2) + 2, :].rearrange("p b n -> p (b n)")

    with nc.Block() as block:
        @block.tensor
        def _(pe):
            pe.wait_ge(s_w, 16 * NL)
            for u, (w, _, cols, _, M, _) in enumerate(units):
                for i, col in enumerate(cols):
                    bank = (4 * (u % 2) + 2 * i) if rope else 2 * (u % 2)
                    if u >= 2:
                        pe.wait_ge(s_bias if rope else s_lo, 2 * (u - 1) if rope else 2 * u - 3)
                    for h in range(2):
                        for c in range(KC):
                            mm = nc.tensor.matmul(ps[0:M, bank + h, :], w[:, c, col:col + M],
                                                  yT[:, c, 512 * h:512 * h + 512], start=c == 0, stop=c == KC - 1)
                    mm.then_inc(s_mm, 1)
            if rope:
                pe.wait_ge(s_bias, 2 * len(units))
            for t in range(NT):
                if t >= 4:
                    pe.wait_ge(s_v, t - 3)
                for c in range(KC):
                    mm = nc.tensor.matmul(ps[:, 4 + t % 4, 0:NV], yT[:, c, t * P:(t + 1) * P], wv[:, c, :],
                                          start=c == 0, stop=c == KC - 1)
                mm.then_inc(s_one, 1)

        @block.scalar
        def _(act):
            n = 0
            for u, (_, b, cols, bc, M, _) in enumerate(units):
                if rope:
                    for i in range(2):
                        act.wait_ge(s_mm, 2 * u + i + 1)
                        if u >= 2:
                            act.wait_ge(s_res, u - 1)
                            act.wait_ge(s_pt, 3 * (u - 1))
                        bank = 4 * (u % 2) + 2 * i
                        nc.scalar.activation(ab[0:M, u % 2, i, :],
                                             ps[0:M, bank:bank + 2, :].rearrange("p b n -> p (b n)"),
                                             ACT.Identity, bias=b[0:M, bc[i]:bc[i] + 1]).then_inc(s_bias, 1)
                for i in range(len(cols)):
                    if rope and i == 0:
                        act.wait_ge(s_res, u + 1)
                    elif rope:
                        act.wait_ge(s_pt, 3 * u + 3)
                    else:
                        act.wait_ge(s_mm, n + 1)
                    if n >= 2:
                        act.wait_ge(s_store[n % 2], 48 * (n // 2))
                    nc.scalar.copy(part[0:M, n % 2, 0, :], tile_of(n)).then_inc(s_part, 1)
                    act.wait_ge(s_lo, 2 * n + 1)
                    nc.scalar.copy(part[0:M, n % 2, 1, :], rest[0:M, n % 2, :]).then_inc(s_part, 1)
                    n += 1

        @block.gpsimd
        def _(pool):
            nc.gpsimd.memset(vext[:, :, :, HD:2 * HD], 1.0)
            if rope:
                for u, (_, _, _, _, M, _) in enumerate(units):
                    pool.wait_ge(s_bias, 2 * u + 2)
                    nc.gpsimd.tensor_tensor(tmp[0:M, 1, 0, :], ab[0:M, u % 2, 0, :], sin[0:M, :], ALU.mult).then_inc(s_pt, 1)
                    nc.gpsimd.tensor_tensor(tmp[0:M, 1, 1, :], ab[0:M, u % 2, 1, :], cos[0:M, :], ALU.mult).then_inc(s_pt, 1)
                    pool.wait_ge(s_pt, 3 * u + 2)
                    if u >= 1:
                        pool.wait_ge(s_lo, 4 * u - 1)
                    nc.gpsimd.tensor_tensor(res[0:M, 1, :], tmp[0:M, 1, 0, :], tmp[0:M, 1, 1, :], ALU.add).then_inc(s_pt, 1)

        @block.vector
        def _(dve):
            n = 0
            for u, (_, _, cols, _, M, _) in enumerate(units):
                if rope:
                    dve.wait_ge(s_bias, 2 * u + 2)
                    nc.vector.tensor_tensor(tmp[0:M, 0, 0, :], ab[0:M, u % 2, 0, :], cos[0:M, :], ALU.mult).then_inc(s_rot, 1)
                    nc.vector.tensor_tensor(tmp[0:M, 0, 1, :], ab[0:M, u % 2, 1, :], sin[0:M, :], ALU.mult).then_inc(s_rot, 1)
                    dve.wait_ge(s_rot, 2 * u + 2)
                    nc.vector.tensor_tensor(res[0:M, 0, :], tmp[0:M, 0, 0, :], tmp[0:M, 0, 1, :], ALU.subtract).then_inc(s_res, 1)
                for i in range(len(cols)):
                    if rope and i == 1:
                        dve.wait_ge(s_pt, 3 * u + 3)
                    dve.wait_ge(s_part, 2 * n + 1)
                    nc.vector.tensor_tensor(rest[0:M, n % 2, :], tile_of(n), part[0:M, n % 2, 0, :],
                                            ALU.subtract).then_inc(s_lo, 1)
                    dve.wait_ge(s_part, 2 * n + 2)
                    nc.vector.tensor_tensor(part[0:M, n % 2, 2, :], rest[0:M, n % 2, :], part[0:M, n % 2, 1, :],
                                            ALU.subtract).then_inc(s_lo, 1)
                    n += 1
            for t in range(NT):
                dve.wait_ge(s_one, t + 1)
                src = ps[:, 4 + t % 4, 0:NV].rearrange("p (h e) -> p h e", e=HD)
                if rope:
                    nc.vector.tensor_tensor(vext[:, t, :, 0:HD], src, bv[:].rearrange("p (h e) -> p h e", e=HD),
                                            ALU.add).then_inc(s_v, 1)
                else:
                    nc.vector.tensor_copy(vext[:, t, :, 0:HD], src).then_inc(s_v, 1)

        @block.sync
        def _(sp):
            for n, (u, i) in enumerate(tiles):
                M, dst = units[u][4], units[u][5][i]
                for k in range(3):
                    sp.wait_ge((s_part, s_part, s_lo)[k], 2 * n + (1, 2, 2)[k])
                    sp.dma_start(dst[k], part[0:M, n % 2, k, :]).then_inc(s_store[n % 2], 16)
            for i in range(2):
                sp.wait_ge(s_store[i], 48 * (len(tiles) // 2))


def small_attn(chip, add_f, name, a, kv_heads, rope):
    nc, ps, f = chip.nc, chip.ps, chip.f
    KH = GROUP if kv_heads == HEADS else 1
    SCALE = float(HD) ** -0.5
    q_parts = nc.dram_tensor(f"{name}_q_parts", (3, HD, HEADS, T), BF16).ap()
    k_parts = nc.dram_tensor(f"{name}_k_parts", (3, HD, kv_heads, T), BF16).ap()
    with ExitStack() as outer:
        vext = outer.enter_context(nc.sbuf_tensor(f"{name}_vext", [P, NT, kv_heads, 2 * HD], F32))
        with ExitStack() as mem:
            split_qkv(chip, name, mem, a, kv_heads, rope, add_f, q_parts, k_parts, vext)
        attend(chip, name, outer, a, KH, SCALE, q_parts, k_parts, vext)
    if not rope:
        rows_out(chip, name, a[name + "_wo"])


def attend(chip, name, mem, a, KH, SCALE, q_parts, k_parts, vext):
    nc, ps, f = chip.nc, chip.ps, chip.f

    def sb(n, shape, dt=F32):
        return mem.enter_context(nc.sbuf_tensor(f"{name}_{n}", shape, dt))
    SLOTS = 3
    q6 = sb("q6", [EXT, SLOTS, GROUP, T], BF16)
    k6 = sb("k6", [EXT, SLOTS, KH, T], BF16)
    prob = sb("prob", [P, 2 * GROUP, T])
    vst = sb("vst", [P, SLOTS, NT, KH, 2 * HD])
    osb = sb("osb", [P, T])
    mx = sb("mx", [P, GROUP, NT, 2])
    mcol = sb("mcol", [P, 2, NT, GROUP // 2], BF16)
    mrow = sb("mrow", [GROUP // 2, 2, T], BF16)
    ident16 = sb("ident16", [P, P], BF16)
    rden = sb("rden", [P, NT, GROUP])
    s_ld = [chip.sem(f"{name}_heads_loaded{i}") for i in range(SLOTS)]
    s_row = [chip.sem(f"{name}_max_stored{i}") for i in range(2)]
    (s_c, s_v, s_mm, s_red0, s_red1, s_neg, s_mt, s_mrow, s_st, s_exp, s_pv, s_oev, s_ot, s_rd, s_out,
     s_ones) = (
        chip.sem(f"{name}_{n}") for n in (
            "consts", "v_staged", "max_scores", "reduced0", "reduced1", "negated", "max_turned",
            "max_rows", "scores", "exps", "pv", "o_out", "o_turned", "recip", "o_done", "rows_of_ones"))
    ST = [ps[:, 0:2, :], ps[:, 2:4, :]]
    O = ps[:, 4:6, :]
    MB = [ps[:, 6, :], ps[:, 7, :]]
    TURN = MB[0].bitcast(BF16)[0:GROUP // 2, :]
    STEPS = NT * GROUP
    TILES = GROUP * NT
    LOADS = 16 * 6
    CHUNKS = 2 * TILES
    HALF_CHUNKS = CHUNKS // 2
    PV_AT = {s: [] for s in range(STEPS)}
    for c, s in enumerate((5, 5, 6, 6)):
        PV_AT[s].append((0, c))
    for j in range(1, NT):
        for c in range(4):
            PV_AT[min(GROUP * j + 3 + c, STEPS - 1)].append((j, c))
    LAST_TURN, TURN_LAG = 29, 4
    work, slots = 0, []
    for s in range(LAST_TURN):
        slots.append((work, (s, 0)))
        for i in range(1 + len(PV_AT[s])):
            work += 1
            slots.append((work, (s, 1 + i)))
    SLOT_OF = [next(at for w, at in slots if w * CHUNKS >= n * work) for n in range(CHUNKS)]
    FIRST_TURN = SLOT_OF[HALF_CHUNKS + TURN_LAG - 1][0]
    EPILOGUE_CHUNK = sum(at[0] <= 4 for at in SLOT_OF)

    def kh(hh):
        return hh if KH == GROUP else 0

    with nc.Block() as block:
        @block.sync
        def _(sp):
            sp.dma_start(ident16[:], a["ident16"]).then_inc(s_c, 16)

            def load(g, par):
                row = 0
                for part, n in Q_RUNS:
                    src = q_parts[part, :, bass.ds(g * GROUP, GROUP), :].rearrange("r h t -> r (h t)")
                    sp.dma_start(q6[row:row + n * HD, par, :, :].rearrange("r h t -> r (h t)"),
                                 src.unsqueeze(0).broadcast_to([n, HD, GROUP * T])).then_inc(s_ld[par], 16)
                    row += n * HD
                row = 0
                for part, n in K_RUNS:
                    src = k_parts[part:part + n, :, bass.ds(g * KH, KH), :].rearrange("s r h t -> s r (h t)")
                    sp.dma_start(k6[row:row + n * HD, par, :, :].rearrange("r h t -> r (h t)"),
                                 src).then_inc(s_ld[par], 16)
                    row += n * HD

            def place_max(g, par):
                for i in range(2):
                    sp.wait_ge(s_mrow, g * 2 + i + 1)
                    sp.dma_start(q6[MAX_ROW:EXT, par, 2 * i:2 * i + 2, :], mrow[:, i, :]).then_inc(s_row[i], 16)

            def reload(g, par):
                sp.wait_ge(s_st, (g - 2) * STEPS)
                load(g, par)

            for g in range(SLOTS):
                load(g, g)
            place_max(0, 0)
            place_max(1, 1)
            with sp.Fori(1, 2) as i:
                for k in range(SLOTS):
                    reload(i * 3 + k, k)
                    place_max(i * 3 + k - 1, (k + 2) % SLOTS)
            for g in (6, 7):
                reload(g, g % SLOTS)
                place_max(g - 1, (g - 1) % SLOTS)
            place_max(GROUPS - 1, (GROUPS - 1) % SLOTS)

        @block.gpsimd
        def _(pool):
            def stage(g, par):
                nc.gpsimd.tensor_copy(vst[:, par, :, :, :], vext[:, :, bass.ds(g * KH, KH), :]).then_inc(s_v, 1)
            for g in range(GROUPS):
                if g < SLOTS:
                    if g:
                        pool.wait_ge(s_v, g)
                    nc.gpsimd.memset(k6[MAX_ROW:EXT, g, :, :], 1.0).then_inc(s_ones, 1)
                    pool.wait_ge(s_ones, g + 1)
                else:
                    pool.wait_ge(s_pv, (g - SLOTS + 1) * NT)
                stage(g, g % SLOTS)

        @block.tensor
        def _(pe):
            def max_chunk(g, par, turn, n, first=False):
                m, c = n // 2, n % 2
                hh, qt = m // NT, m % NT
                if n == 0:
                    pe.wait_ge(s_ld[par], turn * LOADS + LOADS)
                    if not first:
                        pe.wait_ge(s_mrow, g * 2)
                if m:
                    pe.wait_ge((s_red0, s_red1)[c], g * TILES + m)
                nc.tensor.matmul(MB[c], q6[0:ROWS, par, hh, qt * P:(qt + 1) * P],
                                 k6[0:ROWS, par, kh(hh), 512 * c:512 * c + 512],
                                 start=True, stop=True).then_inc(s_mm, 1)

            def max_turn(g, i):
                pe.wait_ge(s_neg, g * 2 + i + 1)
                if i == 0:
                    pe.wait_ge(s_red0, g * TILES + (HALF_CHUNKS + TURN_LAG) // 2)
                for t in range(NT):
                    mm = nc.tensor.transpose(TURN[:, t * P:(t + 1) * P], mcol[:, i, t, :], ident16[:])
                mm.then_inc(s_mt, 1)

            def scores(g, par, s):
                j, hh = s // GROUP, s % GROUP
                if s in (0, 2):
                    pe.wait_ge(s_row[s // 2], g * 16 + 16)
                for c in range(2):
                    mm = nc.tensor.matmul(ST[s % 2][:, c, :], k6[:, par, kh(hh), j * P:(j + 1) * P],
                                          q6[:, par, hh, 512 * c:512 * c + 512], start=True, stop=True)
                mm.then_inc(s_st, 1)

            def pv(g, par, j, c):
                cut = slice(256 * (c % 2), 256 * (c % 2) + 256)
                for hh in range(GROUP):
                    mm = nc.tensor.matmul(O[32 * hh:32 * hh + 32, c // 2, cut], vst[:, par, j, kh(hh), :],
                                          prob[:, (j % 2) * GROUP + hh, 256 * c:256 * c + 256],
                                          start=j == 0 and c % 2 == 0, stop=j == NT - 1 and c % 2 == 1)
                if c == 3:
                    mm.then_inc(s_pv, 1)

            def o_turn(g):
                pe.wait_ge(s_oev, g + 1)
                for t in range(NT):
                    mm = nc.tensor.transpose(O[:, t // 4, (t % 4) * P:(t % 4 + 1) * P], osb[:, t * P:(t + 1) * P],
                                             chip.ident[:])
                mm.then_inc(s_ot, 1)

            def group(g, par, next_turn, first, last):
                after = (par + 1) % SLOTS

                def chunks(s, k):
                    for n in range(CHUNKS):
                        if not last and SLOT_OF[n] == (s, k):
                            if n == HALF_CHUNKS + TURN_LAG:
                                pe.wait_ge(s_mrow, g * 2 + 3)
                            max_chunk(g + 1, after, next_turn, n)
                            if n == HALF_CHUNKS + TURN_LAG - 1:
                                max_turn(g + 1, 0)

                for s in range(STEPS):
                    chunks(s, 0)
                    pe.wait_ge(s_exp, g * STEPS + s + 1)
                    if s + 2 < STEPS:
                        scores(g, par, s + 2)
                    elif not last:
                        scores(g + 1, after, s + 2 - STEPS)
                    if s == 2 and not first:
                        o_turn(g - 1)
                    chunks(s, 1)
                    for k, (j, c) in enumerate(PV_AT[s]):
                        if (j, c) == (0, 0):
                            pe.wait_ge(s_v, g + 1)
                            if not first:
                                pe.wait_ge(s_out, g)
                        pv(g, par, j, c)
                        chunks(s, 2 + k)
                    if s == LAST_TURN and not last:
                        max_turn(g + 1, 1)

            pe.wait_ge(s_c, 16)
            for n in range(CHUNKS):
                if n == HALF_CHUNKS + TURN_LAG:
                    max_turn(0, 0)
                    pe.wait_ge(s_mrow, 1)
                max_chunk(0, 0, 0, n, first=True)
            max_turn(0, 1)
            pe.wait_ge(s_ones, SLOTS)
            scores(0, 0, 0)
            scores(0, 0, 1)
            group(0, 0, 0, True, False)
            with pe.Fori(0, (GROUPS - 2) // SLOTS) as i:
                group(i * SLOTS + 1, 1, i, False, False)
                group(i * SLOTS + 2, 2, i + 1, False, False)
                group(i * SLOTS + 3, 0, i + 1, False, False)
            group(GROUPS - 1, (GROUPS - 1) % SLOTS, None, False, True)
            o_turn(GROUPS - 1)

        @block.scalar
        def _(act):
            def max_out(g, i):
                act.wait_ge(s_mt, g * 2 + i + 1)
                nc.scalar.copy(mrow[:, i, :], TURN).then_inc(s_mrow, 1)

            def o_out(g):
                act.wait_ge(s_pv, g * NT + NT)
                nc.scalar.copy(osb[:], O.rearrange("p b n -> p (b n)")).then_inc(s_oev, 1)

            def group(g, first, last):
                for s in range(STEPS):
                    act.wait_ge(s_st, g * STEPS + s + 1)
                    if s % GROUP == 0 and not (first and s < 2 * GROUP):
                        act.wait_ge(s_pv, g * NT + s // GROUP - 1)
                    nc.scalar.activation(prob[:, s % (2 * GROUP), :], ST[s % 2].rearrange("p b n -> p (b n)"),
                                         ACT.Exp, scale=SCALE).then_inc(s_exp, 1)
                    if s == 1 and not first:
                        o_out(g - 1)
                    if s in (FIRST_TURN, LAST_TURN + 1) and not last:
                        max_out(g + 1, int(s > LAST_TURN))

            max_out(0, 0)
            max_out(0, 1)
            group(0, True, False)
            with act.Fori(1, GROUPS - 1) as g:
                group(g, False, False)
            group(GROUPS - 1, False, True)
            o_out(GROUPS - 1)

        @block.vector
        def _(dve):
            def maxima(g, done=None):
                for n in range(CHUNKS):
                    if n == EPILOGUE_CHUNK and done is not None:
                        epilogue(done)
                    m, c = n // 2, n % 2
                    dve.wait_ge(s_mm, g * CHUNKS + n + 1)
                    nc.vector.tensor_reduce(mx[:, m // NT, m % NT, c:c + 1], MB[c], AX.X,
                                            ALU.max).then_inc((s_red0, s_red1)[c], 1)
                    if n % HALF_CHUNKS == HALF_CHUNKS - 1:
                        i = n // HALF_CHUNKS
                        dve.wait_ge(s_red0, g * TILES + m + 1)
                        dve.wait_ge(s_red1, g * TILES + m + 1)
                        nc.vector.tensor_reduce(mcol[:, i, :, :].rearrange("p t h -> p h t"), mx[:, 2 * i:2 * i + 2], AX.X,
                                                ALU.max, negate=True).then_inc(s_neg, 1)

            def epilogue(g):
                dve.wait_ge(s_ot, g + 1)
                both = O.rearrange("p b (t h e) -> p (b t) h e", h=GROUP, e=2 * HD)
                nc.vector.reciprocal(rden[:], both[:, :, :, HD]).then_inc(s_rd, 1)
                dve.wait_ge(s_rd, g + 1)
                for hh in range(GROUP):
                    o = nc.vector.tensor_tensor(f[:, :, bass.ds((g * GROUP + hh) * HD, HD)], both[:, :, hh, 0:HD],
                                                rden[:, :, hh:hh + 1].broadcast_to([P, NT, HD]), ALU.mult)
                o.then_inc(s_out, 1)

            maxima(0)
            maxima(1)
            with dve.Fori(0, GROUPS - 2) as g:
                maxima(g + 2, g)
            epilogue(GROUPS - 2)
            epilogue(GROUPS - 1)


MLA_HEADS = 32
Q_RANK, KV_RANK, NOPE, ROPE, VD = 192, 64, 128, 64, 128
HALF = ROPE // 2
RMS_EPS = 1e-6
JOBS = 17
MAX_CHUNKS = []
for _qt in range(NT):
    if _qt < 4:
        MAX_CHUNKS.append((_qt, 0, P * (_qt + 1), P * _qt))
    else:
        MAX_CHUNKS.append((_qt, 0, 512, None))
        MAX_CHUNKS.append((_qt, 1, P * (_qt - 3), P * (_qt - 4)))
NMAX = len(MAX_CHUNKS)


def l0_attn(chip, add_f, a):
    nc, ps = chip.nc, chip.ps
    flat = chip.f[:].rearrange("p t d -> p (t d)")
    qT0, qT1, kT = flat[:, 0:T], flat[:, T:2 * T], flat[:, 2 * T:3 * T]
    cext = flat[:, 3 * T:4 * T].rearrange("p (t e) -> p t e", t=NT)
    with ExitStack() as mem:
        k16 = mem.enter_context(nc.sbuf_tensor("l0a_k16", [P, T], BF16))
        oT = mem.enter_context(nc.sbuf_tensor("l0a_oT", [P, MLA_HEADS // 2, T], F32))
        wo = mem.enter_context(nc.sbuf_tensor("l0a_wo", [P, MLA_HEADS // 2, D], F32))
        with ExitStack() as temp:
            latents(chip, temp, add_f, a, qT0, qT1, kT, k16, cext)
        with ExitStack() as temp:
            mla_heads(chip, temp, a, qT0, qT1, kT, k16, cext, oT, wo)
        s_row = chip.sem("l0a_rows")
        s_f, norms = stage_norms(chip)
        with nc.Block() as block:
            @block.tensor
            def _(pe):
                for t in range(NT):
                    for i in range(MLA_HEADS // 2):
                        mm = nc.tensor.matmul(ps[:, t, :], oT[:, i, t * P:(t + 1) * P], wo[:, i, :],
                                              start=i == 0, stop=i == MLA_HEADS // 2 - 1)
                    mm.then_inc(s_row, 1)

            @block.vector
            def _(dve):
                for t in range(NT):
                    dve.wait_ge(s_row, t + 1)
                    nc.vector.tensor_copy(chip.f[:, t, :], ps[:, t, :]).then_inc(s_f, 1)
                    if t % 2:
                        norms.vector(dve, t // 2)
                for k in (4, 5):
                    norms.vector(dve, k)

            @block.scalar
            def _(act):
                norms.scalar(act)

            @block.gpsimd
            def _(pool):
                norms.gpsimd(pool)

            @block.sync
            def _(sp):
                norms.sync(sp)


def latents(chip, mem, add_f, a, qT0, qT1, kT, k16, cext):
    nc, ps, yT = chip.nc, chip.ps, chip.yT
    NW = Q_RANK + KV_RANK + ROPE

    def sb(n, shape, dt=F32):
        return mem.enter_context(nc.sbuf_tensor("l0a_" + n, shape, dt))
    w = sb("wa", [P, KC, NW])
    wkv = sb("wkv", [P, KV_RANK])
    wq = sb("wqn", [P, 2])
    cos, sin = sb("cos_t", [P, NT, HALF]), sb("sin_t", [P, NT, HALF])
    sq = sb("sq", [P, 2, Q_RANK])
    ss, ms, rs = sb("ss", [P, 2, NT]), sb("ms", [P, 2, NT]), sb("rs", [P, 2, NT])
    qn = sb("qn", [P, NT, 2 * P])
    kf = sb("kf", [P, NT, P])
    tmp = sb("tmp", [P, 4, NT, HALF])
    s_w, s_mm, s_sq, s_ms, s_rs, s_qn, s_kf, s_rt, s_z, s_t, s_c = (
        chip.sem("l0a_" + n) for n in ("loaded", "latent", "squares", "mean", "rms", "qn", "kf", "rot", "pad",
                                       "turned", "ready"))

    def loads(sp):
        def ld(dst, src):
            sp.dma_start(dst, src).then_inc(s_w, 16)
        ld(w[:], weights_view(a["l0a_wa"]))
        ld(wkv[:], a["l0a_wkv"].partition_broadcast(P))
        ld(wq[:], a["l0a_wqn"])
        ld(cos[:], a["l0a_cos_t"])
        ld(sin[:], a["l0a_sin_t"])

    renorm(chip, "l0a", add_f, loads=loads)
    with nc.Block() as block:
        @block.tensor
        def _(pe):
            pe.wait_ge(s_w, 80)
            for t in range(NT):
                for c in range(KC):
                    mm = nc.tensor.matmul(ps[:, t, 0:NW], yT[:, c, t * P:(t + 1) * P], w[:, c, :],
                                          start=c == 0, stop=c == KC - 1)
                mm.then_inc(s_mm, 1)
            pe.wait_ge(s_qn, NT)
            pe.wait_ge(s_kf, NT + 2)
            pe.wait_ge(s_z, 2)
            for b in range(3):
                for t in range(NT):
                    src = kf[:, t, :] if b == 2 else qn[:, t, b * P:(b + 1) * P]
                    mm = nc.tensor.transpose(ps[:, 2 * b + t // 4, (t % 4) * P:(t % 4 + 1) * P], src, chip.ident[:])
                mm.then_inc(s_t, 1)

        @block.scalar
        def _(act):
            for t in range(NT):
                act.wait_ge(s_mm, t + 1)
                if t:
                    act.wait_ge(s_sq, 2 * t)
                nc.scalar.activation(sq[:, 0, :], ps[:, t, 0:Q_RANK], ACT.Square,
                                     accum_out=ss[:, 0, t:t + 1]).then_inc(s_sq, 1)
                nc.scalar.activation(sq[:, 1, 0:KV_RANK], ps[:, t, Q_RANK:Q_RANK + KV_RANK], ACT.Square,
                                     accum_out=ss[:, 1, t:t + 1]).then_inc(s_sq, 1)
            act.wait_ge(s_rs, 1)
            act.wait_ge(s_rt, 4)
            for t in range(NT):
                nc.scalar.activation(qn[:, t, 0:Q_RANK], ps[:, t, 0:Q_RANK], ACT.Copy,
                                     scale=rs[:, 0, t:t + 1]).then_inc(s_qn, 1)
            act.wait_ge(s_t, 2)
            nc.scalar.activation(qT0, ps[:, 0:2, :].rearrange("p b n -> p (b n)"), ACT.Copy, scale=wq[:, 0:1])
            nc.scalar.activation(qT1[0:64], ps[0:64, 2:4, :].rearrange("p b n -> p (b n)"), ACT.Copy,
                                 scale=wq[0:64, 1:2])
            act.wait_ge(s_c, 1)
            nc.scalar.copy(k16[:], kT)

        @block.gpsimd
        def _(pool):
            nc.gpsimd.memset(qn[:, :, Q_RANK:2 * P], 0.0).then_inc(s_z, 1)
            nc.gpsimd.memset(cext[:, :, KV_RANK:P], 1.0).then_inc(s_z, 1)
            pool.wait_ge(s_ms, 2)
            nc.gpsimd.tensor_tensor(rs[:].rearrange("p a t -> p (a t)"), ms[:].rearrange("p a t -> p (a t)"),
                                    chip.neghalf[:], ALU.pow).then_inc(s_rs, 1)

        @block.vector
        def _(dve):
            dve.wait_ge(s_w, 80)
            dve.wait_ge(s_mm, NT)
            dve.wait_ge(s_sq, 2 * NT)
            ra = ps[:, 0:NT, Q_RANK + KV_RANK:Q_RANK + KV_RANK + HALF]
            rb = ps[:, 0:NT, Q_RANK + KV_RANK + HALF:NW]
            for k, (x, y) in enumerate(((ra, cos), (rb, sin), (ra, sin), (rb, cos))):
                nc.vector.tensor_tensor(tmp[:, k], x, y[:], ALU.mult).then_inc(s_rt, 1)
            dve.wait_ge(s_rt, 4)
            nc.vector.tensor_tensor(kf[:, :, KV_RANK:KV_RANK + HALF], tmp[:, 0], tmp[:, 1], ALU.subtract).then_inc(s_kf, 1)
            nc.vector.tensor_tensor(kf[:, :, KV_RANK + HALF:P], tmp[:, 2], tmp[:, 3], ALU.add).then_inc(s_kf, 1)
            for k, n in enumerate((Q_RANK, KV_RANK)):
                nc.vector.tensor_scalar(ms[:, k, :], ss[:, k, :], 1.0 / n, RMS_EPS, ALU.mult, ALU.add).then_inc(s_ms, 1)
            dve.wait_ge(s_rs, 1)
            for t in range(NT):
                dve.wait_ge(s_qn, t + 1)
                nc.vector.scalar_tensor_tensor(out=kf[:, t, 0:KV_RANK], in0=ps[:, t, Q_RANK:Q_RANK + KV_RANK],
                                               scalar=rs[:, 1, t:t + 1], in1=wkv[:], op0=ALU.mult,
                                               op1=ALU.mult).then_inc(s_kf, 1)
            dve.wait_ge(s_kf, NT + 2)
            nc.vector.tensor_copy(cext[:, :, 0:KV_RANK], kf[:, :, 0:KV_RANK])
            dve.wait_ge(s_t, 3)
            nc.vector.tensor_copy(kT, ps[:, 4:6, :].rearrange("p b n -> p (b n)")).then_inc(s_c, 1)


def mla_heads(chip, mem, a, qT0, qT1, kT, k16, cext, oT, wo):
    nc, ps = chip.nc, chip.ps
    prob = chip.yT
    SCALE = float(NOPE + ROPE) ** -0.5

    def sb(n, shape, dt=F32):
        return mem.enter_context(nc.sbuf_tensor("l0a_" + n, shape, dt))
    cos, sin = sb("cosT", [P, T]), sb("sinT", [P, T])
    ident16, mask = sb("ident16", [P, P], BF16), sb("mask", [P, P], BF16)
    ones, diag = sb("ones", [NT, P], BF16), sb("diag8", [NT, NT, P])
    wqn, wk, wv = sb("wqnT", [P, 2, Q_RANK]), sb("wkT", [P, 2, KV_RANK]), sb("wvT", [P, 2, KV_RANK])
    woh, wh = sb("woh", [P, 2, D]), sb("wh", [P, 2, 2, P])
    q32, q16 = sb("q32", [P, 2, T]), sb("q16", [P, 2, T], BF16)
    rot = sb("rot", [P, 2, 512])
    mx, mcol = sb("mx", [P, NT, 2]), sb("mcol0", [P, P])
    mrow = sb("mrow", [NT, 2, T], BF16)
    osum = sb("osum", [KV_RANK + 1, T])
    rows8, recip8 = sb("rows8", [P, NT]), sb("recip8", [P, NT])
    rbc = sb("recip_all", [KV_RANK, T])
    recip_row = nc.dram_tensor("l0a_recip_row", (T,), F32).ap()
    s_ld = [chip.sem(f"l0a_weights{i}") for i in range(2)]
    (s_c, s_one, s_absmm, s_abs, s_prj, s_qc, s_rt, s_rope, s_q16, s_womm, s_wo, s_mm, s_red, s_neg, s_mt, s_mrow,
     s_st, s_exp, s_pv, s_os, s_r8, s_rd, s_rst, s_rb, s_on) = (chip.sem("l0h_" + n) for n in (
         "consts", "ones", "absorbed", "absorbed_out", "q", "q_copied", "rot_terms", "rotated", "q16", "vo", "vo_out",
         "max_scores", "reduced", "negated", "max_turned", "max_rows", "scores", "exps", "pv", "o_out", "sums_spread", "recip", "recip_stored",
         "recip_loaded", "o_done"))
    ST = [ps[:, 0:2, :].rearrange("p b n -> p (b n)"), ps[:, 2:4, :].rearrange("p b n -> p (b n)")]
    O = ps[:, 4:6, :].rearrange("p b n -> p (b n)")
    LOADS = 16 * 6
    NH = MLA_HEADS

    def bank(par, k):
        return ps[:, 6 + (par + k) % 2, :]

    def spans(j):
        return [(max(P * j, 512 * c), 512 * c + 512) for c in range(2) if P * j < 512 * c + 512]

    with nc.Block() as block:
        @block.sync
        def _(sp):
            for dst, name in ((cos[64:P, :], "l0a_cosT"), (sin[64:P, :], "l0a_sinT"), (ident16[:], "ident16"),
                              (mask[:], "l0a_mask"), (diag[:], "l0a_diag")):
                sp.dma_start(dst, a[name]).then_inc(s_c, 16)

            def load(n, par):
                def ld(dst, src):
                    sp.dma_start(dst, src).then_inc(s_ld[par], 16)
                one = bass.ds(n, 1)
                ld(wqn[:, par, :], a["l0a_wqnT"][one].rearrange("h p r -> p (h r)"))
                ld(wk[:, par, :], a["l0a_wkT"][one].rearrange("h p r -> p (h r)"))
                ld(wh[:, par, 0, KV_RANK:P], a["l0a_wqpe"][one, 0:P].rearrange("h p r -> p (h r)"))
                ld(wh[0:64, par, 1, KV_RANK:P], a["l0a_wqpe"][one, P:Q_RANK].rearrange("h p r -> p (h r)"))
                ld(wv[:, par, :], a["l0a_wvT"][one].rearrange("h p r -> p (h r)"))
                ld(woh[:, par, :], a["l0a_wo"][one].rearrange("h p r -> p (h r)"))
            load(0, 0)
            load(1, 1)

            def reload(n, par):
                sp.wait_ge(s_womm, n - 1)
                load(n, par)

            def spread(h):
                sp.wait_ge(s_os, h + 1)
                sp.dma_start(rows8[:], osum[KV_RANK:KV_RANK + 1, :]).then_inc(s_r8, 16)
                sp.wait_ge(s_rd, h + 1)
                sp.dma_start(recip_row.rearrange("(p c) -> p c", p=P), recip8[:]).then_inc(s_rst, 16)
                sp.wait_ge(s_rst, h * 16 + 16)
                sp.dma_start(rbc[:], recip_row.partition_broadcast(KV_RANK)).then_inc(s_rb, 16)

            reload(2, 0)
            reload(3, 1)
            spread(0)
            reload(4, 0)
            with sp.Fori(0, NH // 2 - 3) as i:
                spread(i * 2 + 1)
                reload(i * 2 + 5, 1)
                spread(i * 2 + 2)
                reload(i * 2 + 6, 0)
            spread(NH - 5)
            reload(NH - 1, 1)
            with sp.Fori(NH - 4, NH) as h:
                spread(h)

        @block.tensor
        def _(pe):
            def job(h, par, turn, k, first):
                b = bank(par, k)
                if k == 0:
                    pe.wait_ge(s_ld[par], turn * LOADS + LOADS)
                    if not first:
                        pe.wait_ge(s_red, h * NMAX)
                    nc.tensor.matmul(b[:, 0:64], wqn[:, par, 0:P], wk[:, par, :], start=True, stop=True)
                    nc.tensor.matmul(b[0:64, 64:128], wqn[:, par, P:Q_RANK], wk[:, par, :], start=True,
                                     stop=True).then_inc(s_absmm, 1)
                elif k in (1, 2):
                    pe.wait_ge(s_abs, h + 1)
                    if k == 1 and not first:
                        pe.wait_ge(s_mrow, h)
                    cut = slice(512 * (k - 1), 512 * k)
                    nc.tensor.matmul(b, wh[:, par, 0, :], qT0[:, cut], start=True, stop=False)
                    nc.tensor.matmul(b, wh[0:64, par, 1, :], qT1[0:64, cut], start=False, stop=True).then_inc(s_prj, 1)
                elif k == 3:
                    pe.wait_ge(s_qc, h * 2 + 1)
                    pe.wait_ge(s_rope, h * 2 + 1)
                    nc.tensor.matmul(b[0:64, :], wv[:, par, :], woh[:, par, :], start=True, stop=True).then_inc(s_womm, 1)
                elif k < 4 + NMAX:
                    n = k - 4
                    qt, c, width, dg = MAX_CHUNKS[n]
                    if n == 0:
                        pe.wait_ge(s_qc, h * 2 + 2)
                        pe.wait_ge(s_rope, h * 2 + 2)
                        pe.wait_ge(s_q16, h * 2 + 1)
                    elif n == 1:
                        pe.wait_ge(s_wo, h + 1)
                    else:
                        pe.wait_ge(s_red, h * NMAX + n - 1)
                    if n == 4:
                        pe.wait_ge(s_q16, h * 2 + 2)
                    mm = nc.tensor.matmul(b[:, 0:width], q16[:, par, qt * P:(qt + 1) * P], k16[:, 512 * c:512 * c + width],
                                          start=True, stop=dg is None)
                    if dg is not None:
                        mm = nc.tensor.matmul(b[:, dg:dg + P], ident16[:], mask[:], start=False, stop=True)
                    mm.then_inc(s_mm, 1)
                else:
                    pe.wait_ge(s_neg, h + 1)
                    nc.tensor.transpose(b[:, 0:P], mcol[:], chip.ident[:]).then_inc(s_mt, 1)

            def scores(h, par, j):
                if j == 0:
                    pe.wait_ge(s_mrow, h + 1)
                for lo, hi in spans(j):
                    out = ST[j % 2][:, lo:hi]
                    diagonal = lo == P * j
                    nc.tensor.matmul(out, kT[:, j * P:(j + 1) * P], q32[:, par, lo:hi], start=True, stop=False)
                    mm = nc.tensor.matmul(out, ones[:], mrow[:, par, lo:hi], start=False, stop=not diagonal)
                    if diagonal:
                        mm = nc.tensor.matmul(ST[j % 2][:, lo:lo + P], mask[:], ident16[:], start=False, stop=True)
                mm.then_inc(s_st, 1)

            def pv(j):
                for lo, hi in spans(j):
                    mm = nc.tensor.matmul(O[:, lo:hi], cext[:, j, :], prob[:, j % 4, lo:hi], start=j == 0,
                                          stop=j == (3 if hi == 512 else NT - 1))
                mm.then_inc(s_pv, 1)

            PLAN = [(0, 3, 3), (3, 4, 5), (5, 7, 8), (8, 10, 12), (12, 14, 16), (16, 17, 17), (17, 17, 17), (17, 17, 17)]

            def head(h, par, next_turn, first, last):
                for j in range(NT):
                    pe.wait_ge(s_exp, h * NT + j + 1)
                    if j + 2 < NT:
                        scores(h, par, j + 2)
                    elif not last:
                        scores(h + 1, 1 - par, j + 2 - NT)
                    if not last:
                        for k in range(*PLAN[j][0:2]):
                            job(h + 1, 1 - par, next_turn, k, False)
                    if j == 0 and not first:
                        pe.wait_ge(s_os, h)
                    pv(j)
                    if not last:
                        for k in range(*PLAN[j][1:3]):
                            job(h + 1, 1 - par, next_turn, k, False)

            pe.wait_ge(s_c, 80)
            pe.wait_ge(s_one, 3)
            for k in range(JOBS):
                job(0, 0, 0, k, True)
            scores(0, 0, 0)
            scores(0, 0, 1)
            head(0, 0, 0, True, False)
            with pe.Fori(0, NH // 2 - 1) as i:
                head(i * 2 + 1, 1, i + 1, False, False)
                head(i * 2 + 2, 0, i + 1, False, False)
            head(NH - 1, 1, None, False, True)

        @block.scalar
        def _(act):
            def ready(h, par, pair, stage):
                if stage == 0:
                    act.wait_ge(s_absmm, h + 1)
                    nc.scalar.copy(wh[:, par, 0, 0:64], bank(par, 0)[:, 0:64])
                    nc.scalar.copy(wh[0:64, par, 1, 0:64], bank(par, 0)[0:64, 64:128]).then_inc(s_abs, 1)
                elif stage == 1:
                    for c in range(2):
                        act.wait_ge(s_prj, h * 2 + c + 1)
                        nc.scalar.copy(q32[0:64, par, 512 * c:512 * c + 512], bank(par, 1 + c)[0:64, :]).then_inc(s_qc, 1)
                elif stage == 2:
                    act.wait_ge(s_womm, h + 1)
                    nc.scalar.copy(wo[64 * par:64 * par + 64, bass.ds(pair, 1), :].rearrange("p a n -> p (a n)"),
                                   bank(par, 3)[0:64, :]).then_inc(s_wo, 1)
                    cast(h, par, 0)
                elif stage == 3:
                    cast(h, par, 1)

            def cast(h, par, c):
                act.wait_ge(s_rope, h * 2 + c + 1)
                act.wait_ge(s_qc, h * 2 + c + 1)
                nc.scalar.copy(q16[:, par, 512 * c:512 * c + 512], q32[:, par, 512 * c:512 * c + 512]).then_inc(s_q16, 1)

            def head(h, par, next_pair, first, last, second=False):
                for j in range(NT):
                    act.wait_ge(s_st, h * NT + j + 1)
                    if not (first and j < 4):
                        act.wait_ge(s_pv, h * NT + j - 3)
                    nc.scalar.activation(prob[:, j % 4, P * j:T], ST[j % 2][:, P * j:T], ACT.Exp,
                                         scale=SCALE).then_inc(s_exp, 1)
                    if j == 0 and not first:
                        if not second:
                            act.wait_ge(s_on, h - 1)
                        lift(h - 1)
                    if not last:
                        ready(h + 1, 1 - par, next_pair, j)

            def lift(h):
                act.wait_ge(s_pv, h * NT + NT)
                nc.scalar.copy(osum[:], O[0:KV_RANK + 1, :]).then_inc(s_os, 1)

            act.wait_ge(s_one, 3)
            for stage in range(4):
                ready(0, 0, 0, stage)
            head(0, 0, 0, True, False)
            head(1, 1, 1, False, False, second=True)
            head(2, 0, 1, False, False)
            with act.Fori(1, NH // 2 - 1) as i:
                head(i * 2 + 1, 1, i + 1, False, False)
                head(i * 2 + 2, 0, i + 1, False, False)
            head(NH - 1, 1, None, False, True)
            act.wait_ge(s_on, NH - 1)
            lift(NH - 1)

        @block.vector
        def _(dve):
            def prepare(h, par, done=None):
                for c in range(2):
                    cut = slice(512 * c, 512 * c + 512)
                    b = bank(par, 1 + c)
                    dve.wait_ge(s_prj, h * 2 + c + 1)
                    if c:
                        dve.wait_ge(s_rope, h * 2 + 1)
                    nc.vector.tensor_tensor(rot[64:128, 0, :], b[64:128, :], cos[64:128, cut], ALU.mult).then_inc(s_rt, 1)
                    nc.vector.tensor_tensor(rot[64:96, 1, :], b[96:128, :], sin[64:96, cut], ALU.mult).then_inc(s_rt, 1)
                    nc.vector.tensor_tensor(rot[96:128, 1, :], b[64:96, :], sin[96:128, cut], ALU.mult).then_inc(s_rt, 1)
                    dve.wait_ge(s_rt, h * 6 + 3 * c + 3)
                    nc.vector.tensor_tensor(q32[64:128, par, cut], rot[64:128, 0, :], rot[64:128, 1, :],
                                            ALU.add).then_inc(s_rope, 1)
                for n, (qt, c, width, _) in enumerate(MAX_CHUNKS):
                    if n == 6 and done is not None:
                        invert(done)
                    dve.wait_ge(s_mm, h * NMAX + n + 1)
                    nc.vector.tensor_reduce(mx[:, qt, c:c + 1], bank(par, 4 + n)[:, 0:width], AX.X,
                                            ALU.max).then_inc(s_red, 1)
                dve.wait_ge(s_red, h * NMAX + NMAX)
                nc.vector.tensor_reduce(mcol[:, 0:NT], mx[:], AX.X, ALU.max, negate=True).then_inc(s_neg, 1)
                dve.wait_ge(s_mt, h + 1)
                nc.vector.tensor_tensor(mrow[:, par, :].rearrange("r (t q) -> r t q", t=NT),
                                        bank(par, 16)[0:NT, 0:P].unsqueeze(1).broadcast_to([NT, NT, P]), diag[:],
                                        ALU.mult).then_inc(s_mrow, 1)

            def invert(h):
                dve.wait_ge(s_r8, h * 16 + 16)
                nc.vector.reciprocal(recip8[:], rows8[:]).then_inc(s_rd, 1)

            def finish(h, par, pair):
                dve.wait_ge(s_rb, h * 16 + 16)
                nc.vector.tensor_tensor(oT[64 * par:64 * par + 64, bass.ds(pair, 1), :].rearrange("p a n -> p (a n)"),
                                        osum[0:KV_RANK, :], rbc[:], ALU.mult).then_inc(s_on, 1)

            nc.vector.memset(ones[:], 1.0).then_inc(s_one, 1)
            nc.vector.memset(mcol[:], 0.0).then_inc(s_one, 1)
            nc.vector.memset(mx[:, 0:4, 1], -3.0e38).then_inc(s_one, 1)
            dve.wait_ge(s_one, 3)
            dve.wait_ge(s_c, 80)
            prepare(0, 0)
            prepare(1, 1)
            with dve.Fori(0, NH // 2 - 1) as i:
                prepare(i * 2 + 2, 0, i * 2)
                finish(i * 2, 0, i)
                prepare(i * 2 + 3, 1, i * 2 + 1)
                finish(i * 2 + 1, 1, i)
            for h in (NH - 2, NH - 1):
                invert(h)
                finish(h, h % 2, NH // 2 - 1)


def program(nc, a, out):
    with ExitStack() as ctx:
        chip = Chip(nc, ctx, a)
        chip.out = out
        start(chip, a["x"])
        add_f = False
        for layer in LAYERS:
            chip.last = layer == LAYERS[-1]
            if layer == "L0_attn":
                l0_attn(chip, add_f, a)
            if layer == "L0_ffn":
                l0_ffn(chip, add_f, a["l0f_w"], a["l0f_bias"], a["l0f_a"], a["l0f_b"], a["l0f_starts"], a["l0f_want"])
            if layer == "L1_attn":
                small_attn(chip, add_f, "l1a", a, kv_heads=8, rope=True)
            if layer == "L1_ffn":
                l1_ffn(chip, add_f, a["l1f_w"])
            if layer == "L2_attn":
                small_attn(chip, add_f, "l2a", a, kv_heads=32, rope=False)
            if layer == "L2_ffn":
                l2_ffn(chip, add_f, a["l2f_g"], a["l2f_u"], a["l2f_dn"], a["l2f_gs"], a["l2f_us"], a["l2f_ds"])
            if layer == "L3_attn":
                l3_attn(chip, add_f, a["l3a_wd"], a["l3a_bd"], a["l3a_wu"], a["l3a_bu"], a["l3a_gate"], a["l3a_in"],
                        a["l3a_cw"], a["l3a_cb"], a["l3a_d"], a["l3a_fc"], a["l3a_nw"], a["l3a_out"])
            if layer == "L3_ffn":
                l3_ffn(chip, add_f, a["l3f_g"], a["l3f_w"], a["l3f_bias"], a["l3f_a"], a["l3f_b"], a["l3f_iota"])
            add_f = True
        if not chip.normed:
            store(chip)


def _rope_tables(dim, period):
    inv = (1.0 / np.float32(10000.0) ** (np.arange(0, dim, 2, dtype=np.float32) / np.float32(dim))).astype(np.float32)
    ang = (inv[:, None] * np.arange(T, dtype=np.float32)[None, :]).astype(np.float32)
    return np.cos(ang).astype(np.float32), np.sin(ang).astype(np.float32)


def kernel(**inputs):
    import numpy as _np
    import concourse.bacc as _bacc
    from concourse import mybir as _mybir
    from concourse.bass_utils import run_bass_kernel_spmd as _run

    g = {k: _np.asarray(v) for k, v in inputs.items()}
    h = {"x": g["L0_attn_hidden_states"], "ident": _np.eye(P, dtype=_np.float32)}
    if "L0_ffn" in LAYERS:
        h.update(l0f_w=g["L0_ffn_weight"].T, l0f_bias=g["L0_ffn_bias"],
                 l0f_a=g["L0_ffn_lora_A"].reshape(48, D).T,
                 l0f_b=g["L0_ffn_lora_B"].transpose(0, 2, 1).reshape(48, D),
                 l0f_starts=g["L0_ffn_lora_start_indices"],
                 l0f_want=(_np.arange(48) // 16 + 2).astype(_np.float32).reshape(48, 1))
    if "L1_ffn" in LAYERS:
        h.update(l1f_w=g["L1_ffn_weight"])
    if "L2_ffn" in LAYERS:
        h.update(l2f_g=g["L2_ffn_gate_w"].T, l2f_u=g["L2_ffn_up_w"].T, l2f_dn=g["L2_ffn_down_w"].T,
                 l2f_gs=g["L2_ffn_gate_scale"].reshape(1), l2f_us=g["L2_ffn_up_scale"].reshape(1),
                 l2f_ds=g["L2_ffn_down_scale"].reshape(1))
    if "L3_attn" in LAYERS:
        p = "L3_attn_"
        h.update(l3a_wd=g[p + "w_down"].T, l3a_bd=g[p + "b_down"], l3a_wu=g[p + "w_up"].T, l3a_bu=g[p + "b_up"],
                 l3a_gate=g[p + "gate1"].reshape(1), l3a_in=g[p + "hy_in_w"].T,
                 l3a_cw=g[p + "hy_conv_w"][:, 0, 6].reshape(-1, 1), l3a_cb=g[p + "hy_conv_b"].reshape(-1, 1),
                 l3a_d=g[p + "hy_D"], l3a_fc=g[p + "hy_fcD_w"].T, l3a_nw=g[p + "hy_norm_w"].reshape(-1, 1),
                 l3a_out=g[p + "hy_out_w"].T)
    if "L3_ffn" in LAYERS:
        h.update(l3f_g=g["L3_ffn_gate_w"].T, l3f_w=g["L3_ffn_base_w"].T, l3f_bias=g["L3_ffn_base_b"],
                 l3f_a=g["L3_ffn_lora_A"].reshape(P, D).T,
                 l3f_b=g["L3_ffn_lora_B"].transpose(0, 2, 1).reshape(P, D),
                 l3f_iota=_np.arange(8, dtype=_np.float32))
    import ml_dtypes as _ml
    h.update(ident16=_np.eye(P).astype(_ml.bfloat16))
    if "L1_attn" in LAYERS:
        p = "L1_attn_"
        cos, sin = _rope_tables(HD, T)
        h.update(l1a_wq=g[p + "wq"].reshape(D, HEADS, 2, 8).transpose(0, 2, 1, 3).reshape(D, D),
                 l1a_bq=g[p + "bq"].reshape(HEADS, 2, 8).transpose(1, 0, 2).reshape(4, P).T,
                 l1a_wk=g[p + "wk"].reshape(D, 8, 2, 8).transpose(0, 2, 1, 3).reshape(D, P),
                 l1a_bk=g[p + "bk"].reshape(8, 2, 8).transpose(1, 0, 2).reshape(2, 64).T,
                 l1a_wv=g[p + "wv"], l1a_bv=g[p + "bv"],
                 l1a_cos=_np.tile(cos, (16, 1)), l1a_sin=_np.tile(sin, (16, 1)))
    if "L2_attn" in LAYERS:
        p = "L2_attn_"
        h.update(l2a_wq=g[p + "w_q"].T, l2a_wk=g[p + "w_k"].T, l2a_wv=g[p + "w_v"].T, l2a_wo=g[p + "w_o"].T)
    if "L0_attn" in LAYERS:
        p = "L0_attn_"
        turn = _np.r_[_np.arange(0, ROPE, 2), _np.arange(1, ROPE, 2)]
        wqb = g[p + "Wq_b"].reshape(Q_RANK, MLA_HEADS, NOPE + ROPE)
        wkv = g[p + "Wkv_b"].reshape(KV_RANK, MLA_HEADS, NOPE + VD)
        wkva = g[p + "Wkv_a"]
        cos, sin = _rope_tables(ROPE, T)
        q_scale = _np.zeros((P, 2), _np.float32)
        q_scale[:, 0] = g[p + "q_a_ln_w"][0:P]
        q_scale[0:64, 1] = g[p + "q_a_ln_w"][P:]
        h.update(l0a_wa=_np.concatenate([g[p + "Wq_a"], wkva[:, :KV_RANK], wkva[:, KV_RANK:][:, turn]], 1),
                 l0a_wkv=g[p + "kv_a_ln_w"], l0a_wqn=q_scale,
                 l0a_cos_t=cos.T.reshape(NT, P, HALF).transpose(1, 0, 2),
                 l0a_sin_t=sin.T.reshape(NT, P, HALF).transpose(1, 0, 2),
                 l0a_cosT=_np.concatenate([cos, cos]), l0a_sinT=_np.concatenate([-sin, sin]),
                 l0a_mask=_np.triu(_np.full((P, P), -1e30), 1).astype(_ml.bfloat16),
                 l0a_diag=_np.repeat(_np.eye(NT, dtype=_np.float32)[:, :, None], P, 2),
                 l0a_wqnT=wqb[:, :, :NOPE].transpose(1, 2, 0),
                 l0a_wqpe=wqb[:, :, NOPE:][:, :, turn].transpose(1, 0, 2),
                 l0a_wkT=wkv[:, :, :NOPE].transpose(1, 2, 0), l0a_wvT=wkv[:, :, NOPE:].transpose(1, 2, 0),
                 l0a_wo=g[p + "Wo"].reshape(MLA_HEADS, VD, D))
    nc = _bacc.Bacc("TRN2", target_bir_lowering=False, num_devices=1)
    arrays, args = {}, {}
    for name, v in h.items():
        v = _np.ascontiguousarray(v)
        arrays[f"in_{name}"] = v
        args[name] = nc.dram_tensor(f"in_{name}", v.shape, _mybir.dt.from_np(v.dtype), kind="ExternalInput").ap()
    out = nc.dram_tensor("out_0", (1, T, D), _mybir.dt.float32, kind="ExternalOutput").ap()
    program(nc, args, out)
    r = _run(nc, [arrays], core_ids=[0])
    return r.results[0]["out_0"]
```
